# Optimizing a Trainium2 kernel written in Bass

```python
import numpy as np
import jax
import jax.numpy as jnp

def _softmax(x, axis=-1):
    return jax.nn.softmax(x, axis=axis)

def _gelu(x):
    return jax.nn.gelu(x, approximate=True)

def _silu(x):
    return jax.nn.silu(x)

def _sigmoid(x):
    return jax.nn.sigmoid(x)

def _layernorm(x, axis=-1, eps=1e-05):
    m = jnp.mean(x, axis=axis, keepdims=True)
    v = jnp.var(x, axis=axis, keepdims=True)
    return (x - m) / jnp.sqrt(v + eps)

def _scatter_add(tgt, idx, src, axis=0):
    return tgt.at[idx].add(src)

def _segment_sum(src, seg, n):
    return jax.ops.segment_sum(src, seg, n)
kernel_name = 'mk_gnn_preln_d4_gnn_r16_8c2189'

def setup_inputs(seed: int=0):
    np.random.seed(seed)
    _w = jnp.asarray

    def _rec_inputs():
        import jax
        import jax.numpy as jnp
        _gk = jax.random.key(seed)
        x = -0.0003713 + 1 * jax.random.normal(jax.random.fold_in(_gk, 1), (3125, 256), jnp.float32)
        src = jax.random.randint(jax.random.fold_in(_gk, 2), (100000,), 0, 3125, jnp.int32)
        dst = jnp.minimum((3125 * jax.random.uniform(jax.random.fold_in(_gk, 3), (100000,)) ** 2.0).astype(jnp.int32), 49999)
        _o = jnp.argsort(dst, stable=True)
        src = src[_o]
        dst = dst[_o]
        edge_attr_2 = 0.000452788 + 0.999756 * jax.random.normal(jax.random.fold_in(_gk, 12), (100000, 2), jnp.float32)
        edge_weight = -7.32377e-05 + 0.176746 * jax.random.normal(jax.random.fold_in(_gk, 14), (100000,), jnp.float32)
        return (x, src, dst, edge_attr_2, edge_weight)
    x, src, dst, edge_attr_2, edge_weight = _rec_inputs()

    def _L0_gnn_setup():
        import jax, jax.numpy as jnp
        import numpy as np
        N_NODES = 3125
        NNZ = 100000
        D_FEAT = 256
        key = jax.random.key(seed)
        k_x, k_v, k_r, k_c = jax.random.split(key, 4)
        x = jax.random.normal(k_x, (N_NODES, D_FEAT), dtype=jnp.float32)
        std = 1.0 / np.sqrt(NNZ / N_NODES)
        values = jax.random.normal(k_v, (NNZ,), dtype=jnp.float32) * std
        row = jax.random.randint(k_r, (NNZ,), 0, N_NODES, dtype=jnp.int64)
        col = jax.random.randint(k_c, (NNZ,), 0, N_NODES, dtype=jnp.int64)
        return {'x': x, 'values': values, 'row': row, 'col': col}
    _L0_gnn_all = _L0_gnn_setup()
    _L0_gnn_in = {k: v for k, v in _L0_gnn_all.items() if k in ()}
    del _L0_gnn_all

    def _L1_gnn_setup():
        import jax, jax.numpy as jnp
        import numpy as np
        N = 3125
        E = 50000
        D = 256
        SLOPE = 0.2
        EPS = 1e-05

        def _add_self_loops(src, dst, edge_attr, n):
            deg = jax.ops.segment_sum(jnp.ones((src.shape[0],), edge_attr.dtype), dst, n)
            mean_attr = jax.ops.segment_sum(edge_attr, dst, n) / jnp.maximum(deg, 1.0)[:, None]
            loop = jnp.arange(n, dtype=src.dtype)
            return (jnp.concatenate([src, loop]), jnp.concatenate([dst, loop]), jnp.concatenate([edge_attr, mean_attr], axis=0))

        def _gatv2(x, src, dst, eattr, Wl, Wr, We, att, b, n):
            xl = x @ Wl
            xr = x @ Wr
            ee = eattr @ We
            xj = xl[src]
            h = jax.nn.leaky_relu(xj + xr[dst] + ee, SLOPE)
            logits = h @ att
            m = jax.ops.segment_max(logits, dst, n)
            ex = jnp.exp(logits - m[dst])
            denom = jax.ops.segment_sum(ex, dst, n)
            alpha = ex / denom[dst]
            out = jax.ops.segment_sum(xj * alpha[:, None], dst, n)
            return out + b

        def _bn_train(x, g, b):
            mu = jnp.mean(x, axis=0)
            var = jnp.var(x, axis=0)
            return (x - mu) * jax.lax.rsqrt(var + EPS) * g + b

        def _prelu(x, a):
            return jnp.where(x >= 0, x, a * x)
        key = jax.random.key(seed)
        ks = jax.random.split(key, 24)
        s = 0.05
        inp = {'x': jax.random.normal(ks[0], (N, D), jnp.float32), 'edge_index': jax.random.randint(ks[1], (2, E), 0, N, jnp.int32), 'edge_attr': jax.random.normal(ks[2], (E, 2), jnp.float32)}

        def conv_params(koff):
            return dict(Wl=jax.random.normal(ks[koff + 0], (D, D), jnp.float32) * s, Wr=jax.random.normal(ks[koff + 1], (D, D), jnp.float32) * s, We=jax.random.normal(ks[koff + 2], (2, D), jnp.float32) * s, att=jax.random.normal(ks[koff + 3], (D,), jnp.float32) * s, b=jnp.zeros((D,), jnp.float32))
        p1, p2 = (conv_params(3), conv_params(8))
        inp.update({k + '1': v for k, v in p1.items()})
        inp.update({k + '2': v for k, v in p2.items()})
        inp.update(g1=jnp.ones((D,), jnp.float32), beta1=jnp.zeros((D,), jnp.float32), g2=jnp.ones((D,), jnp.float32), beta2=jnp.zeros((D,), jnp.float32), a1=jnp.asarray(0.25, jnp.float32), a2=jnp.asarray(0.25, jnp.float32))
        return inp
    _L1_gnn_all = _L1_gnn_setup()
    _L1_gnn_in = {k: v for k, v in _L1_gnn_all.items() if k in ('Wl1', 'Wr1', 'We1', 'att1', 'b1', 'g1', 'beta1', 'a1', 'Wl2', 'Wr2', 'We2', 'att2', 'b2', 'g2', 'beta2', 'a2')}
    del _L1_gnn_all

    def _L2_gnn_setup():
        import jax, jax.numpy as jnp
        import numpy as np
        N, E, DIN, H, DOUT = (3125, 50000, 256, 4, 64)
        NEG_SLOPE = 0.2
        key = jax.random.key(seed)
        ks = jax.random.split(key, 7)
        x = jax.random.normal(ks[0], (N, DIN), dtype=jnp.float32)
        edge_index = jax.random.randint(ks[1], (2, E), 0, N, dtype=jnp.int64)
        edge_weight = jax.random.uniform(ks[2], (E,), dtype=jnp.float32)
        W = jax.random.normal(ks[3], (DIN, H * DOUT), dtype=jnp.float32) * (1.0 / np.sqrt(DIN))
        att_src = jax.random.normal(ks[4], (H, DOUT), dtype=jnp.float32) * (1.0 / np.sqrt(DOUT))
        att_dst = jax.random.normal(ks[5], (H, DOUT), dtype=jnp.float32) * (1.0 / np.sqrt(DOUT))
        bias = jnp.zeros((H * DOUT,), dtype=jnp.float32)
        return {'x': x, 'edge_index': edge_index, 'edge_weight': edge_weight, 'W': W, 'att_src': att_src, 'att_dst': att_dst, 'bias': bias}
    _L2_gnn_all = _L2_gnn_setup()
    _L2_gnn_in = {k: v for k, v in _L2_gnn_all.items() if k in ('W', 'att_src', 'att_dst', 'bias')}
    del _L2_gnn_all

    def _L3_gnn_setup():
        import jax, jax.numpy as jnp
        import numpy as np
        N_NODES = 3125
        N_EDGES = 50000
        IN_SIZE = 256
        OUT_SIZE = 256
        key = jax.random.key(seed)
        kx, ks, kd, kw, kb = jax.random.split(key, 5)
        x = jax.random.normal(kx, (N_NODES, IN_SIZE), dtype=jnp.float32)
        src_rand = jax.random.randint(ks, (N_EDGES - N_NODES,), 0, N_NODES)
        src = jnp.concatenate([jnp.arange(N_NODES), src_rand]).astype(jnp.int64)
        dst = jax.random.randint(kd, (N_EDGES,), 0, N_NODES).astype(jnp.int64)
        edge_index = jnp.stack([src, dst])
        bound = 1.0 / np.sqrt(IN_SIZE)
        W = jax.random.uniform(kw, (OUT_SIZE, IN_SIZE), dtype=jnp.float32, minval=-bound, maxval=bound)
        b = jax.random.uniform(kb, (OUT_SIZE,), dtype=jnp.float32, minval=-bound, maxval=bound)
        return {'x': x, 'edge_index': edge_index, 'W': W, 'b': b}
    _L3_gnn_all = _L3_gnn_setup()
    _L3_gnn_in = {k: v for k, v in _L3_gnn_all.items() if k in ('W', 'b')}
    del _L3_gnn_all
    return {'x': x, 'src': src, 'dst': dst, 'edge_attr_2': edge_attr_2, 'edge_weight': edge_weight, 'L1_gnn_Wl1': _L1_gnn_in['Wl1'], 'L1_gnn_Wr1': _L1_gnn_in['Wr1'], 'L1_gnn_We1': _L1_gnn_in['We1'], 'L1_gnn_att1': _L1_gnn_in['att1'], 'L1_gnn_b1': _L1_gnn_in['b1'], 'L1_gnn_g1': _L1_gnn_in['g1'], 'L1_gnn_beta1': _L1_gnn_in['beta1'], 'L1_gnn_a1': _L1_gnn_in['a1'], 'L1_gnn_Wl2': _L1_gnn_in['Wl2'], 'L1_gnn_Wr2': _L1_gnn_in['Wr2'], 'L1_gnn_We2': _L1_gnn_in['We2'], 'L1_gnn_att2': _L1_gnn_in['att2'], 'L1_gnn_b2': _L1_gnn_in['b2'], 'L1_gnn_g2': _L1_gnn_in['g2'], 'L1_gnn_beta2': _L1_gnn_in['beta2'], 'L1_gnn_a2': _L1_gnn_in['a2'], 'L2_gnn_W': _L2_gnn_in['W'], 'L2_gnn_att_src': _L2_gnn_in['att_src'], 'L2_gnn_att_dst': _L2_gnn_in['att_dst'], 'L2_gnn_bias': _L2_gnn_in['bias'], 'L3_gnn_W': _L3_gnn_in['W'], 'L3_gnn_b': _L3_gnn_in['b']}

def reference(x, src, dst, edge_attr_2, edge_weight, L1_gnn_Wl1, L1_gnn_Wr1, L1_gnn_We1, L1_gnn_att1, L1_gnn_b1, L1_gnn_g1, L1_gnn_beta1, L1_gnn_a1, L1_gnn_Wl2, L1_gnn_Wr2, L1_gnn_We2, L1_gnn_att2, L1_gnn_b2, L1_gnn_g2, L1_gnn_beta2, L1_gnn_a2, L2_gnn_W, L2_gnn_att_src, L2_gnn_att_dst, L2_gnn_bias, L3_gnn_W, L3_gnn_b):
    import jax
    import jax.numpy as jnp

    def _L0_gnn_ref(x, values, row, col):
        import jax, jax.numpy as jnp
        import numpy as np
        N_NODES = 3125
        NNZ = 100000
        D_FEAT = 256
        msgs = values[:, None] * x[col]
        out = jax.ops.segment_sum(msgs, row, num_segments=N_NODES)
        return out

    def _L1_gnn_ref(x, edge_index, edge_attr, Wl1, Wr1, We1, att1, b1, g1, beta1, a1, Wl2, Wr2, We2, att2, b2, g2, beta2, a2):
        import jax, jax.numpy as jnp
        import numpy as np
        N = 3125
        E = 50000
        D = 256
        SLOPE = 0.2
        EPS = 1e-05

        def _add_self_loops(src, dst, edge_attr, n):
            deg = jax.ops.segment_sum(jnp.ones((src.shape[0],), edge_attr.dtype), dst, n)
            mean_attr = jax.ops.segment_sum(edge_attr, dst, n) / jnp.maximum(deg, 1.0)[:, None]
            loop = jnp.arange(n, dtype=src.dtype)
            return (jnp.concatenate([src, loop]), jnp.concatenate([dst, loop]), jnp.concatenate([edge_attr, mean_attr], axis=0))

        def _gatv2(x, src, dst, eattr, Wl, Wr, We, att, b, n):
            xl = x @ Wl
            xr = x @ Wr
            ee = eattr @ We
            xj = xl[src]
            h = jax.nn.leaky_relu(xj + xr[dst] + ee, SLOPE)
            logits = h @ att
            m = jax.ops.segment_max(logits, dst, n)
            ex = jnp.exp(logits - m[dst])
            denom = jax.ops.segment_sum(ex, dst, n)
            alpha = ex / denom[dst]
            out = jax.ops.segment_sum(xj * alpha[:, None], dst, n)
            return out + b

        def _bn_train(x, g, b):
            mu = jnp.mean(x, axis=0)
            var = jnp.var(x, axis=0)
            return (x - mu) * jax.lax.rsqrt(var + EPS) * g + b

        def _prelu(x, a):
            return jnp.where(x >= 0, x, a * x)
        n = x.shape[0]
        src, dst, eattr = _add_self_loops(edge_index[0], edge_index[1], edge_attr, n)
        residual = x
        h = _gatv2(x, src, dst, eattr, Wl1, Wr1, We1, att1, b1, n)
        h = _prelu(_bn_train(h, g1, beta1), a1)
        h = _gatv2(h, src, dst, eattr, Wl2, Wr2, We2, att2, b2, n)
        h = _bn_train(h, g2, beta2)
        return _prelu(residual + h, a2)

    def _L2_gnn_ref(x, edge_index, edge_weight, W, att_src, att_dst, bias):
        import jax, jax.numpy as jnp
        import numpy as np
        N, E, DIN, H, DOUT = (3125, 50000, 256, 4, 64)
        NEG_SLOPE = 0.2
        src, dst = (edge_index[0], edge_index[1])
        h = (x @ W).reshape(-1, H, DOUT)
        a_src = jnp.einsum('nhd,hd->nh', h, att_src)
        a_dst = jnp.einsum('nhd,hd->nh', h, att_dst)
        e = jax.nn.leaky_relu(a_src[src] + a_dst[dst], NEG_SLOPE)
        m = jax.ops.segment_max(e, dst, num_segments=N)
        m = jnp.where(jnp.isfinite(m), m, 0.0)
        ex = jnp.exp(e - m[dst])
        s = jax.ops.segment_sum(ex, dst, num_segments=N)
        alpha = ex / jnp.where(s[dst] > 0, s[dst], 1.0)
        msgs = alpha[:, :, None] * h[src]
        out = jax.ops.segment_sum(msgs, dst, num_segments=N)
        out = out.reshape(-1, H * DOUT) + bias
        return jax.nn.sigmoid(out)

    def _L3_gnn_ref(x, edge_index, W, b):
        import jax, jax.numpy as jnp
        import numpy as np
        N_NODES = 3125
        N_EDGES = 50000
        IN_SIZE = 256
        OUT_SIZE = 256
        N = x.shape[0]
        src, dst = (edge_index[0], edge_index[1])
        deg = jnp.zeros((N,), dtype=x.dtype).at[src].add(1.0)
        dinv = deg ** (-0.5)
        loop = jnp.arange(N, dtype=src.dtype)
        src_sl = jnp.concatenate([src, loop])
        dst_sl = jnp.concatenate([dst, loop])
        coef = dinv[src_sl] * dinv[dst_sl]
        msg = x[dst_sl] * coef[:, None]
        agg = jax.ops.segment_sum(msg, src_sl, num_segments=N)
        return jax.nn.relu(agg @ W.T + b)
    edge_index = jnp.stack([src, dst])
    h = jnp.maximum(_layernorm(x, axis=-1), 0.0)
    x = x + _L0_gnn_ref(h, edge_weight, src, dst)
    h = jnp.maximum(_layernorm(x, axis=-1), 0.0)
    x = x + _L1_gnn_ref(h, edge_index, edge_attr_2, L1_gnn_Wl1, L1_gnn_Wr1, L1_gnn_We1, L1_gnn_att1, L1_gnn_b1, L1_gnn_g1, L1_gnn_beta1, L1_gnn_a1, L1_gnn_Wl2, L1_gnn_Wr2, L1_gnn_We2, L1_gnn_att2, L1_gnn_b2, L1_gnn_g2, L1_gnn_beta2, L1_gnn_a2)
    h = jnp.maximum(_layernorm(x, axis=-1), 0.0)
    x = x + _L2_gnn_ref(h, edge_index, edge_weight, L2_gnn_W, L2_gnn_att_src, L2_gnn_att_dst, L2_gnn_bias)
    h = jnp.maximum(_layernorm(x, axis=-1), 0.0)
    x = x + _L3_gnn_ref(h, edge_index, L3_gnn_W, L3_gnn_b)
    return x

_drawn_inputs = setup_inputs


def setup_inputs(seed=0):
    import zlib

    import numpy as np

    out = dict(_drawn_inputs(seed))
    spreads = {'L1_gnn_b1': (0.0, 0.8),
     'L1_gnn_g1': (1.0, 0.2),
     'L1_gnn_beta1': (0.0, 0.351),
     'L1_gnn_b2': (0.0, 0.8),
     'L1_gnn_g2': (1.0, 0.2),
     'L1_gnn_beta2': (0.0, 0.1),
     'L2_gnn_bias': (0.0, 0.714)}
    factors = {'L1_gnn_We1': 2.699,
     'L1_gnn_We2': 4.716,
     'L2_gnn_att_src': 7.042,
     'L2_gnn_att_dst': 8.0,
     'L3_gnn_b': 4.78}
    for name, (base, spread) in spreads.items():
        noise = np.random.default_rng([zlib.crc32(name.encode()), seed]).standard_normal(out[name].shape)
        drawn = base * np.exp(spread * noise) if base else spread * noise
        out[name] = jnp.asarray(drawn.astype(out[name].dtype))
    for name, factor in factors.items():
        out[name] = (out[name] * factor).astype(out[name].dtype)
    return out
```

```python
import concourse.bass as bass
from concourse import mybir
from concourse.alu_op_type import AluOpType as ALU
from contextlib import ExitStack, contextmanager

F32 = mybir.dt.float32
BF16 = mybir.dt.bfloat16
I32 = mybir.dt.int32
ACT = mybir.ActivationFunctionType
AX = mybir.AxisListType

P = 128
N = 3125
NB = (N + P - 1) // P
NP = NB * P
D = 256
E = 100000
T = 4
WIN = T * P
NW = (E + WIN - 1) // WIN
EP = NW * WIN
NG = NW + NB - 1
U = 10
R = 5
TURNS = NG // U
TW = 264
HEADS = 4
DH = D // HEADS
DUMP = NP
BIG = 1.0e30
SLOPE = 0.2
EPS = 1e-5
WH = NW // 2
GH = [(0, P), (P, NG - P)]
assert NG % U == 0 and U % R == 0 and NW % 2 == 0


def flat(ap):
    return ap.rearrange("p a c -> p (a c)")


def blk(t, b, lo, hi):
    return flat(t[:, bass.ds(b, 1), lo:hi])


def mid(ap, n):
    return ap.unsqueeze(1).to_broadcast([ap.shape[0], n, ap.shape[1]])


def last(ap, n):
    return ap.unsqueeze(2).to_broadcast([ap.shape[0], ap.shape[1], n])


def drow(t, g):
    return t[bass.ds(g, 1), :].rearrange("a n -> (a n)")


def pipelined(eng, stages):
    deepest = max(lag for lag, _ in stages)
    for s in range(U):
        for lag, stage in stages:
            if s >= lag:
                stage(s - lag, s - lag, 0)
    with eng.Fori(1, TURNS) as i:
        for s in range(U):
            for lag, stage in stages:
                u, turn = (s - lag, i) if s >= lag else (s - lag + U, i - 1)
                stage(turn * U + u, u, turn)
    for s in range(deepest):
        for lag, stage in stages:
            if s < lag:
                stage(NG + s - lag, (s - lag) % U, TURNS - 1)


def after(eng, sem, t, back=0, each=1):
    if not isinstance(t, int) or t >= back:
        eng.wait_ge(sem, (t - back + 1) * each)


def nth(u, turn, ring):
    return turn * (U // ring) + (u // ring + 1)


class Semaphores:

    def __init__(self, nc, stage):
        self.nc, self.stage, self.used = nc, stage, []

    def sem(self, what):
        self.used.append(self.nc.alloc_semaphore(f"{self.stage}_{what}"))
        return self.used[-1]

    def sems(self, what, n):
        return [self.sem(f"{what}{i}") for i in range(n)]


@contextmanager
def stage_of(nc, name):
    st = Semaphores(nc, name)
    with nc.Block() as block:
        yield st, block
    nc.clear_and_free_semaphores(st.used)
    nc.all_engine_barrier()


class Memory:
    pass


def constants(nc, m, a):
    with stage_of(nc, "const") as (st, block):
        loaded, zeroed, made, step = st.sem("loaded"), st.sem("zeroed"), st.sem("made"), st.sem("step")

        @block.sync
        def _(sp):
            loads = [(m.x[:, :, :], a["x"].rearrange("(b p) c -> p b c", p=P))]
            loads += [(t[:, :], a[k].partition_broadcast(P)) for k, t in m.bc.items()]
            loads += [(t[:, r, :], a[k][r].partition_broadcast(P)) for k, t in m.We_bc.items() for r in (0, 1)]
            loads += [(t[:, :], a[k]) for k, t in m.We.items()]
            for dst, src in loads:
                sp.dma_start(dst, src).then_inc(loaded, 16)
            sp.wait_ge(made, 1)
            count = 0
            for acc in (m.sum0, m.sum3):
                for j in range(T):
                    rows = acc[j].rearrange("(b p) c -> p b c", p=P)
                    sp.dma_start(rows, m.acc[:, 0:NB + 1, 0:rows.shape[2]]).then_inc(zeroed, 16)
                    count += 16
            sp.wait_ge(loaded, 16 * len(loads))
            sp.wait_ge(zeroed, count)

        @block.gpsimd
        def _(pool):
            nc.gpsimd.memset(m.acc[:, :, :], 0.0).then_inc(made, 1)
            nc.gpsimd.memset(m.ident[:, :], 0.0).then_inc(made, 1)
            nc.gpsimd.memset(m.before[:, :], 0.0).then_inc(made, 1)
            nc.gpsimd.iota(m.icol[:, :], [[0, 1]], base=0, channel_multiplier=1,
                           allow_small_or_imprecise_dtypes=True).then_inc(made, 1)
            nc.gpsimd.iota(m.irow[:, :], [[1, P]], base=0, channel_multiplier=0,
                           allow_small_or_imprecise_dtypes=True).then_inc(made, 1)
            pool.wait_ge(made, 3)
            nc.gpsimd.affine_select(out=m.ident[:, :], in_=m.ident[:, :], compare_op=ALU.not_equal, fill=1.0,
                                    base=0, pattern=[[-1, P]], channel_multiplier=1).then_inc(made, 1)
            nc.gpsimd.affine_select(out=m.before[:, :], in_=m.before[:, :], compare_op=ALU.is_ge, fill=1.0,
                                    base=0, pattern=[[1, P]], channel_multiplier=-1).then_inc(made, 1)

        @block.vector
        def _(dve):
            dve.wait_ge(made, 7)
            nc.vector.tensor_copy(m.ident_bf[:, :], m.ident[:, :]).then_inc(step, 1)
            nc.vector.tensor_scalar(m.real[:, :], m.icol[:, :], float(N - (NB - 1) * P), 1.0 / N,
                                    ALU.is_lt, ALU.mult).then_inc(step, 1)
            nc.vector.memset(m.mean_w[:, 0, :], 1.0 / N).then_inc(step, 1)
            nc.vector.tensor_scalar(m.dumprow[:, :], m.icol[:, :], float(DUMP), None, ALU.add).then_inc(step, 1)
            nc.vector.memset(m.attr[:, :, :], 0.0).then_inc(step, 1)
            nc.vector.memset(m.top[:, :, :], 0.0).then_inc(step, 1)
            nc.vector.memset(m.adst[:, :, :], 0.0).then_inc(step, 1)
            nc.vector.memset(m.h[:, NB, :], 0.0).then_inc(step, 1)
            for r in range(R):
                nc.vector.memset(m.ea3[r][:, 2, :], 1.0).then_inc(step, 1)
            for H in (1, HEADS):
                K = T * H * 3
                rows = m.ident[0:K, 0:K].rearrange("k (j h s) -> k j h s", j=T, h=H)
                nc.vector.tensor_reduce(m.of_tile[H][:, :], rows, AX.XY, ALU.add).then_inc(step, 1)
                nc.vector.tensor_reduce(m.of_head[H][:, :], rows.rearrange("k j h s -> k h j s"), AX.XY,
                                        ALU.add).then_inc(step, 1)
            dve.wait_ge(step, 12 + R)
            nc.vector.tensor_copy(m.mean_w[:, 1, :], m.real[:, 0:1].to_broadcast([P, P])).then_inc(step, 1)
            for H in (1, HEADS):
                nc.vector.tensor_copy(m.tilesel[H][:, :, :], last(m.of_tile[H][:, :], P)).then_inc(step, 1)
                nc.vector.tensor_copy(m.headsel[H][:, :, :], last(m.of_head[H][:, :], P)).then_inc(step, 1)


def group_list(nc, m, a):
    with stage_of(nc, "list") as (st, block):
        loaded, step, spread = st.sem("loaded"), st.sem("step"), st.sem("spread")
        picked, windows, laid, done = st.sem("picked"), st.sem("windows"), st.sem("laid"), st.sem("done")
        local = st.sem("local")
        stage = m.h[:, 0:NB, :].rearrange("p b c -> p (b c)")
        part = [[stage[:, (5 * hh + q) * WIN:(5 * hh + q + 1) * WIN] for q in range(5)] for hh in (0, 1)]
        sb = m.list
        ps = m.ps[0]

        @block.sync
        def _(sp):
            ends_of = a["dst"].rearrange("(h p n) -> p h n", p=WH, n=WIN)
            with nc.allow_non_contiguous_dma(reason="the two ends of each window"):
                sp.dma_start(sb["ends"][:, 0:2], ends_of[:, :, 0]).then_inc(loaded, 16)
                sp.dma_start(sb["ends"][:, 2:4], ends_of[:, :, WIN - 1]).then_inc(loaded, 16)
            sp.wait_ge(picked, 1)
            for hh, (g0, k) in enumerate(GH):
                sp.dma_start(m.block_of[g0:g0 + k].rearrange("(k a) -> k a", a=1),
                             sb["b_int"][0:k, hh:hh + 1]).then_inc(laid, 16)
            sp.wait_ge(windows, 16 * 10)
            sp.wait_ge(local, 2)
            for hh, (g0, k) in enumerate(GH):
                for q, t in enumerate((m.g_src, None, m.g_ea[0], m.g_ea[1], m.g_ew)):
                    if t is not None:
                        src = part[hh][q][0:k, :]
                        sp.dma_start(t[g0:g0 + k, :], src.bitcast(I32) if q == 0 else src).then_inc(laid, 16)
                sp.dma_start(m.g_loc[g0:g0 + k, :], sb["loc"][0:k, hh, :]).then_inc(laid, 16)
                sp.dma_start(m.g_locb[g0:g0 + k, :], sb["locb"][0:k, hh, :]).then_inc(laid, 16)
            sp.wait_ge(laid, 16 * 14)
            sp.dma_start(m.tab[0:1, 0:NG], m.block_of[0:NG].rearrange("(a g) -> a g", a=1)).then_inc(done, 16)
            sp.wait_ge(done, 16)

        @block.tensor
        def _(pe):
            pe.wait_ge(step, 3)
            for q in range(4):
                mm = nc.tensor.matmul(ps[:, q * WH:(q + 1) * WH], sb["spread"][:, q, :], m.ident[0:WH, 0:WH],
                                      start=True, stop=True)
            mm.then_inc(spread, 1)

        @block.vector
        def _(dve):
            count = [0]

            def link(ins):
                count[0] += 1
                ins.then_inc(step, 1)
                dve.wait_ge(step, count[0])

            dve.wait_ge(loaded, 32)
            link(nc.vector.tensor_scalar(sb["ends"][:, :], sb["ends"][:, :], 7, None, ALU.logical_shift_right))
            link(nc.vector.tensor_copy(sb["ends_f"][:, :], sb["ends"][:, :]))
            link(nc.vector.tensor_copy(sb["spread"][:, :, :], last(sb["ends_f"][:, :], P)))
            dve.wait_ge(spread, 1)
            link(nc.vector.tensor_copy(sb["fl"][:, :], ps[:, 0:2 * NW]))
            first, final = sb["fl"][:, 0:NW], sb["fl"][:, NW:2 * NW]
            link(nc.vector.tensor_tensor(sb["cnt"][:, :], final, first, ALU.subtract))
            link(nc.vector.tensor_scalar(sb["cnt"][:, :], sb["cnt"][:, :], 1.0, None, ALU.add))
            link(nc.vector.memset(sb["one"][:, :], 1.0))
            link(nc.vector.tensor_tensor_scan(sb["off"][:, :], sb["one"][:, :], sb["cnt"][:, :], 0.0,
                                              ALU.mult, ALU.add))
            link(nc.vector.tensor_tensor(sb["off"][:, :], sb["off"][:, :], sb["cnt"][:, :], ALU.subtract))
            for hh in (0, 1):
                gid, w, o, b = (sb[k][:, hh:hh + 1] for k in ("gid", "w", "o", "b"))
                link(nc.vector.tensor_scalar(gid, m.icol[:, :], float(P * hh), None, ALU.add))
                link(nc.vector.tensor_scalar(sb["one"][:, :], sb["off"][:, :], gid, None, ALU.is_le))
                link(nc.vector.tensor_reduce(w, sb["one"][:, :], AX.X, ALU.add))
                link(nc.vector.tensor_scalar(w, w, 1.0, None, ALU.subtract))
                link(nc.vector.tensor_tensor(sb["cnt"][:, :], sb["one"][:, :], sb["off"][:, :], ALU.mult))
                link(nc.vector.tensor_reduce(o, sb["cnt"][:, :], AX.X, ALU.max))
                link(nc.vector.tensor_tensor(sb["cnt"][:, :], sb["one"][:, :], first, ALU.mult))
                link(nc.vector.tensor_reduce(b, sb["cnt"][:, :], AX.X, ALU.max))
                link(nc.vector.tensor_tensor(b, b, gid, ALU.add))
                link(nc.vector.tensor_tensor(b, b, o, ALU.subtract))
                link(nc.vector.tensor_scalar(b, b, float(NB), None, ALU.min))
            link(nc.vector.tensor_copy(sb["w_int"][:, :], sb["w"][:, :]))
            link(nc.vector.tensor_scalar(sb["base"][:, :], sb["b"][:, :], float(P), None, ALU.mult))
            nc.vector.tensor_copy(sb["b_int"][:, :], sb["b"][:, :]).then_inc(picked, 1)
            dve.wait_ge(windows, 16 * 10)
            for hh, (g0, k) in enumerate(GH):
                loc = sb["loc"][0:k, hh, :]
                link(nc.vector.tensor_scalar(loc, part[hh][1][0:k, :].bitcast(I32), sb["base"][0:k, hh:hh + 1], -1.0,
                                             ALU.subtract, ALU.max))
                link(nc.vector.tensor_scalar(loc, loc, float(P), None, ALU.min))
                nc.vector.tensor_copy(sb["locb"][0:k, hh, :], loc).then_inc(local, 1)

        @block.gpsimd
        def _(pool):
            pool.wait_ge(picked, 1)
            for hh, (g0, k) in enumerate(GH):
                for q, name in enumerate(("src", "dst", "ea0", "ea1", "edge_weight")):
                    out = part[hh][q][0:k, :]
                    pool.indirect_dma_start(out.bitcast(I32) if q < 2 else out, None,
                                            a[name].rearrange("(w n) -> w n", n=WIN),
                                            bass.IndirectOffsetOnAxis(sb["w_int"][0:k, hh:hh + 1], 0)
                                            ).then_inc(windows, 16)


def layer_norm(nc, m, name):
    with stage_of(nc, name) as (st, block):
        stats, step, root = st.sem("stats"), st.sem("step"), st.sem("root")

        @block.scalar
        def _(act):
            act.wait_ge(step, 1)
            nc.scalar.activation(m.rstd[:, :], m.mv[:, :, 1], ACT.Sqrt).then_inc(root, 1)

        @block.vector
        def _(dve):
            for b in range(NB):
                nc.vector.bn_stats(m.st6[:, b, :], m.x[:, b, :]).then_inc(stats, 1)
            for b in range(NB):
                dve.wait_ge(stats, b + 1)
                nc.vector.bn_aggr(m.mv[:, b, :], m.st6[:, b, :]).then_inc(stats, 1)
            dve.wait_ge(stats, 2 * NB)
            nc.vector.tensor_scalar(m.mv[:, :, 1], m.mv[:, :, 1], EPS, None, ALU.add).then_inc(step, 1)
            dve.wait_ge(root, 1)
            nc.vector.reciprocal(m.rstd[:, :], m.rstd[:, :]).then_inc(step, 1)
            dve.wait_ge(step, 2)
            for b in range(NB):
                nc.vector.tensor_scalar(m.h[:, b, :], m.x[:, b, :], m.mv[:, b, 0:1], m.rstd[:, b:b + 1],
                                        ALU.subtract, ALU.mult).then_inc(step, 1)
            dve.wait_ge(step, 2 + NB)
            nc.vector.tensor_scalar(m.h[:, 0:NB, :], m.h[:, 0:NB, :], 0.0, None, ALU.max).then_inc(step, 1)


def scatter_loop(nc, m, name, sums, weighted):
    W = D + 1 if weighted else D
    spare = m.xr[:, :, :].rearrange("p b c -> p (b c)")
    spare2 = m.acc[:, :, :].rearrange("p b c -> p (b c)")
    tiles = [spare[:, q * WIN:(q + 1) * WIN].rearrange("p (j e) -> p j e", j=T) for q in range(2 * R)]
    eqw, pick = tiles[:R], tiles[R:]
    srow = [spare2[:, r * WIN:(r + 1) * WIN].bitcast(I32) for r in range(R)]
    eqb = spare2[:, R * WIN:(R + 1) * WIN].rearrange("p (j e) -> p j e", j=T)
    eq = [spare2[:, (R + 1 + r) * WIN:(R + 2 + r) * WIN].rearrange("p (j e) -> p j e", j=T) for r in range(R)]
    oh, y = m.ohT, m.gath
    with stage_of(nc, name) as (st, block):
        arrived = st.sems("arrived", R)
        eq_made, inb_made, matrices = st.sem("eq_made"), st.sem("inb_made"), st.sem("matrices")
        repeats, targets = st.sem("repeats"), st.sem("targets")
        multiplied, pick_ready, rows_made = st.sem("multiplied"), st.sem("pick_ready"), st.sem("rows_made")
        act_copied, dve_copied, attr_added = st.sem("act_copied"), st.sem("dve_copied"), st.sem("attr_added")
        added, begun = st.sems("added", T), st.sem("begun")
        n_loads = 6 if weighted else 3

        @block.sync
        def _(sp):
            def load(t, u, turn):
                r = u % R
                for j in range(T):
                    after(sp, added[j], t, R, 16)

                def col(dst, src):
                    sp.dma_start(dst, drow(src, t).rearrange("(p j) -> p j", j=T)).then_inc(arrived[r], 16)

                col(m.src_col[r][:, :], m.g_src)
                col(m.loc[r][:, :], m.g_loc)
                sp.dma_start(srow[r], drow(m.g_src, t).partition_broadcast(P)).then_inc(arrived[r], 16)
                if weighted:
                    col(m.ew[r][:, :], m.g_ew)
                    col(m.ea3[r][:, 0, :], m.g_ea[0])
                    col(m.ea3[r][:, 1, :], m.g_ea[1])

            pipelined(sp, [(0, load)])
            for j in range(T):
                sp.wait_ge(added[j], 16 * NG)

        @block.vector
        def _(dve):
            def make_matrices(t, u, turn):
                r = u % R
                dve.wait_ge(arrived[r], 16 * n_loads * nth(u, turn, R))
                nc.vector.tensor_tensor(eq[r][:, :, :], srow[r].rearrange("p (e j) -> p j e", j=T),
                                        last(m.src_col[r][:, :], P), ALU.is_equal).then_inc(eq_made, 1)
                nc.vector.tensor_tensor(oh[r][:, :, :], mid(m.irow[:, :], T), last(m.loc[r][:, :], P),
                                        ALU.is_equal).then_inc(matrices, 1)
                dve.wait_ge(eq_made, t + 1)
                if weighted:
                    nc.vector.tensor_scalar(m.inb[r][:, :], m.loc[r][:, :], 0.0, None,
                                            ALU.is_ge).then_inc(inb_made, 1)
                    nc.vector.tensor_tensor(eqw[r][:, :, :], eq[r][:, :, :], last(m.ew[r][:, :], P),
                                            ALU.mult).then_inc(matrices, 1)
                    dve.wait_ge(inb_made, t + 1)
                    nc.vector.scalar_tensor_tensor(m.inb[r][:, :], m.loc[r][:, :], float(P), m.inb[r][:, :],
                                                   ALU.is_lt, ALU.mult).then_inc(matrices, 1)
                nc.vector.tensor_tensor(eqb, eq[r][:, :, :], mid(m.before[:, :], T), ALU.mult).then_inc(repeats, 1)
                nc.vector.tensor_tensor(m.away[:, :], m.dumprow[:, 0:1].to_broadcast([P, T]), m.src_col[r][:, :],
                                        ALU.subtract).then_inc(repeats, 1)
                dve.wait_ge(repeats, 4 * t + 2)
                nc.vector.tensor_reduce(m.dup[:, :], eqb, AX.X, ALU.max).then_inc(repeats, 1)
                dve.wait_ge(repeats, 4 * t + 3)
                nc.vector.tensor_tensor(m.away[:, :], m.away[:, :], m.dup[:, :], ALU.mult).then_inc(repeats, 1)
                dve.wait_ge(repeats, 4 * t + 4)
                nc.vector.tensor_tensor(m.to_row[r][:, :], m.away[:, :], m.src_col[r][:, :],
                                        ALU.add).then_inc(targets, 1)

            def copy_rows(t, u, turn):
                r = u % R
                dve.wait_ge(rows_made, t + 1)
                for j in (2, 3):
                    ins = nc.vector.tensor_copy(y[r][:, j, 0:W], m.ps[2 + j][:, 0:W])
                ins.then_inc(dve_copied, 1)
                if weighted:
                    b = nc.vector.value_load(m.tab[0:1, bass.ds(t, 1)], min_val=0, max_val=NB)
                    after(dve, attr_added, t, 1)
                    nc.vector.tensor_tensor(blk(m.attr, b, 0, 3), blk(m.attr, b, 0, 3), m.ps[6 + u % 2][:, 0:3],
                                            ALU.add).then_inc(attr_added, 1)

            pipelined(dve, [(0, make_matrices), (2, copy_rows)])

        @block.tensor
        def _(pe):
            n_mat = 3 if weighted else 1

            def pick_rows(t, u, turn):
                r = u % R
                pe.wait_ge(matrices, n_mat * (t + 1))
                pe.wait_ge(eq_made, t + 1)
                after(pe, pick_ready, t, 2)
                for j in range(T):
                    mm = nc.tensor.matmul(m.ps[u % 2][:, j * P:(j + 1) * P], oh[r][:, j, :],
                                          (eqw if weighted else eq)[r][:, j, :], start=True, stop=True)
                if weighted:
                    after(pe, attr_added, t, 2)
                    for j in range(T):
                        mm = nc.tensor.matmul(m.ps[6 + u % 2][:, 0:3], oh[r][:, j, :], m.ea3[r][:, :, j],
                                              start=(j == 0), stop=(j == T - 1))
                mm.then_inc(multiplied, 1)

            def make_rows(t, u, turn):
                r = u % R
                b = nc.tensor.value_load(m.tab[0:1, bass.ds(t, 1)], min_val=0, max_val=NB)
                pe.wait_ge(pick_ready, t + 1)
                after(pe, act_copied, t, 1)
                after(pe, dve_copied, t, 1)
                for j in range(T):
                    mm = nc.tensor.matmul(m.ps[2 + j][:, 0:D], pick[r][:, j, :], blk(m.h, b, 0, D),
                                          start=True, stop=True)
                    if weighted:
                        mm = nc.tensor.matmul(m.ps[2 + j][:, D:D + 1], eq[r][:, j, :], m.inb[r][:, j:j + 1],
                                              start=True, stop=True)
                mm.then_inc(rows_made, 1)

            pipelined(pe, [(0, pick_rows), (1, make_rows)])

        @block.scalar
        def _(act):
            def copy_pick(t, u, turn):
                r = u % R
                act.wait_ge(multiplied, t + 1)
                nc.scalar.copy(pick[r][:, :, :].rearrange("p j e -> p (j e)"), m.ps[u % 2][:, :]).then_inc(pick_ready, 1)

            def copy_rows(t, u, turn):
                r = u % R
                act.wait_ge(rows_made, t + 1)
                for j in (0, 1):
                    ins = nc.scalar.copy(y[r][:, j, 0:W], m.ps[2 + j][:, 0:W])
                ins.then_inc(act_copied, 1)

            pipelined(act, [(0, copy_pick), (1, copy_rows)])

        @block.gpsimd
        def _(pool):
            def add_rows(t, u, turn):
                r = u % R
                for sem in (act_copied, dve_copied, targets):
                    pool.wait_ge(sem, t + 1)
                for j in range(T):
                    after(pool, added[j], t, 1, 16)
                pool.sem_inc(begun, 1)
                for j in range(T):
                    pool.indirect_dma_start(sums[j], bass.IndirectOffsetOnAxis(m.to_row[r][:, j:j + 1], 0),
                                            y[r][:, j, 0:W], None, compute_op=ALU.add).then_inc(added[j], 16)

            pipelined(pool, [(0, add_rows)])


def softmax_loop(nc, m, name, table, H):
    C = T * H
    K = 3 * C
    WA = D + 1 if H == 1 else HEADS * (DH + 1)
    att, We = m.att, m.We_now
    with stage_of(nc, name) as (st, block):
        arrived, gathered = st.sems("arrived", R), st.sems("gathered", R)
        begun, place, mixed = st.sem("begun"), st.sem("place"), st.sem("mixed")
        summed, leaked, logits = st.sem("summed"), st.sem("leaked"), st.sem("logits")
        hi_made, rest_made, mid_made, parts = (st.sem(k) for k in ("hi_made", "rest_made", "mid_made", "parts"))
        turned, spread, shown = st.sem("turned"), st.sem("spread"), st.sem("shown")
        seen, raised, top_set, new_top = (st.sem(k) for k in ("seen", "raised", "top_set", "new_top"))
        shrink, top_here, below, depth = st.sem("shrink"), st.sem("top_here"), st.sem("below"), st.sem("depth")
        exps, weights, scaled, group_sum, done = (st.sem(k) for k in ("exps", "weights", "scaled", "group_sum", "done"))
        rescaled = st.sem("rescaled")
        n_loads = 5 if H == 1 else 3
        ps = m.ps
        zb = [m.psum[:, 2 * q:2 * q + 2, :].rearrange("p a (c f) -> p (a c) f", f=D) for q in (0, 1)]
        shown_ps = m.psum[:, 4:5, :] if H == 1 else m.psum[:, 0:4, :]
        adst_ps, sum_ps, turn_ps, here_ps = ps[4], ps[5], ps[6], ps[7]

        @block.sync
        def _(sp):
            def load(t, u, turn):
                r = u % R
                after(sp, done, t, R)

                def col(dst, src):
                    sp.dma_start(dst, drow(src, t).rearrange("(p j) -> p j", j=T)).then_inc(arrived[r], 16)

                col(m.src_col[r][:, :], m.g_src)
                col(m.loc[r][:, :], m.g_loc)
                sp.dma_start(m.locrow[r][:, :], drow(m.g_locb, t).partition_broadcast(P)).then_inc(arrived[r], 16)
                if H == 1:
                    for c in (0, 1):
                        sp.dma_start(m.eaT[r][c:c + 1, :], m.g_ea[c][bass.ds(t, 1), :]).then_inc(arrived[r], 16)

            pipelined(sp, [(0, load)])

        @block.gpsimd
        def _(pool):
            def gather(t, u, turn):
                r = u % R
                pool.wait_ge(arrived[r], 16 * n_loads * nth(u, turn, R))
                pool.sem_inc(begun, 1)
                for j in range(T):
                    pool.indirect_dma_start(m.gath[r][:, j, :], None, table,
                                            bass.IndirectOffsetOnAxis(m.src_col[r][:, j:j + 1], 0)
                                            ).then_inc(gathered[r], 16)

            pipelined(pool, [(0, gather)])

        @block.vector
        def _(dve):
            def make_places(t, u, turn):
                r = u % R
                dve.wait_ge(arrived[r], 16 * n_loads * nth(u, turn, R))
                rows = m.locrow[r][:, :].rearrange("p (e j) -> p j e", j=T)
                nc.vector.tensor_scalar(m.ohT[r][:, :, :], rows, m.icol[:, 0:1], None, ALU.is_equal)
                nc.vector.tensor_scalar(m.off[r][:, :, :], rows, m.icol[:, 0:1], -BIG, ALU.not_equal,
                                        ALU.mult).then_inc(place, 1)

            def sum_inputs(t, u, turn):
                r = u % R
                dve.wait_ge(mixed, t + 1)
                dve.wait_ge(gathered[r], 16 * T * nth(u, turn, R))
                if H == 1:
                    nc.vector.tensor_tensor(m.zs[:, :, :], zb[u % 2], m.gath[r][:, :, 0:D], ALU.add).then_inc(summed, 1)
                else:
                    nc.vector.tensor_tensor(m.e4[:, :, :], adst_ps[:, 0:C].rearrange("p (j h) -> p j h", h=H),
                                            m.gath[r][:, :, WA:WA + H], ALU.add).then_inc(summed, 1)

            def make_logits(t, u, turn):
                r = u % R
                lg = m.lg[r][:, 0:C]
                dve.wait_ge(summed, t + 1)
                if H == 1:
                    nc.vector.scalar_tensor_tensor(m.zs[:, :, :], m.zs[:, :, :], SLOPE, m.zs[:, :, :], ALU.mult,
                                                   ALU.max).then_inc(leaked, 1)
                    dve.wait_ge(leaked, t + 1)
                    nc.vector.tensor_tensor(m.zs[:, :, :], m.zs[:, :, :], mid(att[:, :], T), ALU.mult).then_inc(scaled, 1)
                    dve.wait_ge(scaled, t + 1)
                    nc.vector.tensor_reduce(lg, m.zs[:, :, :], AX.X, ALU.add).then_inc(logits, 1)
                else:
                    e4 = m.e4[:, :, :].rearrange("p j h -> p (j h)")
                    nc.vector.scalar_tensor_tensor(lg, e4, SLOPE, e4, ALU.mult, ALU.max).then_inc(logits, 1)
                hi, md, lo = (m.parts[r][:, 0:K].rearrange("p (c s) -> p c s", s=3)[:, :, s] for s in range(3))
                dve.wait_ge(logits, t + 1)
                nc.vector.tensor_copy(hi, lg).then_inc(hi_made, 1)
                dve.wait_ge(hi_made, t + 1)
                nc.vector.tensor_tensor(m.rest[:, 0:C], lg, hi, ALU.subtract).then_inc(rest_made, 1)
                dve.wait_ge(rest_made, t + 1)
                nc.vector.tensor_copy(md, m.rest[:, 0:C]).then_inc(mid_made, 1)
                dve.wait_ge(mid_made, t + 1)
                nc.vector.tensor_tensor(lo, m.rest[:, 0:C], md, ALU.subtract).then_inc(parts, 1)

            def spread_parts(t, u, turn):
                r = u % R
                dve.wait_ge(turned, t + 1)
                nc.vector.tensor_tensor(m.rows[u % 2][0:K, :, :], mid(turn_ps[0:K, 0:P], T), m.tilesel[H][:, :, :],
                                        ALU.mult).then_inc(spread, 1)

            def raise_top(t, u, turn):
                r = u % R
                b = nc.vector.value_load(m.tab[0:1, bass.ds(t, 1)], min_val=0, max_val=NB)
                dve.wait_ge(shown, t + 1)
                nc.vector.tensor_reduce(m.seen[:, 0:H], shown_ps, AX.X, ALU.max).then_inc(seen, 1)
                after(dve, top_set, t, 1)
                dve.wait_ge(seen, t + 1)
                top = blk(m.top, b, 0, H)
                nc.vector.tensor_tensor(m.new[r][:, 0:H], top, m.seen[:, 0:H], ALU.max).then_inc(raised, 1)
                dve.wait_ge(raised, t + 1)
                nc.vector.tensor_tensor(m.drop[r][:, 0:H], top, m.new[r][:, 0:H], ALU.subtract).then_inc(new_top, 1)
                dve.wait_ge(new_top, t + 1)
                nc.vector.tensor_tensor(top, top, m.seen[:, 0:H], ALU.max).then_inc(top_set, 1)

            def sink(t, u, turn):
                r = u % R
                dve.wait_ge(top_here, t + 1)
                nc.vector.tensor_tensor(m.below[:, 0:C], here_ps[:, 0:C], m.lg[r][:, 0:C],
                                        ALU.subtract).then_inc(below, 1)
                dve.wait_ge(below, t + 1)
                nc.vector.tensor_scalar(m.depth[r][:, 0:C], m.below[:, 0:C], 0.0, None, ALU.max).then_inc(depth, 1)

            def weigh(t, u, turn):
                r = u % R
                dve.wait_ge(exps, t + 1)
                if H == 1:
                    for j in range(T):
                        ins = nc.vector.tensor_scalar(m.prob[u % 2][:, j, :], m.irow[:, :], m.loc[r][:, j:j + 1],
                                                      m.ex[r][:, j:j + 1], ALU.is_equal, ALU.mult)
                    ins.then_inc(weights, 1)
                else:
                    nc.vector.tensor_tensor(m.prob[u % 2][:, :, :], mid(m.irow[:, :], T), last(m.loc[r][:, :], P),
                                            ALU.is_equal)
                    rows = m.gath[r][:, :, 0:WA].rearrange("p j (h c) -> p j h c", h=H)
                    by = m.ex[r][:, 0:C].rearrange("p (j h) -> p j h", h=H).unsqueeze(3).to_broadcast([P, T, H, DH + 1])
                    nc.vector.tensor_tensor(rows, rows, by, ALU.mult).then_inc(weights, 1)

            def add_group(t, u, turn):
                r = u % R
                b = nc.vector.value_load(m.tab[0:1, bass.ds(t, 1)], min_val=0, max_val=NB)
                dve.wait_ge(group_sum, t + 1)
                dve.wait_ge(shrink, t + 1)
                after(dve, done, t, 1)
                acc = blk(m.acc, b, 0, WA)
                if H == 1:
                    nc.vector.scalar_tensor_tensor(acc, acc, m.less[r][:, 0:1], sum_ps[:, 0:WA], ALU.mult,
                                                   ALU.add).then_inc(done, 1)
                else:
                    nc.vector.tensor_tensor(acc.rearrange("p (h c) -> p h c", h=H),
                                            acc.rearrange("p (h c) -> p h c", h=H),
                                            last(m.less[r][:, 0:H], DH + 1), ALU.mult).then_inc(rescaled, 1)
                    dve.wait_ge(rescaled, t + 1)
                    nc.vector.tensor_tensor(acc, acc, sum_ps[:, 0:WA], ALU.add).then_inc(done, 1)

            pipelined(dve, [(4, add_group), (2, spread_parts), (3, sink), (0, make_places), (2, raise_top),
                            (3, weigh), (1, sum_inputs), (1, make_logits)])
            dve.wait_ge(done, NG)

        @block.scalar
        def _(act):
            def exp_shrink(t, u, turn):
                r = u % R
                act.wait_ge(new_top, t + 1)
                nc.scalar.activation(m.less[r][:, 0:H], m.drop[r][:, 0:H], ACT.Exp).then_inc(shrink, 1)

            def exp_edges(t, u, turn):
                r = u % R
                act.wait_ge(depth, t + 1)
                nc.scalar.activation(m.ex[r][:, 0:C], m.depth[r][:, 0:C], ACT.Exp, scale=-1.0).then_inc(exps, 1)

            pipelined(act, [(3, exp_edges), (2, exp_shrink)])

        @block.tensor
        def _(pe):
            def mix(t, u, turn):
                r = u % R
                b = nc.tensor.value_load(m.tab[0:1, bass.ds(t, 1)], min_val=0, max_val=NB)
                pe.wait_ge(place, t + 1)
                after(pe, summed, t, 2 if H == 1 else 1)
                for j in range(T):
                    if H == 1:
                        nc.tensor.matmul(zb[u % 2][:, j, :], m.ohT[r][:, j, :], blk(m.xr, b, 0, D),
                                         start=True, stop=False)
                        mm = nc.tensor.matmul(zb[u % 2][:, j, :],
                                              m.eaT[r][:, :].rearrange("c (e j) -> c j e", j=T)[:, j, :], We[:, :],
                                              start=False, stop=True)
                    else:
                        mm = nc.tensor.matmul(adst_ps[:, j * H:(j + 1) * H], m.ohT[r][:, j, :], blk(m.adst, b, 0, H),
                                              start=True, stop=True)
                mm.then_inc(mixed, 1)

            def turn_parts(t, u, turn):
                r = u % R
                pe.wait_ge(parts, t + 1)
                after(pe, spread, t, 1)
                nc.tensor.matmul(turn_ps[0:K, 0:P], m.parts[r][:, 0:K], m.ident_bf[:, :],
                                 start=True, stop=True).then_inc(turned, 1)

            def show_logits(t, u, turn):
                r = u % R
                pe.wait_ge(spread, t + 1)
                after(pe, seen, t, 1)
                for h in range(H):
                    nc.tensor.matmul(shown_ps[:, h, :], m.headsel[H][:, h, :],
                                     m.rows[u % 2][0:K, :, :].rearrange("k j e -> k (j e)"), start=True, stop=False)
                    mm = nc.tensor.matmul(shown_ps[:, h, :], m.ident_bf[:, :],
                                          m.off[r][:, :, :].rearrange("p j e -> p (j e)"), start=False, stop=True)
                mm.then_inc(shown, 1)

            def bring_top(t, u, turn):
                r = u % R
                pe.wait_ge(new_top, t + 1)
                after(pe, below, t, 1)
                for j in range(T):
                    mm = nc.tensor.matmul(here_ps[:, j * H:(j + 1) * H], m.ohT[r][:, j, :], m.new[r][:, 0:H],
                                          start=True, stop=True)
                mm.then_inc(top_here, 1)

            def sum_group(t, u, turn):
                r = u % R
                pe.wait_ge(weights, t + 1)
                after(pe, done, t, 1)
                for j in range(T):
                    mm = nc.tensor.matmul(sum_ps[:, 0:WA], m.prob[u % 2][:, j, :], m.gath[r][:, j, 0:WA],
                                          start=(j == 0), stop=(j == T - 1))
                mm.then_inc(group_sum, 1)

            pipelined(pe, [(2, show_logits), (0, mix), (2, bring_top), (3, sum_group), (1, turn_parts)])


def add_sums(nc, m, name):
    with stage_of(nc, name) as (st, block):
        arrived, summed, used, step = st.sems("arrived", R), st.sem("summed"), st.sem("used"), st.sem("step")

        @block.sync
        def _(sp):
            for b in range(NB):
                if b >= R:
                    sp.wait_ge(summed, b - R + 1)
                for j in range(T):
                    sp.dma_start(m.gath[b % R][:, j, 0:D + 1], m.sum0[j][b * P:(b + 1) * P, :]).then_inc(arrived[b % R], 16)

        @block.vector
        def _(dve):
            for b in range(NB):
                dve.wait_ge(arrived[b % R], 16 * T * (b // R + 1))
                if b >= 2:
                    dve.wait_ge(used, 2 * (b - 1))
                nc.vector.tensor_reduce(m.prob2[b % 2][:, 0:D + 1],
                                        m.gath[b % R][:, :, 0:D + 1].rearrange("p j c -> p c j"), AX.X,
                                        ALU.add).then_inc(summed, 1)
                dve.wait_ge(summed, b + 1)
                nc.vector.tensor_tensor(m.x[:, b, :], m.x[:, b, :], m.prob2[b % 2][:, 0:D], ALU.add).then_inc(used, 1)
                nc.vector.tensor_copy(m.deg[:, b:b + 1], m.prob2[b % 2][:, D:D + 1]).then_inc(used, 1)
            nc.vector.tensor_scalar(m.cnt[:, :], m.attr[:, 0:NB, 2], 1.0, None, ALU.max).then_inc(step, 1)
            dve.wait_ge(step, 1)
            nc.vector.reciprocal(m.cnt[:, :], m.cnt[:, :]).then_inc(step, 1)
            dve.wait_ge(step, 2)
            nc.vector.tensor_tensor(m.attr[:, 0:NB, 0:2], m.attr[:, 0:NB, 0:2], last(m.cnt[:, :], 2),
                                    ALU.mult).then_inc(step, 1)


def gatv2_nodes(nc, m, a, name, c, table):
    with stage_of(nc, name) as (st, block):
        loaded, taken, filled, written = st.sem("loaded"), st.sem("taken"), st.sem("filled"), st.sem("written")
        mixed = st.sem("mixed")
        turned, moved = st.sem("turned"), st.sem("moved")
        product = st.sem("product")

        @block.sync
        def _(sp):
            for q, k in enumerate((f"L1_gnn_Wl{c}", f"L1_gnn_Wr{c}")):
                sp.dma_start(m.w[:, :, q * D:(q + 1) * D], a[k].rearrange("(c p) n -> p c n", p=P)).then_inc(loaded, 16)
            sp.wait_ge(taken, NB)
            sp.wait_ge(filled, 2)
            sp.dma_start(table.rearrange("(b p) c -> p b c", p=P), m.acc[:, 0:NB, :]).then_inc(written, 16)
            sp.wait_ge(written, 16)

        @block.tensor
        def _(pe):
            product_by_blocks(nc, m, pe, 2 * D, loaded, 2, turned, moved, product, taken)

        @block.scalar
        def _(act):
            move_transposed(nc, m, act, turned, moved, product)

        @block.vector
        def _(dve):
            nc.vector.memset(m.acc[:, 0:NB, D:TW], 1.0).then_inc(filled, 1)
            nc.vector.memset(m.acc[:, NB, :], 0.0).then_inc(filled, 1)
            nc.vector.memset(m.xr[:, NB, :], 0.0).then_inc(filled, 1)
            n = 0
            for b in range(NB):
                dve.wait_ge(product, b + 1)
                out = m.ps[4 + b % 4]
                nc.vector.tensor_copy(m.acc[:, b, 0:D], out[:, 0:D]).then_inc(mixed, 1)
                nc.vector.tensor_copy(m.xr[:, b, :], out[:, D:2 * D]).then_inc(taken, 1)
                dve.wait_ge(mixed, n + 1)
                dve.wait_ge(taken, b + 1)
                z = m.prob2[b % 2][:, 0:D]
                nc.vector.tensor_tensor(z, m.acc[:, b, 0:D], m.xr[:, b, :], ALU.add).then_inc(mixed, 1)
                for r in (0, 1):
                    dve.wait_ge(mixed, n + 2 + r)
                    nc.vector.scalar_tensor_tensor(z, m.We_bc[f"L1_gnn_We{c}"][:, r, :], m.attr[:, b, r:r + 1], z,
                                                   ALU.mult, ALU.add).then_inc(mixed, 1)
                dve.wait_ge(mixed, n + 4)
                nc.vector.scalar_tensor_tensor(z, z, SLOPE, z, ALU.mult, ALU.max).then_inc(mixed, 1)
                dve.wait_ge(mixed, n + 5)
                nc.vector.tensor_tensor(z, z, m.bc[f"L1_gnn_att{c}"][:, :], ALU.mult).then_inc(mixed, 1)
                dve.wait_ge(mixed, n + 6)
                nc.vector.tensor_reduce(m.top[:, b, 0:1], z, AX.X, ALU.add).then_inc(mixed, 1)
                n += 7
                dve.wait_ge(mixed, n)


def product_by_blocks(nc, m, pe, n_out, loaded, n_loads, turned, moved, product, taken):
    def turn(b):
        if b >= 2:
            pe.wait_ge(moved, b - 1)
        for c in (0, 1):
            mm = nc.tensor.transpose(m.ps[b % 2][:, c * P:(c + 1) * P], m.h[:, b, c * P:(c + 1) * P], m.ident[:, :])
        mm.then_inc(turned, 1)

    pe.wait_ge(loaded, 16 * n_loads)
    turn(0)
    for b in range(NB):
        if b + 1 < NB:
            turn(b + 1)
        pe.wait_ge(moved, b + 1)
        if b >= 4:
            pe.wait_ge(taken, b - 3)
        for c in (0, 1):
            mm = nc.tensor.matmul(m.ps[4 + b % 4][:, 0:n_out], m.hT[b % 2][:, c * P:(c + 1) * P],
                                  m.w[:, c, 0:n_out], start=(c == 0), stop=(c == 1))
        mm.then_inc(product, 1)


def move_transposed(nc, m, act, turned, moved, product):
    for b in range(NB):
        act.wait_ge(turned, b + 1)
        if b >= 2:
            act.wait_ge(product, b - 1)
        nc.scalar.copy(m.hT[b % 2][:, :], m.ps[b % 2][:, 0:D]).then_inc(moved, 1)


def batch_norm(nc, m, name, c, residual):
    with stage_of(nc, name) as (st, block):
        step, means, centred, squared, variances, root, scaled = (
            st.sem(k) for k in ("step", "means", "centred", "squared", "variances", "root", "scaled"))
        biased, shifted, folded, lifted, normed, clipped = (
            st.sem(k) for k in ("biased", "shifted", "folded", "lifted", "normed", "clipped"))
        sq = [m.prob2[q][:, 0:D] for q in (0, 1)]
        mean_ps, var_ps = m.ps[0], m.ps[1]

        @block.tensor
        def _(pe):
            for b in range(NB):
                pe.wait_ge(biased, b + 1)
                mm = nc.tensor.matmul(mean_ps[:, 0:D], m.mean_w[:, b // (NB - 1), :], m.h[:, b, :],
                                      start=(b == 0), stop=(b == NB - 1))
            mm.then_inc(means, 1)
            for b in range(NB):
                pe.wait_ge(squared, b + 1)
                mm = nc.tensor.matmul(var_ps[:, 0:D], m.mean_w[:, b // (NB - 1), :], sq[b % 2],
                                      start=(b == 0), stop=(b == NB - 1))
                if b < NB - 1:
                    mm.then_inc(variances, 1)
            mm.then_inc(variances, 1)

        @block.scalar
        def _(act):
            for b in range(NB):
                act.wait_ge(centred, b + 1)
                if b >= 2:
                    act.wait_ge(variances, b - 1)
                nc.scalar.activation(sq[b % 2], m.h[:, b, :], ACT.Square).then_inc(squared, 1)
            act.wait_ge(step, 3)
            nc.scalar.activation(m.gain[:, :], m.gain[:, :], ACT.Sqrt).then_inc(root, 1)

        @block.vector
        def _(dve):
            nc.vector.reciprocal(m.cnt[:, :], m.acc[:, 0:NB, D]).then_inc(step, 1)
            dve.wait_ge(step, 1)
            for b in range(NB):
                nc.vector.scalar_tensor_tensor(m.h[:, b, :], m.acc[:, b, 0:D], m.cnt[:, b:b + 1],
                                               m.bc[f"L1_gnn_b{c}"][:, :], ALU.mult, ALU.add).then_inc(biased, 1)
            dve.wait_ge(means, 1)
            nc.vector.tensor_copy(m.mean[:, :], mean_ps[:, 0:D]).then_inc(step, 1)
            dve.wait_ge(step, 2)
            dve.wait_ge(biased, NB)
            for b in range(NB):
                nc.vector.tensor_tensor(m.h[:, b, :], m.h[:, b, :], m.mean[:, :], ALU.subtract).then_inc(centred, 1)
            dve.wait_ge(variances, NB)
            nc.vector.tensor_scalar(m.gain[:, :], var_ps[:, 0:D], EPS, None, ALU.add).then_inc(step, 1)
            dve.wait_ge(root, 1)
            nc.vector.reciprocal(m.gain[:, :], m.gain[:, :]).then_inc(step, 1)
            dve.wait_ge(step, 4)
            nc.vector.tensor_tensor(m.gain[:, :], m.gain[:, :], m.bc[f"L1_gnn_g{c}"][:, :], ALU.mult).then_inc(step, 1)
            dve.wait_ge(step, 5)
            dve.wait_ge(squared, NB)
            for b in range(NB):
                nc.vector.tensor_tensor(m.h[:, b, :], m.h[:, b, :], m.gain[:, :], ALU.mult).then_inc(scaled, 1)
            for b in range(NB):
                dve.wait_ge(scaled, b + 1)
                nc.vector.tensor_tensor(m.h[:, b, :], m.h[:, b, :], m.bc[f"L1_gnn_beta{c}"][:, :],
                                        ALU.add).then_inc(shifted, 1)
            if residual:
                for b in range(NB):
                    nc.vector.tensor_scalar(m.acc[:, b, 0:D], m.x[:, b, :], m.mv[:, b, 0:1], m.rstd[:, b:b + 1],
                                            ALU.subtract, ALU.mult).then_inc(normed, 1)
                for b in range(NB):
                    dve.wait_ge(normed, b + 1)
                    dve.wait_ge(shifted, b + 1)
                    nc.vector.scalar_tensor_tensor(m.h[:, b, :], m.acc[:, b, 0:D], 0.0, m.h[:, b, :], ALU.max,
                                                   ALU.add).then_inc(lifted, 1)
            slope = m.bc[f"L1_gnn_a{c}"][:, 0:1]
            for b in range(NB):
                dve.wait_ge(lifted if residual else shifted, b + 1)
                nc.vector.tensor_scalar(m.acc[:, b, 0:D], m.h[:, b, :], 0.0, slope, ALU.min, ALU.mult).then_inc(clipped, 1)
            for b in range(NB):
                dve.wait_ge(clipped, b + 1)
                nc.vector.scalar_tensor_tensor(m.h[:, b, :], m.h[:, b, :], 0.0, m.acc[:, b, 0:D], ALU.max,
                                               ALU.add).then_inc(folded, 1)
            if residual:
                for b in range(NB):
                    dve.wait_ge(folded, b + 1)
                    nc.vector.tensor_tensor(m.x[:, b, :], m.x[:, b, :], m.h[:, b, :], ALU.add).then_inc(step, 1)


def gat_nodes(nc, m, a, name, table):
    WA = HEADS * (DH + 1)
    with stage_of(nc, name) as (st, block):
        loaded, taken, filled, written = st.sem("loaded"), st.sem("taken"), st.sem("filled"), st.sem("written")
        turned, moved, product = st.sem("turned"), st.sem("moved"), st.sem("product")
        by_src, by_dst, cleared = st.sem("by_src"), st.sem("by_dst"), st.sem("cleared")

        @block.sync
        def _(sp):
            sp.dma_start(m.w[:, :, 0:D], a["L2_gnn_W"].rearrange("(c p) n -> p c n", p=P)).then_inc(loaded, 16)
            sp.wait_ge(by_src, 2 * NB)
            sp.wait_ge(taken, NB)
            sp.wait_ge(filled, 2)
            sp.dma_start(table.rearrange("(b p) c -> p b c", p=P), m.acc[:, 0:NB, :]).then_inc(written, 16)
            sp.wait_ge(written, 16)

        @block.tensor
        def _(pe):
            product_by_blocks(nc, m, pe, D, loaded, 1, turned, moved, product, taken)

        @block.scalar
        def _(act):
            move_transposed(nc, m, act, turned, moved, product)

        @block.vector
        def _(dve):
            heads = m.acc[:, 0:NB, 0:WA].rearrange("p b (h c) -> p b h c", h=HEADS)
            nc.vector.memset(heads[:, :, :, DH], 1.0).then_inc(filled, 1)
            nc.vector.memset(m.top[:, :, :], -BIG).then_inc(filled, 1)
            for b in range(NB):
                dve.wait_ge(product, b + 1)
                row = heads[:, b, :, 0:DH]
                nc.vector.tensor_copy(row, m.ps[4 + b % 4][:, 0:D].rearrange("p (h c) -> p h c", h=HEADS)
                                      ).then_inc(taken, 1)
                dve.wait_ge(taken, b + 1)
                for k, out, sem in (("src", m.acc[:, b, WA:WA + HEADS], by_src), ("dst", m.adst[:, b, :], by_dst)):
                    t = m.prob2[0 if k == "src" else 1][:, 0:D].rearrange("p (h c) -> p h c", h=HEADS)
                    nc.vector.tensor_tensor(t, row, m.bc[f"L2_gnn_att_{k}"][:, :].rearrange("p (h c) -> p h c", h=HEADS),
                                            ALU.mult).then_inc(sem, 1)
                    dve.wait_ge(sem, 2 * b + 1)
                    nc.vector.tensor_reduce(out, t, AX.X, ALU.add).then_inc(sem, 1)
                    dve.wait_ge(sem, 2 * b + 2)
            dve.wait_ge(written, 16)
            nc.vector.memset(m.acc[:, :, :], 0.0).then_inc(cleared, 1)


def gat_out(nc, m, name):
    WA = HEADS * (DH + 1)
    with stage_of(nc, name) as (st, block):
        step, biased, divided, opened, added = (st.sem(k) for k in ("step", "biased", "divided", "opened", "added"))
        heads = m.acc[:, 0:NB, 0:WA].rearrange("p b (h c) -> p b h c", h=HEADS)

        @block.vector
        def _(dve):
            s = m.share[:, :, :]
            nc.vector.tensor_scalar(s, heads[:, :, :, DH], 0.0, None, ALU.is_equal).then_inc(step, 1)
            dve.wait_ge(step, 1)
            nc.vector.tensor_tensor(s, s, heads[:, :, :, DH], ALU.add).then_inc(step, 1)
            dve.wait_ge(step, 2)
            nc.vector.reciprocal(s, s).then_inc(step, 1)
            dve.wait_ge(step, 3)
            for b in range(NB):
                nc.vector.tensor_tensor(m.h[:, b, :].rearrange("p (h c) -> p h c", h=HEADS), heads[:, b, :, 0:DH],
                                        last(m.share[:, b, :], DH), ALU.mult).then_inc(divided, 1)
            for b in range(NB):
                dve.wait_ge(divided, b + 1)
                nc.vector.tensor_tensor(m.h[:, b, :], m.h[:, b, :], m.bc["L2_gnn_bias"][:, :], ALU.add).then_inc(biased, 1)
            for b in range(NB):
                dve.wait_ge(opened, b + 1)
                nc.vector.tensor_tensor(m.x[:, b, :], m.x[:, b, :], m.h[:, b, :], ALU.add).then_inc(added, 1)

        @block.scalar
        def _(act):
            for b in range(NB):
                act.wait_ge(biased, b + 1)
                nc.scalar.activation(m.h[:, b, :], m.h[:, b, :], ACT.Sigmoid).then_inc(opened, 1)


def gcn_nodes(nc, m, name):
    with stage_of(nc, name) as (st, block):
        step, root = st.sem("step"), st.sem("root")

        @block.scalar
        def _(act):
            act.wait_ge(step, 2)
            nc.scalar.activation(m.dinv[:, :], m.dinv[:, :], ACT.Sqrt).then_inc(root, 1)

        @block.vector
        def _(dve):
            nc.vector.tensor_scalar(m.dinv[:, :], m.deg[:, :], 1.0e-20, None, ALU.max).then_inc(step, 1)
            dve.wait_ge(step, 1)
            nc.vector.reciprocal(m.dinv[:, :], m.dinv[:, :]).then_inc(step, 1)
            dve.wait_ge(root, 1)
            for b in range(NB):
                nc.vector.tensor_scalar(m.h[:, b, :], m.h[:, b, :], m.dinv[:, b:b + 1], None, ALU.mult).then_inc(step, 1)


def gcn_out(nc, m, a, name, out):
    with stage_of(nc, name) as (st, block):
        arrived, summed, owned, ready = st.sems("arrived", R), st.sem("summed"), st.sem("owned"), st.sem("ready")
        loaded, taken, added, stored = st.sem("loaded"), st.sem("taken"), st.sem("added"), st.sem("stored")
        turned, moved, product = st.sem("turned"), st.sem("moved"), st.sem("product")

        @block.sync
        def _(sp):
            sp.dma_start(m.w[:, :, 0:D], a["L3_gnn_WT"].rearrange("(c p) n -> p c n", p=P)).then_inc(loaded, 16)
            for b in range(NB):
                if b >= R:
                    sp.wait_ge(summed, b - R + 1)
                for j in range(T):
                    sp.dma_start(m.gath[b % R][:, j, 0:D], m.sum3[j][b * P:(b + 1) * P, :]).then_inc(arrived[b % R], 16)
            for b in range(NB):
                sp.wait_ge(added, b + 1)
                sp.dma_start(out[b * P:(b + 1) * P, :], m.x[:, b, :]).then_inc(stored, 16)
            sp.wait_ge(stored, 16 * NB)

        @block.tensor
        def _(pe):
            pe.wait_ge(ready, NB)
            product_by_blocks(nc, m, pe, D, loaded, 1, turned, moved, product, taken)

        @block.scalar
        def _(act):
            move_transposed(nc, m, act, turned, moved, product)

        @block.vector
        def _(dve):
            for b in range(NB):
                dve.wait_ge(arrived[b % R], 16 * T * (b // R + 1))
                if b >= 2:
                    dve.wait_ge(owned, b - 1)
                t = m.prob2[b % 2][:, 0:D]
                nc.vector.tensor_reduce(t, m.gath[b % R][:, :, 0:D].rearrange("p j c -> p c j"), AX.X,
                                        ALU.add).then_inc(summed, 1)
                dve.wait_ge(summed, b + 1)
                nc.vector.tensor_tensor(m.h[:, b, :], m.h[:, b, :], t, ALU.add).then_inc(owned, 1)
                dve.wait_ge(owned, b + 1)
                nc.vector.tensor_scalar(m.h[:, b, :], m.h[:, b, :], m.dinv[:, b:b + 1], None, ALU.mult).then_inc(ready, 1)
            for b in range(NB):
                dve.wait_ge(product, b + 1)
                t = m.prob2[b % 2][:, 0:D]
                if b >= 2:
                    dve.wait_ge(added, b - 1)
                nc.vector.tensor_tensor(t, m.ps[4 + b % 4][:, 0:D], m.bc["L3_gnn_b"][:, :], ALU.add).then_inc(taken, 1)
                dve.wait_ge(taken, b + 1)
                nc.vector.scalar_tensor_tensor(m.x[:, b, :], t, 0.0, m.x[:, b, :], ALU.max, ALU.add).then_inc(added, 1)


ROWS = ["L1_gnn_att1", "L1_gnn_b1", "L1_gnn_g1", "L1_gnn_beta1", "L1_gnn_a1", "L1_gnn_att2", "L1_gnn_b2",
        "L1_gnn_g2", "L1_gnn_beta2", "L1_gnn_a2", "L2_gnn_att_src", "L2_gnn_att_dst", "L2_gnn_bias", "L3_gnn_b"]


def build(nc, a, out):
    m = Memory()
    with ExitStack() as ctx:
        def sb(name, *shape, dt=F32):
            return ctx.enter_context(nc.sbuf_tensor(name, list(shape), dt))

        def ring(name, n, *shape, dt=F32):
            return [sb(f"{name}{r}", *shape, dt=dt) for r in range(n)]

        def dram(name, *shape, dt=F32):
            return nc.dram_tensor(name, shape, dt, kind="Internal").ap()

        m.x, m.h = sb("x", P, NB, D), sb("h", P, NB + 1, D)
        m.xr, m.acc = sb("xr", P, NB + 1, D), sb("acc", P, NB + 1, TW)
        m.top, m.adst, m.attr = (sb(k, P, NB + 1, 4) for k in ("top", "adst", "attr"))
        m.deg, m.dinv, m.rstd, m.cnt = (sb(k, P, NB) for k in ("deg", "dinv", "rstd", "cnt"))
        m.mv, m.st6, m.share = sb("mv", P, NB, 2), sb("st6", P, NB, 6), sb("share", P, NB, HEADS)
        m.ident, m.ident_bf, m.before = sb("ident", P, P), sb("ident_bf", P, P, dt=BF16), sb("before", P, P)
        m.icol, m.irow, m.dumprow, m.real = sb("icol", P, 1), sb("irow", P, P), sb("dumprow", P, 1), sb("real", P, 1)
        m.mean_w = sb("mean_w", P, 2, P)
        m.of_tile = {H: sb(f"of_tile{H}", 3 * T * H, T) for H in (1, HEADS)}
        m.of_head = {H: sb(f"of_head{H}", 3 * T * H, H) for H in (1, HEADS)}
        m.tilesel = {H: sb(f"tilesel{H}", 3 * T * H, T, P, dt=BF16) for H in (1, HEADS)}
        m.headsel = {H: sb(f"headsel{H}", 3 * T * H, H, P, dt=BF16) for H in (1, HEADS)}
        m.bc = {k: sb(f"{k}_rows", P, a[k].shape[0]) for k in ROWS}
        m.We = {f"L1_gnn_We{c}": sb(f"We{c}", 2, D) for c in (1, 2)}
        m.We_bc = {f"L1_gnn_We{c}": sb(f"We{c}_rows", P, 2, D) for c in (1, 2)}
        m.w, m.hT = sb("w", P, 2, 2 * D), ring("hT", 2, P, D)
        m.mean, m.gain = sb("mean", P, D), sb("gain", P, D)
        m.tab = sb("tab", 1, NG, dt=I32)
        m.src_col, m.to_row = ring("src_col", R, P, T, dt=I32), ring("to_row", R, P, T, dt=I32)
        m.loc, m.ew, m.inb = ring("loc", R, P, T), ring("ew", R, P, T), ring("inb", R, P, T)
        m.ea3, m.eaT = ring("ea3", R, P, 3, T), ring("eaT", R, 2, WIN)
        m.locrow = ring("locrow", R, P, WIN, dt=BF16)
        m.gath, m.ohT, m.prob = ring("gath", R, P, T, TW), ring("ohT", R, P, T, P), ring("prob", 2, P, T, P)
        m.off = ring("off", R, P, T, P, dt=BF16)
        m.parts, m.rows = ring("parts", R, P, 48, dt=BF16), ring("rows", 2, 48, T, P, dt=BF16)
        m.lg, m.new, m.drop, m.less, m.depth, m.ex = (
            ring(k, R, P, n) for k, n in (("lg", 16), ("new", 4), ("drop", 4), ("less", 4), ("depth", 16), ("ex", 16)))
        m.zs, m.e4, m.rest, m.below = sb("zs", P, T, D), sb("e4", P, T, HEADS), sb("rest", P, 16), sb("below", P, 16)
        m.seen, m.dup, m.away = (sb(k, P, 4) for k in ("seen", "dup", "away"))
        m.prob2 = ring("sums", 2, P, TW)
        ls = m.zs[:, :, :].rearrange("p j c -> p (j c)")
        m.list = {"ends": sb("ends", WH, 4, dt=I32), "ends_f": sb("ends_f", WH, 4), "spread": m.xr[0:WH, 6:8, :].rearrange("p b c -> p (b c)").rearrange("p (q c) -> p q c", q=4),
                  "fl": ls[:, 0:2 * NW], "cnt": ls[:, 2 * NW:3 * NW], "off": ls[:, 3 * NW:4 * NW],
                  "one": ls[:, 4 * NW:5 * NW]}
        for k in ("gid", "w", "o", "b", "base"):
            m.list[k] = sb(f"list_{k}", P, 2)
        for k in ("w_int", "b_int"):
            m.list[k] = sb(f"list_{k}", P, 2, dt=I32)
        m.list["loc"] = m.xr[:, 0:4, :].rearrange("p b c -> p (b c)").rearrange("p (h n) -> p h n", h=2)
        m.list["locb"] = m.xr[:, 4:6, :].rearrange("p b c -> p (b c)").bitcast(BF16).rearrange("p (h n) -> p h n", h=2)
        m.psum = ctx.enter_context(nc.psum_tensor("psum", [P, 8, WIN], F32))
        m.ps = [m.psum[:, q, :] for q in range(8)]
        m.g_src, m.g_loc, m.g_ew = dram("g_src", NG, WIN, dt=I32), dram("g_loc", NG, WIN), dram("g_ew", NG, WIN)
        m.g_locb, m.g_ea = dram("g_locb", NG, WIN, dt=BF16), [dram(f"g_ea{c}", NG, WIN) for c in (0, 1)]
        m.block_of = dram("block_of", 2 * P, dt=I32)
        tables = [dram(f"table{q}", NP, TW) for q in range(3)]
        m.sum0 = [dram(f"sum0_{j}", NP + P, D + 1) for j in range(T)]
        m.sum3 = [dram(f"sum3_{j}", NP + P, D) for j in range(T)]

        constants(nc, m, a)
        group_list(nc, m, a)
        layer_norm(nc, m, "ln0")
        scatter_loop(nc, m, "spmm", m.sum0, True)
        add_sums(nc, m, "spmm_out")
        layer_norm(nc, m, "ln1")
        for c in (1, 2):
            gatv2_nodes(nc, m, a, f"gatv2_{c}", c, tables[c - 1])
            m.att, m.We_now = m.bc[f"L1_gnn_att{c}"], m.We[f"L1_gnn_We{c}"]
            softmax_loop(nc, m, f"edges{c}", tables[c - 1], 1)
            batch_norm(nc, m, f"bn{c}", c, residual=(c == 2))
        layer_norm(nc, m, "ln2")
        gat_nodes(nc, m, a, "gat", tables[2])
        softmax_loop(nc, m, "gat_edges", tables[2], HEADS)
        gat_out(nc, m, "gat_out")
        layer_norm(nc, m, "ln3")
        gcn_nodes(nc, m, "gcn")
        scatter_loop(nc, m, "gcn_edges", m.sum3, False)
        gcn_out(nc, m, a, "gcn_out", out)


def kernel(**inputs):
    import numpy as np
    import concourse.bacc as bacc
    from concourse.bass_utils import run_bass_kernel_spmd

    def padded(v, n, fill):
        v = np.asarray(v)
        return np.concatenate([v, np.full((n - v.shape[0],) + v.shape[1:], fill, v.dtype)])

    arrays = {k: np.asarray(v) for k, v in inputs.items()}
    arrays["x"] = padded(arrays["x"], NP, 0)
    for k in ("src", "dst"):
        arrays[k] = padded(arrays[k], EP, NP - 1)
    ea = arrays.pop("edge_attr_2")
    for c in (0, 1):
        arrays[f"ea{c}"] = padded(ea[:, c], EP, 0)
    arrays["edge_weight"] = padded(arrays["edge_weight"], EP, 0)
    arrays["L3_gnn_WT"] = arrays.pop("L3_gnn_W").T
    for k in ROWS:
        arrays[k] = arrays[k].reshape(-1)
    arrays = {f"in_{k}": np.ascontiguousarray(v) for k, v in arrays.items()}

    nc = bacc.Bacc("TRN2", target_bir_lowering=False, num_devices=1)
    a = {k[3:]: nc.dram_tensor(k, v.shape, mybir.dt.from_np(v.dtype), kind="ExternalInput").ap()
         for k, v in arrays.items()}
    out = nc.dram_tensor("out", (NP, D), F32, kind="ExternalOutput").ap()
    build(nc, a, out)
    r = run_bass_kernel_spmd(nc, [arrays], core_ids=[0])
    return r.results[0]["out"][0:N]
```

```python
import concourse.bass as bass
from concourse import mybir
from concourse.alu_op_type import AluOpType as ALU
from contextlib import ExitStack, contextmanager

F32 = mybir.dt.float32
BF16 = mybir.dt.bfloat16
I32 = mybir.dt.int32
ACT = mybir.ActivationFunctionType
AX = mybir.AxisListType

P = 128
N = 3125
NB = (N + P - 1) // P
NP = NB * P
D = 256
E = 100000
T = 4
WIN = T * P
NW = (E + WIN - 1) // WIN
EP = NW * WIN
NG = NW + NB - 1
U = 10
R = 5
TURNS = NG // U
TW = 264
HEADS = 4
DH = D // HEADS
DUMP = NP
BIG = 2.0 ** 100
SLOPE = 0.2
EPS = 1e-5
WE_PARTS = [(0, 6), (6, 10), (10, 12)]
KE = 12
WH = NW // 2
GH = [(0, P), (P, NG - P)]
assert NG % U == 0 and U % R == 0 and NW % 2 == 0


def flat(ap):
    return ap.rearrange("p a c -> p (a c)")


def blk(t, b, lo, hi):
    return flat(t[:, bass.ds(b, 1), lo:hi])


def mid(ap, n):
    return ap.unsqueeze(1).to_broadcast([ap.shape[0], n, ap.shape[1]])


def last(ap, n):
    return ap.unsqueeze(2).to_broadcast([ap.shape[0], ap.shape[1], n])


def drow(t, g):
    return t[bass.ds(g, 1), :].rearrange("a n -> (a n)")


def pipelined(eng, stages, blocks=None):
    deepest = max(lag for lag, _ in stages)
    load = blocks if blocks else lambda first, n: [None] * n
    of = load(0, U)
    for s in range(U):
        for lag, stage in stages:
            if s >= lag:
                stage(s - lag, s - lag, 0, of[s - lag])
    with eng.Fori(1, TURNS) as i:
        of = load(i * U - deepest, U + deepest)
        for s in range(U):
            for lag, stage in stages:
                u, turn = (s - lag, i) if s >= lag else (s - lag + U, i - 1)
                stage(turn * U + u, u, turn, of[s - lag + deepest])
    if deepest:
        of = load(NG - deepest, deepest)
    for s in range(deepest):
        for lag, stage in stages:
            if s < lag:
                stage(NG + s - lag, (s - lag) % U, TURNS - 1, of[s - lag + deepest])


def blocks_on(nc, m, engine):
    def load(first, n):
        _, values = nc.values_load_multi_w_load_instructions(
            m.tab[0:1, bass.ds(first, n)], engines=[engine], min_val=0, max_val=NB,
            skip_runtime_bounds_check_because="the list of groups has blocks 0 to NB only")
        return values
    return load


def after(eng, sem, t, back=0, each=1):
    if not isinstance(t, int) or t >= back:
        eng.wait_ge(sem, (t - back + 1) * each)


def nth(u, turn, ring):
    return turn * (U // ring) + (u // ring + 1)


class Semaphores:

    def __init__(self, nc, stage):
        self.nc, self.stage, self.used = nc, stage, []

    def sem(self, what):
        self.used.append(self.nc.alloc_semaphore(f"{self.stage}_{what}"))
        return self.used[-1]

    def sems(self, what, n):
        return [self.sem(f"{what}{i}") for i in range(n)]


@contextmanager
def stage_of(nc, name):
    st = Semaphores(nc, name)
    with nc.Block() as block:
        yield st, block
    nc.clear_and_free_semaphores(st.used)
    nc.all_engine_barrier()


class Memory:
    pass


def constants(nc, m, a):
    with stage_of(nc, "const") as (st, block):
        loaded, zeroed, made, step = st.sem("loaded"), st.sem("zeroed"), st.sem("made"), st.sem("step")
        replicated, split, stacked = st.sem("replicated"), st.sem("split"), st.sem("stacked")
        we_rep = {c: m.zs[0][0:KE, c - 1, :] for c in (1, 2)}
        we_rest = {c: m.zs[0][0:KE, c + 1, :] for c in (1, 2)}
        we_part = {c: [m.zs[1][0:KE, 2 * (c - 1) + s // 2, :].bitcast(BF16)[:, (s % 2) * D:(s % 2 + 1) * D]
                       for s in range(3)] for c in (1, 2)}

        @block.sync
        def _(sp):
            loads = [(m.x[:, :, :], a["x"].rearrange("(b p) c -> p b c", p=P))]
            loads += [(t[:, :], a[k].partition_broadcast(P)) for k, t in m.bc.items()]
            loads += [(t[:, r, :], a[k][r].partition_broadcast(P)) for k, t in m.We_bc.items() for r in (0, 1)]
            for c in (1, 2):
                for q in range(KE // 2):
                    sp.dma_start(we_rep[c][2 * q:2 * q + 2, :], a[f"L1_gnn_We{c}"]).then_inc(replicated, 16)
            for dst, src in loads:
                sp.dma_start(dst, src).then_inc(loaded, 16)
            sp.wait_ge(split, 8)
            for c in (1, 2):
                for s, (lo, hi) in enumerate(WE_PARTS):
                    sp.dma_start(m.We12[c][lo:hi, :], we_part[c][s][lo:hi, :]).then_inc(stacked, 16)
            sp.wait_ge(made, 1)
            count = 0
            for acc in (m.sum0, m.sum3):
                for j in range(T):
                    rows = acc[j].rearrange("(b p) c -> p b c", p=P)
                    sp.dma_start(rows, m.acc[:, 0:NB + 1, 0:rows.shape[2]]).then_inc(zeroed, 16)
                    count += 16
            sp.wait_ge(loaded, 16 * len(loads))
            sp.wait_ge(zeroed, count)
            sp.wait_ge(stacked, 16 * 2 * len(WE_PARTS))

        @block.gpsimd
        def _(pool):
            nc.gpsimd.memset(m.acc[:, :, :], 0.0).then_inc(made, 1)
            nc.gpsimd.memset(m.ident[:, :], 0.0).then_inc(made, 1)
            nc.gpsimd.memset(m.later32[:, :], 0.0).then_inc(made, 1)
            nc.gpsimd.iota(m.icol[:, :], [[0, 1]], base=0, channel_multiplier=1,
                           allow_small_or_imprecise_dtypes=True).then_inc(made, 1)
            nc.gpsimd.iota(m.irow[:, :], [[1, P]], base=0, channel_multiplier=0,
                           allow_small_or_imprecise_dtypes=True).then_inc(made, 1)
            pool.wait_ge(made, 3)
            nc.gpsimd.affine_select(out=m.ident[:, :], in_=m.ident[:, :], compare_op=ALU.not_equal, fill=1.0,
                                    base=0, pattern=[[-1, P]], channel_multiplier=1).then_inc(made, 1)
            nc.gpsimd.affine_select(out=m.later32[:, :], in_=m.later32[:, :], compare_op=ALU.is_ge, fill=1.0,
                                    base=0, pattern=[[-1, P]], channel_multiplier=1).then_inc(made, 1)

        @block.vector
        def _(dve):
            dve.wait_ge(made, 7)
            count = 0
            for ins in (
                    nc.vector.tensor_copy(m.ident_bf[:, :], m.ident[:, :]),
                    nc.vector.tensor_copy(m.later[:, :], m.later32[:, :]),
                    nc.vector.tensor_scalar(m.real[:, :], m.icol[:, :], float(N - (NB - 1) * P), 1.0 / N,
                                            ALU.is_lt, ALU.mult),
                    nc.vector.memset(m.mean_w[:, 0, :], 1.0 / N),
                    nc.vector.tensor_scalar(m.dumprow[:, :], m.icol[:, :], float(DUMP), None, ALU.add),
                    nc.vector.memset(m.one_bf[:, :], 1.0),
                    nc.vector.memset(m.minus_big[:, :], -BIG),
                    nc.vector.memset(m.attr[:, :, :], 0.0),
                    nc.vector.memset(m.top[:, :, :], 0.0),
                    nc.vector.memset(m.adst3[:, :, :], 0.0),
                    nc.vector.memset(m.h[:, NB, :], 0.0)):
                ins.then_inc(step, 1)
                count += 1
            for C, of in ((T, m.of_tile), (T * HEADS, m.of_edge)):
                nc.vector.tensor_reduce(of[:, :], m.ident[0:3 * C, 0:3 * C].rearrange("k (c s) -> k c s", s=3), AX.X,
                                        ALU.add).then_inc(step, 1)
                count += 1
            dve.wait_ge(step, count)
            nc.vector.tensor_copy(m.mean_w[:, 1, :], m.real[:, 0:1].to_broadcast([P, P])).then_inc(step, 1)
            nc.vector.tensor_copy(m.tilesel[:, :, :], last(m.of_tile[:, :], P)).then_inc(step, 1)
            nc.vector.tensor_copy(m.edgesel[:, :, :], last(m.of_edge[:, :], P)).then_inc(step, 1)
            dve.wait_ge(replicated, 16 * KE)
            count = 0
            for c in (1, 2):
                hi, md, lo = we_part[c]
                for op in (lambda: nc.vector.tensor_copy(hi, we_rep[c]),
                           lambda: nc.vector.tensor_tensor(we_rest[c], we_rep[c], hi, ALU.subtract),
                           lambda: nc.vector.tensor_copy(md, we_rest[c]),
                           lambda: nc.vector.tensor_tensor(lo, we_rest[c], md, ALU.subtract)):
                    op().then_inc(split, 1)
                    count += 1
                    dve.wait_ge(split, count)


def group_list(nc, m, a):
    with stage_of(nc, "list") as (st, block):
        loaded, step, spread = st.sem("loaded"), st.sem("step"), st.sem("spread")
        picked, windows, laid, done = st.sem("picked"), st.sem("windows"), st.sem("laid"), st.sem("done")
        local, linear, split, dots = st.sem("local"), st.sem("linear"), st.sem("split"), st.sem("dots")
        stage = m.h[:, 0:NB, :].rearrange("p b c -> p (b c)")
        part = [[stage[:, (5 * hh + q) * WIN:(5 * hh + q + 1) * WIN] for q in range(5)] for hh in (0, 1)]
        room = m.acc[:, :, :].rearrange("p b c -> p (b c)")
        lin = {c: [room[:, (2 * (c - 1) + hh) * WIN:(2 * (c - 1) + hh + 1) * WIN] for hh in (0, 1)] for c in (1, 2)}
        rest = [room[:, (4 + r) * WIN:(5 + r) * WIN] for r in (0, 1)]
        eab = [room[:, (6 + 3 * hh) * WIN:(9 + 3 * hh) * WIN].bitcast(BF16).rearrange("p (k n) -> p k n", k=6)
               for hh in (0, 1)]
        sb = m.list
        ps = m.ps[0]

        @block.sync
        def _(sp):
            ends_of = a["dst"].rearrange("(h p n) -> p h n", p=WH, n=WIN)
            with nc.allow_non_contiguous_dma(reason="the two ends of each window"):
                sp.dma_start(sb["ends"][:, 0:2], ends_of[:, :, 0]).then_inc(loaded, 16)
                sp.dma_start(sb["ends"][:, 2:4], ends_of[:, :, WIN - 1]).then_inc(loaded, 16)
            sp.wait_ge(picked, 1)
            for hh, (g0, k) in enumerate(GH):
                sp.dma_start(m.block_of[g0:g0 + k].rearrange("(k a) -> k a", a=1),
                             sb["b_int"][0:k, hh:hh + 1]).then_inc(laid, 16)
            sp.wait_ge(windows, 16 * 10)
            sp.wait_ge(local, 2)
            for hh, (g0, k) in enumerate(GH):
                for q, t in enumerate((m.g_src, None, m.g_ea[0], m.g_ea[1], m.g_ew)):
                    if t is not None:
                        src = part[hh][q][0:k, :]
                        sp.dma_start(t[g0:g0 + k, :], src.bitcast(I32) if q == 0 else src).then_inc(laid, 16)
                sp.dma_start(m.g_loc[g0:g0 + k, :], sb["loc"][0:k, hh, :]).then_inc(laid, 16)
                sp.dma_start(m.g_locb[g0:g0 + k, :], sb["locb"][0:k, hh, :]).then_inc(laid, 16)
            sp.wait_ge(linear, 4)
            sp.wait_ge(split, 2)
            for hh, (g0, k) in enumerate(GH):
                for c in (1, 2):
                    sp.dma_start(m.g_lin[c][g0:g0 + k, :], lin[c][hh][0:k, :]).then_inc(laid, 16)
                for lo, hi in WE_PARTS:
                    sp.dma_start(m.g_eaT[g0:g0 + k, lo:hi, :], eab[hh][0:k, 0:hi - lo, :]).then_inc(laid, 16)
            sp.wait_ge(laid, 16 * 24)
            sp.dma_start(m.tab[0:1, 0:NG], m.block_of[0:NG].rearrange("(a g) -> a g", a=1)).then_inc(done, 16)
            sp.wait_ge(done, 16)

        @block.tensor
        def _(pe):
            pe.wait_ge(step, 3)
            for q in range(4):
                mm = nc.tensor.matmul(ps[:, q * WH:(q + 1) * WH], sb["spread"][:, q, :], m.ident[0:WH, 0:WH],
                                      start=True, stop=True)
            mm.then_inc(spread, 1)

        @block.vector
        def _(dve):
            count = [0]

            def link(ins):
                count[0] += 1
                ins.then_inc(step, 1)
                dve.wait_ge(step, count[0])

            dve.wait_ge(loaded, 32)
            link(nc.vector.tensor_scalar(sb["ends"][:, :], sb["ends"][:, :], 7, None, ALU.logical_shift_right))
            link(nc.vector.tensor_copy(sb["ends_f"][:, :], sb["ends"][:, :]))
            link(nc.vector.tensor_copy(sb["spread"][:, :, :], last(sb["ends_f"][:, :], P)))
            dve.wait_ge(spread, 1)
            link(nc.vector.tensor_copy(sb["fl"][:, :], ps[:, 0:2 * NW]))
            first, final = sb["fl"][:, 0:NW], sb["fl"][:, NW:2 * NW]
            link(nc.vector.tensor_tensor(sb["cnt"][:, :], final, first, ALU.subtract))
            link(nc.vector.tensor_scalar(sb["cnt"][:, :], sb["cnt"][:, :], 1.0, None, ALU.add))
            link(nc.vector.memset(sb["one"][:, :], 1.0))
            link(nc.vector.tensor_tensor_scan(sb["off"][:, :], sb["one"][:, :], sb["cnt"][:, :], 0.0,
                                              ALU.mult, ALU.add))
            link(nc.vector.tensor_tensor(sb["off"][:, :], sb["off"][:, :], sb["cnt"][:, :], ALU.subtract))
            for hh in (0, 1):
                gid, w, o, b = (sb[k][:, hh:hh + 1] for k in ("gid", "w", "o", "b"))
                link(nc.vector.tensor_scalar(gid, m.icol[:, :], float(P * hh), None, ALU.add))
                link(nc.vector.tensor_scalar(sb["one"][:, :], sb["off"][:, :], gid, None, ALU.is_le))
                link(nc.vector.tensor_reduce(w, sb["one"][:, :], AX.X, ALU.add))
                link(nc.vector.tensor_scalar(w, w, 1.0, None, ALU.subtract))
                link(nc.vector.tensor_tensor(sb["cnt"][:, :], sb["one"][:, :], sb["off"][:, :], ALU.mult))
                link(nc.vector.tensor_reduce(o, sb["cnt"][:, :], AX.X, ALU.max))
                link(nc.vector.tensor_tensor(sb["cnt"][:, :], sb["one"][:, :], first, ALU.mult))
                link(nc.vector.tensor_reduce(b, sb["cnt"][:, :], AX.X, ALU.max))
                link(nc.vector.tensor_tensor(b, b, gid, ALU.add))
                link(nc.vector.tensor_tensor(b, b, o, ALU.subtract))
                link(nc.vector.tensor_scalar(b, b, float(NB), None, ALU.min))
            link(nc.vector.tensor_copy(sb["w_int"][:, :], sb["w"][:, :]))
            link(nc.vector.tensor_scalar(sb["base"][:, :], sb["b"][:, :], float(P), None, ALU.mult))
            nc.vector.tensor_copy(sb["b_int"][:, :], sb["b"][:, :]).then_inc(picked, 1)
            dve.wait_ge(windows, 16 * 10)
            for hh, (g0, k) in enumerate(GH):
                loc = sb["loc"][0:k, hh, :]
                link(nc.vector.tensor_scalar(loc, part[hh][1][0:k, :].bitcast(I32), sb["base"][0:k, hh:hh + 1], -1.0,
                                             ALU.subtract, ALU.max))
                link(nc.vector.tensor_scalar(loc, loc, float(P), None, ALU.min))
                nc.vector.tensor_copy(sb["locb"][0:k, hh, :].rearrange("p (j e) -> p j e", j=T),
                                      loc.rearrange("p (e j) -> p j e", j=T)).then_inc(local, 1)
            for c in (1, 2):
                for r in (0, 1):
                    link(nc.vector.scalar_tensor_tensor(m.junk[:, :], m.We_bc[f"L1_gnn_We{c}"][:, r, :], SLOPE,
                                                        m.bc[f"L1_gnn_att{c}"][:, :], ALU.mult, ALU.mult,
                                                        accum_out=m.ea_lin[c][:, r:r + 1]))
            for hh, (g0, k) in enumerate(GH):
                ea = [part[hh][2 + r][0:k, :] for r in (0, 1)]
                for c in (1, 2):
                    out = lin[c][hh][0:k, :]
                    link(nc.vector.tensor_scalar(out, ea[0], m.ea_lin[c][0:k, 0:1], None, ALU.mult))
                    nc.vector.scalar_tensor_tensor(out, ea[1], m.ea_lin[c][0:k, 1:2], out, ALU.mult,
                                                   ALU.add).then_inc(linear, 1)
                by_tile = [v.rearrange("p (e j) -> p j e", j=T) for v in ea]
                hi, md, lo = ([eab[hh][0:k, 2 * s + r, :].rearrange("p (j e) -> p j e", j=T) for r in (0, 1)]
                              for s in range(3))
                left = [rest[r][0:k, :].rearrange("p (j e) -> p j e", j=T) for r in (0, 1)]
                for r in (0, 1):
                    link(nc.vector.tensor_copy(hi[r], by_tile[r]))
                    link(nc.vector.tensor_tensor(left[r], by_tile[r], hi[r], ALU.subtract))
                    link(nc.vector.tensor_copy(md[r], left[r]))
                    link(nc.vector.tensor_tensor(lo[r], left[r], md[r], ALU.subtract))
                nc.vector.memset(m.junk[:, 0:1], 0.0).then_inc(split, 1)

        @block.gpsimd
        def _(pool):
            pool.wait_ge(picked, 1)
            for hh, (g0, k) in enumerate(GH):
                for q, name in enumerate(("src", "dst", "ea0", "ea1", "edge_weight")):
                    out = part[hh][q][0:k, :]
                    pool.indirect_dma_start(out.bitcast(I32) if q < 2 else out, None,
                                            a[name].rearrange("(w n) -> w n", n=WIN),
                                            bass.IndirectOffsetOnAxis(sb["w_int"][0:k, hh:hh + 1], 0)
                                            ).then_inc(windows, 16)


def layer_norm(nc, m, name):
    with stage_of(nc, name) as (st, block):
        stats, step, root = st.sem("stats"), st.sem("step"), st.sem("root")

        @block.scalar
        def _(act):
            act.wait_ge(step, 1)
            nc.scalar.activation(m.rstd[:, :], m.mv[:, :, 1], ACT.Sqrt).then_inc(root, 1)

        @block.vector
        def _(dve):
            for b in range(NB):
                nc.vector.bn_stats(m.st6[:, b, :], m.x[:, b, :]).then_inc(stats, 1)
            for b in range(NB):
                dve.wait_ge(stats, b + 1)
                nc.vector.bn_aggr(m.mv[:, b, :], m.st6[:, b, :]).then_inc(stats, 1)
            dve.wait_ge(stats, 2 * NB)
            nc.vector.tensor_scalar(m.mv[:, :, 1], m.mv[:, :, 1], EPS, None, ALU.add).then_inc(step, 1)
            dve.wait_ge(root, 1)
            nc.vector.reciprocal(m.rstd[:, :], m.rstd[:, :]).then_inc(step, 1)
            dve.wait_ge(step, 2)
            for b in range(NB):
                nc.vector.tensor_scalar(m.h[:, b, :], m.x[:, b, :], m.mv[:, b, 0:1], m.rstd[:, b:b + 1],
                                        ALU.subtract, ALU.mult).then_inc(step, 1)
            dve.wait_ge(step, 2 + NB)
            nc.vector.tensor_scalar(m.h[:, 0:NB, :], m.h[:, 0:NB, :], 0.0, None, ALU.max).then_inc(step, 1)


def scatter_loop(nc, m, name, sums, weighted):
    W = D + 1 if weighted else D
    PW = P + 3 if weighted else P
    spare = m.xr3[:, :, :].rearrange("p b c -> p (b c)").bitcast(F32)
    spare2 = m.acc[:, :, :].rearrange("p b c -> p (b c)")

    def ring_in(space, start, n, width, dt=F32):
        words = T * width * (2 if dt == BF16 else 4) // 4
        bufs = [space[:, start + r * words:start + (r + 1) * words] for r in range(n)]
        return [(t if dt == F32 else t.bitcast(dt)).rearrange("p (j e) -> p j e", j=T) for t in bufs]

    pick, eqw = ring_in(spare, 0, R, P), ring_in(spare, R * WIN, R, P + 3)
    oh = ring_in(spare, R * T * (2 * P + 3), R, P, F32 if weighted else BF16)
    srow = [spare2[:, r * WIN:(r + 1) * WIN].bitcast(I32) for r in range(R)]
    eq, eqb = ring_in(spare2, R * WIN, R, P, BF16), ring_in(spare2, 2 * R * WIN, 2, P, BF16)
    rhs = eqw if weighted else eq
    y = m.gath
    banks = [m.psum[:, 2 * q:2 * q + 2, :] for q in range(4)]
    pick_ps = [banks[q][:, :, 0:2 * PW].rearrange("p a (i c) -> p a i c", i=2) for q in (0, 1)]
    dup_ps, cnt_ps = ([banks[q][:, a, 2 * PW:2 * PW + T] for q in (0, 1)] for a in (0, 1))
    rows_ps = [banks[2 + q].rearrange("p a (i c) -> p (a i) c", i=2) for q in (0, 1)]
    with stage_of(nc, name) as (st, block):
        arrived = st.sems("arrived", R)
        eq_made, inb_made, matrices = st.sem("eq_made"), st.sem("inb_made"), st.sem("matrices")
        ones, eqb_made, away_made, moved = st.sem("ones"), st.sem("eqb_made"), st.sem("away_made"), st.sem("moved")
        targets, attr_summed, attr_added = st.sem("targets"), st.sem("attr_summed"), st.sem("attr_added")
        multiplied, pick_ready, rows_made, copied = (st.sem(k) for k in ("multiplied", "pick_ready", "rows_made", "copied"))
        added, begun = st.sems("added", T), st.sem("begun")
        n_loads = 6 if weighted else 3

        @block.sync
        def _(sp):
            def load(t, u, turn, b):
                r = u % R
                for j in range(T):
                    after(sp, added[j], t, R, 16)

                def col(dst, src):
                    sp.dma_start(dst, drow(src, t).rearrange("(p j) -> p j", j=T)).then_inc(arrived[r], 16)

                col(m.src_col[r][:, :], m.g_src)
                col(m.loc[r][:, :], m.g_loc)
                sp.dma_start(srow[r], drow(m.g_src, t).partition_broadcast(P)).then_inc(arrived[r], 16)
                if weighted:
                    col(m.ew[r][:, :], m.g_ew)
                    col(m.ea[r][:, 0, :], m.g_ea[0])
                    col(m.ea[r][:, 1, :], m.g_ea[1])

            pipelined(sp, [(0, load)])
            for j in range(T):
                sp.wait_ge(added[j], 16 * NG)

        @block.vector
        def _(dve):
            if weighted:
                for r in range(R):
                    nc.vector.memset(eqw[r][:, :, P + 2], 1.0).then_inc(ones, 1)
                dve.wait_ge(ones, R)

            def make_matrices(t, u, turn, b):
                r = u % R
                dve.wait_ge(arrived[r], 16 * n_loads * nth(u, turn, R))
                nc.vector.tensor_tensor(eq[r], srow[r].rearrange("p (e j) -> p j e", j=T),
                                        last(m.src_col[r][:, :], P), ALU.is_equal).then_inc(eq_made, 1)
                nc.vector.tensor_tensor(m.away[r][:, :], m.dumprow[:, 0:1].to_broadcast([P, T]), m.src_col[r][:, :],
                                        ALU.subtract).then_inc(away_made, 1)
                if weighted:
                    nc.vector.tensor_scalar(m.inb[r][:, :], m.loc[r][:, :], 0.0, None, ALU.is_ge).then_inc(inb_made, 1)
                    nc.vector.tensor_copy(eqw[r][:, :, P:P + 2], m.ea[r][:, :, :].rearrange("p c j -> p j c"))
                nc.vector.tensor_tensor(oh[r], mid(m.irow[:, :], T), last(m.loc[r][:, :], P),
                                        ALU.is_equal).then_inc(matrices, 1)
                if weighted:
                    dve.wait_ge(inb_made, t + 1)
                    nc.vector.scalar_tensor_tensor(m.inb[r][:, :], m.loc[r][:, :], float(P), m.inb[r][:, :],
                                                   ALU.is_lt, ALU.mult).then_inc(matrices, 1)
                    dve.wait_ge(eq_made, t + 1)
                    nc.vector.tensor_tensor(eqw[r][:, :, 0:P], eq[r], last(m.ew[r][:, :], P),
                                            ALU.mult).then_inc(matrices, 1)
                dve.wait_ge(eq_made, t + 1)
                after(dve, multiplied, t, 2)
                nc.vector.tensor_tensor(eqb[u % 2], eq[r], mid(m.later[:, :], T), ALU.mult).then_inc(eqb_made, 1)

            def finish(t, u, turn, b):
                r = u % R
                dve.wait_ge(pick_ready, t + 1)
                dve.wait_ge(away_made, t + 1)
                nc.vector.scalar_tensor_tensor(m.away[r][:, :], dup_ps[u % 2], 0.5, m.away[r][:, :], ALU.is_gt,
                                               ALU.mult).then_inc(moved, 1)
                if weighted:
                    nc.vector.tensor_copy(y[r][:, :, D], cnt_ps[u % 2])
                    after(dve, attr_added, t, 1)
                    nc.vector.tensor_reduce(m.attr_sum[:, :], pick_ps[u % 2][:, :, :, P:P + 3].rearrange("p a i c -> p c a i"),
                                            AX.XY, ALU.add).then_inc(attr_summed, 1)
                dve.wait_ge(moved, t + 1)
                nc.vector.tensor_tensor(m.to_row[r][:, :], m.away[r][:, :], m.src_col[r][:, :],
                                        ALU.add).then_inc(targets, 1)
                if weighted:
                    dve.wait_ge(attr_summed, t + 1)
                    nc.vector.tensor_tensor(blk(m.attr, b, 0, 3), blk(m.attr, b, 0, 3), m.attr_sum[:, :],
                                            ALU.add).then_inc(attr_added, 1)

            pipelined(dve, [(0, make_matrices), (1, finish)], blocks_on(nc, m, mybir.EngineType.DVE) if weighted else None)

        @block.tensor
        def _(pe):
            n_mat = 3 if weighted else 1

            def pick_rows(t, u, turn, b):
                r, q = u % R, u % 2
                pe.wait_ge(matrices, n_mat * (t + 1))
                pe.wait_ge(eqb_made, t + 1)
                after(pe, pick_ready, t, 2)
                after(pe, targets, t, 2)
                for j in range(T):
                    nc.tensor.matmul(pick_ps[q][:, j // 2, j % 2, :], oh[r][:, j, :], rhs[r][:, j, 0:PW],
                                     start=True, stop=True)
                for j in range(T):
                    mm = nc.tensor.matmul(dup_ps[q][:, j:j + 1], eqb[q][:, j, :], m.one_bf[:, :],
                                          start=True, stop=True)
                if weighted:
                    for j in range(T):
                        mm = nc.tensor.matmul(cnt_ps[q][:, j:j + 1], eq[r][:, j, :], m.inb[r][:, j:j + 1],
                                              start=True, stop=True)
                mm.then_inc(multiplied, 1)

            def make_rows(t, u, turn, b):
                r, q = u % R, u % 2
                pe.wait_ge(pick_ready, t + 1)
                after(pe, copied, t, 2)
                for j in range(T):
                    mm = nc.tensor.matmul(rows_ps[q][:, j, :], pick[r][:, j, :], blk(m.h, b, 0, D),
                                          start=True, stop=True)
                mm.then_inc(rows_made, 1)

            pipelined(pe, [(0, pick_rows), (1, make_rows)], blocks_on(nc, m, mybir.EngineType.PE))

        @block.scalar
        def _(act):
            def copy_pick(t, u, turn, b):
                r = u % R
                act.wait_ge(multiplied, t + 1)
                nc.scalar.copy(pick[r].rearrange("p (a i) e -> p a i e", i=2),
                               pick_ps[u % 2][:, :, :, 0:P]).then_inc(pick_ready, 1)

            def copy_rows(t, u, turn, b):
                r = u % R
                act.wait_ge(rows_made, t + 1)
                nc.scalar.copy(y[r][:, :, 0:D], rows_ps[u % 2]).then_inc(copied, 1)

            pipelined(act, [(0, copy_pick), (1, copy_rows)])

        @block.gpsimd
        def _(pool):
            def add_rows(t, u, turn, b):
                r = u % R
                for sem in (copied, targets):
                    pool.wait_ge(sem, t + 1)
                for j in range(T):
                    after(pool, added[j], t, 1, 16)
                    pool.sem_inc(begun, 1)
                    pool.indirect_dma_start(sums[j], bass.IndirectOffsetOnAxis(m.to_row[r][:, j:j + 1], 0),
                                            y[r][:, j, 0:W], None, compute_op=ALU.add).then_inc(added[j], 16)

            pipelined(pool, [(0, add_rows)])


def gatv2_loop(nc, m, name, table, c):
    WA = D + 1
    K = 3 * T
    with stage_of(nc, name) as (st, block):
        arrived, gathered, begun = st.sems("arrived", R), st.sems("gathered", R), st.sem("begun")
        placed, masked, mixed, summed = (st.sem(k) for k in ("placed", "masked", "mixed", "summed"))
        dotted, logits, hi_made, rest_made = (st.sem(k) for k in ("dotted", "logits", "hi_made", "rest_made"))
        mid_made, parts, turned, copied = (st.sem(k) for k in ("mid_made", "parts", "turned", "copied"))
        shown, seen, raised, dropped = (st.sem(k) for k in ("shown", "seen", "raised", "dropped"))
        top_set, shrink, exps, flipped = (st.sem(k) for k in ("top_set", "shrink", "exps", "flipped"))
        weights, group_sum, done = (st.sem(k) for k in ("weights", "group_sum", "done"))
        n_loads = 4
        zb = [m.psum[:, 2 * q:2 * q + 2, :].rearrange("p a (c f) -> p (a c) f", f=D) for q in (0, 1)]
        shown_ps, flip_ps, sum_ps, turn_ps = m.ps[4], m.ps[5], m.ps[6], m.ps[7]
        rows = m.rows[0:K, :]

        @block.sync
        def _(sp):
            def load(t, u, turn, b):
                r = u % R
                after(sp, logits, t, R)

                def col(dst, src):
                    sp.dma_start(dst, drow(src, t).rearrange("(p j) -> p j", j=T)).then_inc(arrived[r], 16)

                col(m.src_col[r][:, :], m.g_src)
                col(m.lin[r][:, :], m.g_lin[c])
                sp.dma_start(m.locrow[r][:, :], drow(m.g_locb, t).partition_broadcast(P)).then_inc(arrived[r], 16)
                sp.dma_start(m.eaT[r][:, :], m.g_eaT[bass.ds(t, 1), :, :].rearrange("a k n -> (a k) n")
                             ).then_inc(arrived[r], 16)

            pipelined(sp, [(0, load)])

        @block.gpsimd
        def _(pool):
            def gather(t, u, turn, b):
                r = u % R
                pool.wait_ge(arrived[r], 16 * n_loads * nth(u, turn, R))
                after(pool, group_sum, t, R)
                pool.sem_inc(begun, 1)
                for j in range(T):
                    pool.indirect_dma_start(m.gath[r][:, j, :], None, table,
                                            bass.IndirectOffsetOnAxis(m.src_col[r][:, j:j + 1], 0)
                                            ).then_inc(gathered[r], 16)

            pipelined(pool, [(0, gather)])

        @block.vector
        def _(dve):
            def place(t, u, turn, b):
                r = u % R
                dve.wait_ge(arrived[r], 16 * n_loads * nth(u, turn, R))
                nc.vector.tensor_scalar(m.ohT[r][:, :], m.locrow[r][:, :], m.icol[:, 0:1], None,
                                        ALU.is_equal).then_inc(placed, 1)

            def sum_inputs(t, u, turn, b):
                r, q = u % R, u % 2
                dve.wait_ge(mixed, t + 1)
                dve.wait_ge(gathered[r], 16 * T * nth(u, turn, R))
                nc.vector.tensor_tensor(m.lin[r][:, :], m.gath[r][:, :, WA], m.lin[r][:, :], ALU.add)
                nc.vector.tensor_tensor(m.zs[q][:, :, :], zb[q], m.gath[r][:, :, 0:D], ALU.add).then_inc(summed, 1)

            def dot(t, u, turn, b):
                q = u % 2
                dve.wait_ge(summed, t + 1)
                for j in range(T):
                    ins = nc.vector.scalar_tensor_tensor(m.zs[q][:, j, :], m.zs[q][:, j, :], 0.0, m.att_relu[:, :],
                                                         ALU.max, ALU.mult, accum_out=m.dots[:, j:j + 1])
                ins.then_inc(dotted, 1)

            def see(t, u, turn, b):
                dve.wait_ge(shown, t + 1)
                nc.vector.tensor_reduce(m.seen[:, 0:1], shown_ps[:, :], AX.X, ALU.max).then_inc(seen, 1)

            def add_linear(t, u, turn, b):
                r = u % R
                dve.wait_ge(dotted, t + 1)
                nc.vector.tensor_tensor(m.lg[:, 0:T], m.dots[:, :], m.lin[r][:, :], ALU.add).then_inc(logits, 1)

            hi, md, lo = (m.parts[:, 0:K].rearrange("p (c s) -> p c s", s=3)[:, :, s] for s in range(3))

            def raise_top(t, u, turn, b):
                dve.wait_ge(seen, t + 1)
                after(dve, top_set, t, 1)
                nc.vector.scalar_tensor_tensor(m.new[:, 0:1], m.seen[:, 0:1], -1.0, blk(m.top, b, 0, 1), ALU.mult,
                                               ALU.min).then_inc(raised, 1)

            def high_part(t, u, turn, b):
                dve.wait_ge(logits, t + 1)
                after(dve, turned, t, 1)
                nc.vector.tensor_copy(hi, m.lg[:, 0:T]).then_inc(hi_made, 1)

            def drop(t, u, turn, b):
                dve.wait_ge(raised, t + 1)
                after(dve, shrink, t, 1)
                nc.vector.tensor_tensor(m.drop[:, 0:1], m.new[:, 0:1], blk(m.top, b, 0, 1),
                                        ALU.subtract).then_inc(dropped, 1)

            def without_high(t, u, turn, b):
                dve.wait_ge(hi_made, t + 1)
                nc.vector.tensor_tensor(m.rest[:, 0:T], m.lg[:, 0:T], hi, ALU.subtract).then_inc(rest_made, 1)

            def set_top(t, u, turn, b):
                dve.wait_ge(dropped, t + 1)
                nc.vector.tensor_tensor(blk(m.top, b, 0, 1), blk(m.top, b, 0, 1), m.new[:, 0:1],
                                        ALU.min).then_inc(top_set, 1)

            def middle_part(t, u, turn, b):
                dve.wait_ge(rest_made, t + 1)
                nc.vector.tensor_copy(md, m.rest[:, 0:T]).then_inc(mid_made, 1)

            def add_group(t, u, turn, b):
                r = u % R
                dve.wait_ge(group_sum, t + 1)
                dve.wait_ge(shrink, t + 1)
                after(dve, done, t, 1)
                acc = blk(m.acc, b, 0, WA)
                nc.vector.scalar_tensor_tensor(acc, acc, m.less[r][:, 0:1], sum_ps[:, 0:WA], ALU.mult,
                                               ALU.add).then_inc(done, 1)

            def low_part(t, u, turn, b):
                dve.wait_ge(mid_made, t + 1)
                nc.vector.tensor_tensor(lo, m.rest[:, 0:T], md, ALU.subtract).then_inc(parts, 1)

            pipelined(dve, [(0, place), (1, sum_inputs), (1, dot), (4, add_group), (1, add_linear), (1, high_part),
                            (2, see), (1, without_high), (2, raise_top), (1, middle_part), (2, drop), (1, low_part),
                            (2, set_top)], blocks_on(nc, m, mybir.EngineType.DVE))
            dve.wait_ge(done, NG)

        @block.scalar
        def _(act):
            def copy_turned(t, u, turn, b):
                act.wait_ge(turned, t + 1)
                nc.scalar.copy(rows, turn_ps[0:K, 0:P]).then_inc(copied, 1)

            def copy_weights(t, u, turn, b):
                act.wait_ge(flipped, t + 1)
                nc.scalar.copy(m.prob[:, 0, :], flip_ps[:, :]).then_inc(weights, 1)

            def mask(t, u, turn, b):
                r = u % R
                act.wait_ge(placed, t + 1)
                nc.scalar.activation(m.off[r][:, :], m.ohT[r][:, :], ACT.Identity, scale=BIG,
                                     bias=m.minus_big[:, 0:1]).then_inc(masked, 1)

            def exponentials(t, u, turn, b):
                r = u % R
                act.wait_ge(raised, t + 1)
                nc.scalar.activation(m.expT[:, :], shown_ps[:, :], ACT.Exp, bias=m.new[:, 0:1]).then_inc(exps, 1)
                act.wait_ge(dropped, t + 1)
                nc.scalar.activation(m.less[r][:, 0:1], m.drop[:, 0:1], ACT.Exp).then_inc(shrink, 1)

            pipelined(act, [(2, copy_turned), (3, copy_weights), (0, mask), (2, exponentials)])

        @block.tensor
        def _(pe):
            def turn_parts(t, u, turn, b):
                pe.wait_ge(parts, t + 1)
                nc.tensor.matmul(turn_ps[0:K, 0:P], m.parts[:, 0:K], m.ident_bf[:, :], start=True,
                                 stop=True).then_inc(turned, 1)

            def flip(t, u, turn, b):
                pe.wait_ge(exps, t + 1)
                for j in range(T):
                    mm = nc.tensor.transpose(flip_ps[:, j * P:(j + 1) * P], m.expT[:, j * P:(j + 1) * P], m.ident[:, :])
                mm.then_inc(flipped, 1)

            def mix(t, u, turn, b):
                r, q = u % R, u % 2
                pe.wait_ge(placed, t + 1)
                after(pe, summed, t, 2)
                for j in range(T):
                    e = slice(j * P, (j + 1) * P)
                    for s in range(3):
                        nc.tensor.matmul(zb[q][:, j, :], m.ohT[r][:, e], blk(m.xr3, b, s * D, (s + 1) * D),
                                         start=(s == 0), stop=False)
                    mm = nc.tensor.matmul(zb[q][:, j, :], m.eaT[r][:, e], m.We12[c][:, :], start=False, stop=True)
                mm.then_inc(mixed, 1)

            def show_logits(t, u, turn, b):
                r = u % R
                pe.wait_ge(copied, t + 1)
                pe.wait_ge(masked, t + 1)
                nc.tensor.matmul(shown_ps[:, :], m.ident_bf[:, :], m.off[r][:, :], start=True, stop=False)
                for j in range(T):
                    mm = nc.tensor.matmul(shown_ps[:, j * P:(j + 1) * P], m.tilesel[:, j, :], rows,
                                          start=False, stop=(j == T - 1))
                mm.then_inc(shown, 1)

            def sum_group(t, u, turn, b):
                r = u % R
                pe.wait_ge(weights, t + 1)
                after(pe, done, t, 1)
                for j in range(T):
                    mm = nc.tensor.matmul(sum_ps[:, 0:WA], m.prob[:, 0, j * P:(j + 1) * P], m.gath[r][:, j, 0:WA],
                                          start=(j == 0), stop=(j == T - 1))
                mm.then_inc(group_sum, 1)

            pipelined(pe, [(2, turn_parts), (3, flip), (0, mix), (2, show_logits), (3, sum_group)],
                      blocks_on(nc, m, mybir.EngineType.PE))


def gat_loop(nc, m, name, table):
    H = HEADS
    C = T * H
    K = 3 * C
    DVE_TILES = 2
    WA = H * (DH + 1)
    with stage_of(nc, name) as (st, block):
        arrived, gathered, begun = st.sems("arrived", R), st.sems("gathered", R), st.sem("begun")
        placed, masked, mixed, summed = (st.sem(k) for k in ("placed", "masked", "mixed", "summed"))
        pairs, logits, hi_made, rest_made = (st.sem(k) for k in ("pairs", "logits", "hi_made", "rest_made"))
        mid_made, parts, turned, copied = (st.sem(k) for k in ("mid_made", "parts", "turned", "copied"))
        shown, seen, raised, dropped = (st.sem(k) for k in ("shown", "seen", "raised", "dropped"))
        top_set, shrink, exps, top_here = (st.sem(k) for k in ("top_set", "shrink", "exps", "top_here"))
        top_hi, top_rest, top_mid, top_parts = (st.sem(k) for k in ("top_hi", "top_rest", "top_mid", "top_parts"))
        here, below, depth, flipped, chosen = (st.sem(k) for k in ("here", "below", "depth", "flipped", "chosen"))
        dve_weighed, act_weighed = st.sem("dve_weighed"), st.sem("act_weighed")
        group_sum, rescaled, done = (st.sem(k) for k in ("group_sum", "rescaled", "done"))
        n_loads = 2
        sum_ps, turn_ps, flip_ps = m.ps[5], m.ps[6], m.ps[7]
        adst_ps, here_ps = m.ps[4][:, 0:K], m.ps[4][:, K:2 * K]
        rows = m.rows[0:K, :]

        def heads(ap):
            return ap.rearrange("p j (h c) -> p j h c", h=H)

        @block.sync
        def _(sp):
            def load(t, u, turn, b):
                r = u % R
                after(sp, logits, t, R)

                sp.dma_start(m.src_col[r][:, :], drow(m.g_src, t).rearrange("(p j) -> p j", j=T)).then_inc(arrived[r], 16)
                sp.dma_start(m.locrow[r][:, :], drow(m.g_locb, t).partition_broadcast(P)).then_inc(arrived[r], 16)

            pipelined(sp, [(0, load)])

        @block.gpsimd
        def _(pool):
            def gather(t, u, turn, b):
                r = u % R
                pool.wait_ge(arrived[r], 16 * n_loads * nth(u, turn, R))
                after(pool, group_sum, t, R)
                pool.sem_inc(begun, 1)
                for j in range(T):
                    pool.indirect_dma_start(m.gath[r][:, j, :], None, table,
                                            bass.IndirectOffsetOnAxis(m.src_col[r][:, j:j + 1], 0)
                                            ).then_inc(gathered[r], 16)

            pipelined(pool, [(0, gather)])

        @block.vector
        def _(dve):
            def three(ap):
                return [ap.rearrange("p (c s) -> p c s", s=3)[:, :, s] for s in range(3)]

            def place(t, u, turn, b):
                r = u % R
                dve.wait_ge(arrived[r], 16 * n_loads * nth(u, turn, R))
                nc.vector.tensor_scalar(m.ohT[r][:, :], m.locrow[r][:, :], m.icol[:, 0:1], None,
                                        ALU.is_equal).then_inc(placed, 1)

            def sum_parts(t, u, turn, b):
                dve.wait_ge(mixed, t + 1)
                nc.vector.tensor_reduce(m.e4[:, :], adst_ps.rearrange("p (c s) -> p c s", s=3), AX.X,
                                        ALU.add).then_inc(summed, 1)

            def add_src(t, u, turn, b):
                r = u % R
                dve.wait_ge(summed, t + 1)
                dve.wait_ge(gathered[r], 16 * T * nth(u, turn, R))
                e4 = m.e4[:, :].rearrange("p (j h) -> p j h", h=H)
                nc.vector.tensor_tensor(e4, e4, m.gath[r][:, :, WA:WA + H], ALU.add).then_inc(pairs, 1)

            def leak(t, u, turn, b):
                dve.wait_ge(pairs, t + 1)
                nc.vector.scalar_tensor_tensor(m.lgs[u % R][:, :], m.e4[:, :], SLOPE, m.e4[:, :], ALU.mult,
                                               ALU.max).then_inc(logits, 1)

            hi, md, lo = three(m.parts[:, 0:K])

            def high_part(t, u, turn, b):
                dve.wait_ge(logits, t + 1)
                after(dve, turned, t, 1)
                nc.vector.tensor_copy(hi, m.lgs[u % R][:, :]).then_inc(hi_made, 1)

            def without_high(t, u, turn, b):
                dve.wait_ge(hi_made, t + 1)
                nc.vector.tensor_tensor(m.rest[:, 0:C], m.lgs[u % R][:, :], hi, ALU.subtract).then_inc(rest_made, 1)

            def middle_part(t, u, turn, b):
                dve.wait_ge(rest_made, t + 1)
                nc.vector.tensor_copy(md, m.rest[:, 0:C]).then_inc(mid_made, 1)

            def low_part(t, u, turn, b):
                dve.wait_ge(mid_made, t + 1)
                nc.vector.tensor_tensor(lo, m.rest[:, 0:C], md, ALU.subtract).then_inc(parts, 1)

            def take_top(t, u, turn, b):
                dve.wait_ge(top_here, t + 1)
                nc.vector.tensor_reduce(m.here[:, :], here_ps.rearrange("p (c s) -> p c s", s=3), AX.X,
                                        ALU.add).then_inc(here, 1)

            def sink(t, u, turn, b):
                dve.wait_ge(here, t + 1)
                nc.vector.tensor_tensor(m.here[:, :], m.here[:, :], m.lgs[u % R][:, :], ALU.add).then_inc(below, 1)

            def bound(t, u, turn, b):
                dve.wait_ge(below, t + 1)
                nc.vector.tensor_scalar(m.depth[u % R][:, :], m.here[:, :], 0.0, None, ALU.min).then_inc(depth, 1)

            def weigh(t, u, turn, b):
                r = u % R
                dve.wait_ge(exps, t + 1)
                for j in range(DVE_TILES):
                    own = m.gath[r][:, j, 0:WA].rearrange("p (h c) -> p h c", h=H)
                    ins = nc.vector.tensor_tensor(own, own, last(m.ex[r][:, j * H:(j + 1) * H], DH + 1), ALU.mult)
                ins.then_inc(dve_weighed, 1)

            def see(t, u, turn, b):
                dve.wait_ge(shown, t + 1)
                nc.vector.tensor_reduce(m.seen[:, 0:H], m.psum[:, 0:H, :], AX.X, ALU.max).then_inc(seen, 1)

            def raise_top(t, u, turn, b):
                after(dve, top_set, t, 1)
                dve.wait_ge(seen, t + 1)
                nc.vector.scalar_tensor_tensor(new, m.seen[:, 0:H], -1.0, blk(m.top, b, 0, H), ALU.mult,
                                               ALU.min).then_inc(raised, 1)

            new = m.new[:, 0:H]
            new_hi, new_md, new_lo = three(m.new3[:, 0:3 * H])

            def top_high_part(t, u, turn, b):
                dve.wait_ge(raised, t + 1)
                after(dve, top_here, t, 1)
                nc.vector.tensor_copy(new_hi, new).then_inc(top_hi, 1)

            def drop(t, u, turn, b):
                after(dve, shrink, t, 1)
                nc.vector.tensor_tensor(m.drop[:, 0:H], new, blk(m.top, b, 0, H), ALU.subtract).then_inc(dropped, 1)

            def top_without_high(t, u, turn, b):
                dve.wait_ge(top_hi, t + 1)
                nc.vector.tensor_tensor(m.new_rest[:, 0:H], new, new_hi, ALU.subtract).then_inc(top_rest, 1)

            def set_top(t, u, turn, b):
                dve.wait_ge(dropped, t + 1)
                nc.vector.tensor_tensor(blk(m.top, b, 0, H), blk(m.top, b, 0, H), new, ALU.min).then_inc(top_set, 1)

            def top_middle_part(t, u, turn, b):
                dve.wait_ge(top_rest, t + 1)
                nc.vector.tensor_copy(new_md, m.new_rest[:, 0:H]).then_inc(top_mid, 1)

            def top_low_part(t, u, turn, b):
                dve.wait_ge(top_mid, t + 1)
                nc.vector.tensor_tensor(new_lo, m.new_rest[:, 0:H], new_md, ALU.subtract).then_inc(top_parts, 1)

            def rescale(t, u, turn, b):
                acc = blk(m.acc, b, 0, WA).rearrange("p (h c) -> p h c", h=H)
                dve.wait_ge(shrink, t + 1)
                after(dve, done, t, 1)
                nc.vector.tensor_tensor(acc, acc, last(m.less[u % R][:, 0:H], DH + 1), ALU.mult).then_inc(rescaled, 1)

            def add_group(t, u, turn, b):
                acc = blk(m.acc, b, 0, WA)
                dve.wait_ge(group_sum, t + 1)
                dve.wait_ge(rescaled, t + 1)
                nc.vector.tensor_tensor(acc, acc, sum_ps[:, 0:WA], ALU.add).then_inc(done, 1)

            pipelined(dve, [(2, see), (1, sum_parts), (2, raise_top), (3, take_top), (1, add_src), (2, top_high_part),
                            (3, sink), (1, leak), (2, drop), (3, bound), (1, high_part), (2, top_without_high),
                            (2, set_top), (1, without_high), (2, top_middle_part), (1, middle_part),
                            (2, top_low_part), (1, low_part), (0, place), (4, rescale), (3, weigh), (4, add_group)],
                      blocks_on(nc, m, mybir.EngineType.DVE))
            dve.wait_ge(done, NG)

        @block.scalar
        def _(act):
            def copy_turned(t, u, turn, b):
                act.wait_ge(turned, t + 1)
                nc.scalar.copy(rows, turn_ps[0:K, 0:P]).then_inc(copied, 1)

            def exponentials(t, u, turn, b):
                r = u % R
                act.wait_ge(depth, t + 1)
                nc.scalar.activation(m.ex[r][:, :], m.depth[r][:, :], ACT.Exp).then_inc(exps, 1)

            def weigh_tile(r, j):
                for h in range(H):
                    part = m.gath[r][:, j, h * (DH + 1):(h + 1) * (DH + 1)]
                    ins = nc.scalar.mul(part, part, m.ex[r][:, j * H + h:j * H + h + 1])
                return ins

            def weigh_early(t, u, turn, b):
                act.wait_ge(exps, t + 1)
                for j in range(DVE_TILES, T - 1):
                    weigh_tile(u % R, j)

            def weigh_late(t, u, turn, b):
                weigh_tile(u % R, T - 1).then_inc(act_weighed, 1)

            def mask(t, u, turn, b):
                r = u % R
                act.wait_ge(placed, t + 1)
                nc.scalar.activation(m.off[r][:, :], m.ohT[r][:, :], ACT.Identity, scale=BIG,
                                     bias=m.minus_big[:, 0:1]).then_inc(masked, 1)

            def choose(t, u, turn, b):
                act.wait_ge(flipped, t + 1)
                after(act, group_sum, t, 2)
                nc.scalar.copy(m.prob[:, u % 2, :], flip_ps[:, :]).then_inc(chosen, 1)

            def shrinkage(t, u, turn, b):
                r = u % R
                act.wait_ge(dropped, t + 1)
                nc.scalar.activation(m.less[r][:, 0:H], m.drop[:, 0:H], ACT.Exp).then_inc(shrink, 1)

            pipelined(act, [(2, copy_turned), (4, weigh_late), (1, mask), (3, choose), (3, exponentials), (2, shrinkage),
                            (3, weigh_early)])

        @block.tensor
        def _(pe):
            def bring_top(t, u, turn, b):
                r = u % R
                pe.wait_ge(top_parts, t + 1)
                after(pe, here, t, 1)
                for j in range(T):
                    mm = nc.tensor.matmul(here_ps[:, j * 3 * H:(j + 1) * 3 * H], m.ohT[r][:, j * P:(j + 1) * P],
                                          m.new3[:, 0:3 * H], start=True, stop=True)
                mm.then_inc(top_here, 1)

            def turn_parts(t, u, turn, b):
                pe.wait_ge(parts, t + 1)
                nc.tensor.matmul(turn_ps[0:K, 0:P], m.parts[:, 0:K], m.ident_bf[:, :], start=True,
                                 stop=True).then_inc(turned, 1)

            def show_mask(t, u, turn, b):
                r = u % R
                pe.wait_ge(masked, t + 1)
                after(pe, seen, t, 1)
                for h in range(H):
                    nc.tensor.matmul(m.ps[h][:, :], m.ident_bf[:, :], m.off[r][:, :], start=True, stop=False)

            def show_logits(t, u, turn, b):
                pe.wait_ge(copied, t + 1)
                for h in range(H):
                    for j in range(T):
                        mm = nc.tensor.matmul(m.ps[h][:, j * P:(j + 1) * P], m.edgesel[:, j * H + h, :], rows,
                                              start=False, stop=(j == T - 1))
                mm.then_inc(shown, 1)

            def flip(t, u, turn, b):
                r = u % R
                after(pe, chosen, t, 1)
                for j in range(T):
                    mm = nc.tensor.matmul(flip_ps[:, j * P:(j + 1) * P], m.ohT[r][:, j * P:(j + 1) * P],
                                          m.ident_bf[:, :], start=True, stop=True)
                mm.then_inc(flipped, 1)

            def sum_group(t, u, turn, b):
                r = u % R
                pe.wait_ge(chosen, t + 1)
                pe.wait_ge(dve_weighed, t + 1)
                pe.wait_ge(act_weighed, t + 1)
                after(pe, done, t, 1)
                for j in range(T):
                    mm = nc.tensor.matmul(sum_ps[:, 0:WA], m.prob[:, u % 2, j * P:(j + 1) * P], m.gath[r][:, j, 0:WA],
                                          start=(j == 0), stop=(j == T - 1))
                mm.then_inc(group_sum, 1)

            def mix(t, u, turn, b):
                r = u % R
                pe.wait_ge(placed, t + 1)
                after(pe, summed, t, 1)
                for j in range(T):
                    mm = nc.tensor.matmul(adst_ps[:, j * 3 * H:(j + 1) * 3 * H], m.ohT[r][:, j * P:(j + 1) * P],
                                          blk(m.adst3, b, 0, 3 * H), start=True, stop=True)
                mm.then_inc(mixed, 1)

            pipelined(pe, [(2, show_mask), (2, turn_parts), (2, show_logits), (3, bring_top), (1, mix), (3, flip), (4, sum_group)],
                      blocks_on(nc, m, mybir.EngineType.PE))


def add_sums(nc, m, name):
    with stage_of(nc, name) as (st, block):
        arrived, summed, used, step = st.sems("arrived", R), st.sem("summed"), st.sem("used"), st.sem("step")

        @block.sync
        def _(sp):
            for b in range(NB):
                if b >= R:
                    sp.wait_ge(summed, b - R + 1)
                for j in range(T):
                    sp.dma_start(m.gath[b % R][:, j, 0:D + 1], m.sum0[j][b * P:(b + 1) * P, :]).then_inc(arrived[b % R], 16)

        @block.vector
        def _(dve):
            for b in range(NB):
                dve.wait_ge(arrived[b % R], 16 * T * (b // R + 1))
                if b >= 2:
                    dve.wait_ge(used, 2 * (b - 1))
                nc.vector.tensor_reduce(m.prob2[b % 2][:, 0:D + 1],
                                        m.gath[b % R][:, :, 0:D + 1].rearrange("p j c -> p c j"), AX.X,
                                        ALU.add).then_inc(summed, 1)
                dve.wait_ge(summed, b + 1)
                nc.vector.tensor_tensor(m.x[:, b, :], m.x[:, b, :], m.prob2[b % 2][:, 0:D], ALU.add).then_inc(used, 1)
                nc.vector.tensor_copy(m.deg[:, b:b + 1], m.prob2[b % 2][:, D:D + 1]).then_inc(used, 1)
            nc.vector.tensor_scalar(m.cnt[:, :], m.attr[:, 0:NB, 2], 1.0, None, ALU.max).then_inc(step, 1)
            dve.wait_ge(step, 1)
            nc.vector.reciprocal(m.cnt[:, :], m.cnt[:, :]).then_inc(step, 1)
            dve.wait_ge(step, 2)
            nc.vector.tensor_tensor(m.attr[:, 0:NB, 0:2], m.attr[:, 0:NB, 0:2], last(m.cnt[:, :], 2),
                                    ALU.mult).then_inc(step, 1)


def gatv2_nodes(nc, m, a, name, c, table):
    att = m.bc[f"L1_gnn_att{c}"]
    with stage_of(nc, name) as (st, block):
        loaded, taken, filled, written = st.sem("loaded"), st.sem("taken"), st.sem("filled"), st.sem("written")
        turned, moved, product = st.sem("turned"), st.sem("moved"), st.sem("product")
        mixed, rest_made, mid_made, parts, rows_done = (
            st.sem(k) for k in ("mixed", "rest_made", "mid_made", "parts", "rows_done"))
        step = st.sem("step")

        @block.sync
        def _(sp):
            for q, k in enumerate((f"L1_gnn_Wl{c}", f"L1_gnn_Wr{c}")):
                sp.dma_start(m.w[:, :, q * D:(q + 1) * D], a[k].rearrange("(c p) n -> p c n", p=P)).then_inc(loaded, 16)
            sp.wait_ge(rows_done, NB)
            sp.wait_ge(filled, 4)
            sp.dma_start(table.rearrange("(b p) c -> p b c", p=P), m.acc[:, 0:NB, :]).then_inc(written, 16)
            sp.wait_ge(written, 16)

        @block.tensor
        def _(pe):
            product_by_blocks(nc, m, pe, 2 * D, loaded, 2, turned, moved, product, taken)

        @block.scalar
        def _(act):
            def move(b):
                act.wait_ge(turned, b + 1)
                if b >= 2:
                    act.wait_ge(product, b - 1)
                nc.scalar.copy(m.hT[b % 2][:, :], m.ps[b % 2][:, 0:D]).then_inc(moved, 1)

            move(0)
            act.wait_ge(filled, 4)
            for b in range(NB):
                if b + 1 < NB:
                    move(b + 1)
                act.wait_ge(product, b + 1)
                out = m.ps[4 + b % 4]
                nc.scalar.copy(m.acc[:, b, 0:D], out[:, 0:D])
                nc.scalar.copy(m.h[:, b, :], out[:, D:2 * D])
                nc.scalar.copy(m.xr3[:, b, 0:D], out[:, D:2 * D]).then_inc(taken, 1)

        @block.vector
        def _(dve):
            nc.vector.memset(m.acc[:, 0:NB, D:TW], 1.0).then_inc(filled, 1)
            nc.vector.memset(m.acc[:, NB, :], 0.0).then_inc(filled, 1)
            nc.vector.memset(m.xr3[:, NB, :], 0.0).then_inc(filled, 1)
            nc.vector.tensor_scalar(m.att_relu[:, :], att[:, :], 1.0 - SLOPE, None, ALU.mult).then_inc(filled, 1)
            dve.wait_ge(filled, 4)
            for b in range(NB):
                dve.wait_ge(taken, b + 1)
                z, xr = m.prob2[b % 2][:, 0:D], m.h[:, b, :]
                hi, md, lo = (m.xr3[:, b, s * D:(s + 1) * D] for s in range(3))
                if b >= 2:
                    dve.wait_ge(mixed, 4 * (b - 1))
                nc.vector.tensor_tensor(z, m.acc[:, b, 0:D], xr, ALU.add).then_inc(mixed, 1)
                nc.vector.scalar_tensor_tensor(m.junk[:, :], m.acc[:, b, 0:D], SLOPE, att[:, :], ALU.mult, ALU.mult,
                                               accum_out=m.acc[:, b, D + 1:D + 2]).then_inc(rows_done, 1)
                dve.wait_ge(mixed, 4 * b + 1)
                nc.vector.tensor_tensor(xr, xr, hi, ALU.subtract).then_inc(rest_made, 1)
                for r in (0, 1):
                    dve.wait_ge(mixed, 4 * b + 1 + r)
                    nc.vector.scalar_tensor_tensor(z, m.We_bc[f"L1_gnn_We{c}"][:, r, :], m.attr[:, b, r:r + 1], z,
                                                   ALU.mult, ALU.add).then_inc(mixed, 1)
                    if r == 0:
                        dve.wait_ge(rest_made, b + 1)
                        nc.vector.tensor_copy(md, xr).then_inc(mid_made, 1)
                dve.wait_ge(mid_made, b + 1)
                nc.vector.tensor_tensor(lo, xr, md, ALU.subtract).then_inc(parts, 1)
                dve.wait_ge(mixed, 4 * b + 3)
                nc.vector.scalar_tensor_tensor(z, z, 0.0, m.att_relu[:, :], ALU.max, ALU.mult,
                                               accum_out=m.self_dot[:, b:b + 1]).then_inc(mixed, 1)
                dve.wait_ge(rows_done, b + 1)
            lg = m.self_dot[:, :]
            dve.wait_ge(mixed, 4 * NB)
            nc.vector.tensor_tensor(lg, lg, m.acc[:, 0:NB, D + 1], ALU.add).then_inc(step, 1)
            for r in (0, 1):
                dve.wait_ge(step, r + 1)
                nc.vector.scalar_tensor_tensor(lg, m.attr[:, 0:NB, r], m.ea_lin[c][:, r:r + 1], lg, ALU.mult,
                                               ALU.add).then_inc(step, 1)
            dve.wait_ge(step, 3)
            nc.vector.tensor_scalar(m.top[:, 0:NB, 0], lg, -1.0, None, ALU.mult).then_inc(step, 1)


def product_by_blocks(nc, m, pe, n_out, loaded, n_loads, turned, moved, product, taken):
    def turn(b):
        if b >= 2:
            pe.wait_ge(moved, b - 1)
        for c in (0, 1):
            mm = nc.tensor.transpose(m.ps[b % 2][:, c * P:(c + 1) * P], m.h[:, b, c * P:(c + 1) * P], m.ident[:, :])
        mm.then_inc(turned, 1)

    pe.wait_ge(loaded, 16 * n_loads)
    turn(0)
    for b in range(NB):
        if b + 1 < NB:
            turn(b + 1)
        pe.wait_ge(moved, b + 1)
        if b >= 4:
            pe.wait_ge(taken, b - 3)
        for c in (0, 1):
            mm = nc.tensor.matmul(m.ps[4 + b % 4][:, 0:n_out], m.hT[b % 2][:, c * P:(c + 1) * P],
                                  m.w[:, c, 0:n_out], start=(c == 0), stop=(c == 1))
        mm.then_inc(product, 1)


def move_transposed(nc, m, act, turned, moved, product):
    for b in range(NB):
        act.wait_ge(turned, b + 1)
        if b >= 2:
            act.wait_ge(product, b - 1)
        nc.scalar.copy(m.hT[b % 2][:, :], m.ps[b % 2][:, 0:D]).then_inc(moved, 1)


def batch_norm(nc, m, name, c, residual):
    with stage_of(nc, name) as (st, block):
        step, means, centred, squared, variances, root, scaled = (
            st.sem(k) for k in ("step", "means", "centred", "squared", "variances", "root", "scaled"))
        biased, shifted, folded, lifted, normed, clipped = (
            st.sem(k) for k in ("biased", "shifted", "folded", "lifted", "normed", "clipped"))
        sq = [m.prob2[q][:, 0:D] for q in (0, 1)]
        mean_ps, var_ps = m.ps[0], m.ps[1]

        @block.tensor
        def _(pe):
            for b in range(NB):
                pe.wait_ge(biased, b + 1)
                mm = nc.tensor.matmul(mean_ps[:, 0:D], m.mean_w[:, b // (NB - 1), :], m.h[:, b, :],
                                      start=(b == 0), stop=(b == NB - 1))
            mm.then_inc(means, 1)
            for b in range(NB):
                pe.wait_ge(squared, b + 1)
                mm = nc.tensor.matmul(var_ps[:, 0:D], m.mean_w[:, b // (NB - 1), :], sq[b % 2],
                                      start=(b == 0), stop=(b == NB - 1))
                if b < NB - 1:
                    mm.then_inc(variances, 1)
            mm.then_inc(variances, 1)

        @block.scalar
        def _(act):
            for b in range(NB):
                act.wait_ge(centred, b + 1)
                if b >= 2:
                    act.wait_ge(variances, b - 1)
                nc.scalar.activation(sq[b % 2], m.h[:, b, :], ACT.Square).then_inc(squared, 1)
            act.wait_ge(step, 3)
            nc.scalar.activation(m.gain[:, :], m.gain[:, :], ACT.Sqrt).then_inc(root, 1)

        @block.vector
        def _(dve):
            nc.vector.reciprocal(m.cnt[:, :], m.acc[:, 0:NB, D]).then_inc(step, 1)
            dve.wait_ge(step, 1)
            for b in range(NB):
                nc.vector.scalar_tensor_tensor(m.h[:, b, :], m.acc[:, b, 0:D], m.cnt[:, b:b + 1],
                                               m.bc[f"L1_gnn_b{c}"][:, :], ALU.mult, ALU.add).then_inc(biased, 1)
            dve.wait_ge(means, 1)
            nc.vector.tensor_copy(m.mean[:, :], mean_ps[:, 0:D]).then_inc(step, 1)
            dve.wait_ge(step, 2)
            dve.wait_ge(biased, NB)
            for b in range(NB):
                nc.vector.tensor_tensor(m.h[:, b, :], m.h[:, b, :], m.mean[:, :], ALU.subtract).then_inc(centred, 1)
            dve.wait_ge(variances, NB)
            nc.vector.tensor_scalar(m.gain[:, :], var_ps[:, 0:D], EPS, None, ALU.add).then_inc(step, 1)
            dve.wait_ge(root, 1)
            nc.vector.reciprocal(m.gain[:, :], m.gain[:, :]).then_inc(step, 1)
            dve.wait_ge(step, 4)
            nc.vector.tensor_tensor(m.gain[:, :], m.gain[:, :], m.bc[f"L1_gnn_g{c}"][:, :], ALU.mult).then_inc(step, 1)
            dve.wait_ge(step, 5)
            dve.wait_ge(squared, NB)
            for b in range(NB):
                nc.vector.tensor_tensor(m.h[:, b, :], m.h[:, b, :], m.gain[:, :], ALU.mult).then_inc(scaled, 1)
            for b in range(NB):
                dve.wait_ge(scaled, b + 1)
                nc.vector.tensor_tensor(m.h[:, b, :], m.h[:, b, :], m.bc[f"L1_gnn_beta{c}"][:, :],
                                        ALU.add).then_inc(shifted, 1)
            if residual:
                for b in range(NB):
                    nc.vector.tensor_scalar(m.acc[:, b, 0:D], m.x[:, b, :], m.mv[:, b, 0:1], m.rstd[:, b:b + 1],
                                            ALU.subtract, ALU.mult).then_inc(normed, 1)
                for b in range(NB):
                    dve.wait_ge(normed, b + 1)
                    dve.wait_ge(shifted, b + 1)
                    nc.vector.scalar_tensor_tensor(m.h[:, b, :], m.acc[:, b, 0:D], 0.0, m.h[:, b, :], ALU.max,
                                                   ALU.add).then_inc(lifted, 1)
            slope = m.bc[f"L1_gnn_a{c}"][:, 0:1]
            for b in range(NB):
                dve.wait_ge(lifted if residual else shifted, b + 1)
                nc.vector.tensor_scalar(m.acc[:, b, 0:D], m.h[:, b, :], 0.0, slope, ALU.min, ALU.mult).then_inc(clipped, 1)
            for b in range(NB):
                dve.wait_ge(clipped, b + 1)
                nc.vector.scalar_tensor_tensor(m.h[:, b, :], m.h[:, b, :], 0.0, m.acc[:, b, 0:D], ALU.max,
                                               ALU.add).then_inc(folded, 1)
            if residual:
                for b in range(NB):
                    dve.wait_ge(folded, b + 1)
                    nc.vector.tensor_tensor(m.x[:, b, :], m.x[:, b, :], m.h[:, b, :], ALU.add).then_inc(step, 1)


def gat_nodes(nc, m, a, name, table):
    WA = HEADS * (DH + 1)
    with stage_of(nc, name) as (st, block):
        loaded, taken, filled, written = st.sem("loaded"), st.sem("taken"), st.sem("filled"), st.sem("written")
        turned, moved, product = st.sem("turned"), st.sem("moved"), st.sem("product")
        by_src, by_dst, cleared, parts = st.sem("by_src"), st.sem("by_dst"), st.sem("cleared"), st.sem("parts")

        @block.sync
        def _(sp):
            sp.dma_start(m.w[:, :, 0:D], a["L2_gnn_W"].rearrange("(c p) n -> p c n", p=P)).then_inc(loaded, 16)
            sp.wait_ge(by_src, 2 * NB)
            sp.wait_ge(taken, NB)
            sp.wait_ge(filled, 2)
            sp.dma_start(table.rearrange("(b p) c -> p b c", p=P), m.acc[:, 0:NB, :]).then_inc(written, 16)
            sp.wait_ge(written, 16)

        @block.tensor
        def _(pe):
            product_by_blocks(nc, m, pe, D, loaded, 1, turned, moved, product, taken)

        @block.scalar
        def _(act):
            move_transposed(nc, m, act, turned, moved, product)

        @block.vector
        def _(dve):
            heads = m.acc[:, 0:NB, 0:WA].rearrange("p b (h c) -> p b h c", h=HEADS)
            nc.vector.memset(heads[:, :, :, DH], 1.0).then_inc(filled, 1)
            nc.vector.memset(m.top[:, :, :], BIG).then_inc(filled, 1)
            for b in range(NB):
                dve.wait_ge(product, b + 1)
                row = heads[:, b, :, 0:DH]
                nc.vector.tensor_copy(row, m.ps[4 + b % 4][:, 0:D].rearrange("p (h c) -> p h c", h=HEADS)
                                      ).then_inc(taken, 1)
                dve.wait_ge(taken, b + 1)
                for k, out, sem in (("src", m.acc[:, b, WA:WA + HEADS], by_src), ("dst", m.adst[:, b, :], by_dst)):
                    t = m.prob2[0 if k == "src" else 1][:, 0:D].rearrange("p (h c) -> p h c", h=HEADS)
                    nc.vector.tensor_tensor(t, row, m.bc[f"L2_gnn_att_{k}"][:, :].rearrange("p (h c) -> p h c", h=HEADS),
                                            ALU.mult).then_inc(sem, 1)
                    dve.wait_ge(sem, 2 * b + 1)
                    nc.vector.tensor_reduce(out, t, AX.X, ALU.add).then_inc(sem, 1)
                    dve.wait_ge(sem, 2 * b + 2)
            hi, md, lo = (m.adst3[:, 0:NB, :].rearrange("p b (h s) -> p b h s", s=3)[:, :, :, s] for s in range(3))
            nums = m.adst[:, 0:NB, :]
            nc.vector.tensor_copy(hi, nums).then_inc(parts, 1)
            dve.wait_ge(parts, 1)
            nc.vector.tensor_tensor(nums, nums, hi, ALU.subtract).then_inc(parts, 1)
            dve.wait_ge(parts, 2)
            nc.vector.tensor_copy(md, nums).then_inc(parts, 1)
            dve.wait_ge(parts, 3)
            nc.vector.tensor_tensor(lo, nums, md, ALU.subtract).then_inc(parts, 1)
            dve.wait_ge(written, 16)
            nc.vector.memset(m.acc[:, :, :], 0.0).then_inc(cleared, 1)


def gat_out(nc, m, name):
    WA = HEADS * (DH + 1)
    with stage_of(nc, name) as (st, block):
        step, biased, divided, opened, added = (st.sem(k) for k in ("step", "biased", "divided", "opened", "added"))
        heads = m.acc[:, 0:NB, 0:WA].rearrange("p b (h c) -> p b h c", h=HEADS)

        @block.vector
        def _(dve):
            s = m.share[:, :, :]
            nc.vector.tensor_scalar(s, heads[:, :, :, DH], 0.0, None, ALU.is_equal).then_inc(step, 1)
            dve.wait_ge(step, 1)
            nc.vector.tensor_tensor(s, s, heads[:, :, :, DH], ALU.add).then_inc(step, 1)
            dve.wait_ge(step, 2)
            nc.vector.reciprocal(s, s).then_inc(step, 1)
            dve.wait_ge(step, 3)
            for b in range(NB):
                nc.vector.tensor_tensor(m.h[:, b, :].rearrange("p (h c) -> p h c", h=HEADS), heads[:, b, :, 0:DH],
                                        last(m.share[:, b, :], DH), ALU.mult).then_inc(divided, 1)
            for b in range(NB):
                dve.wait_ge(divided, b + 1)
                nc.vector.tensor_tensor(m.h[:, b, :], m.h[:, b, :], m.bc["L2_gnn_bias"][:, :], ALU.add).then_inc(biased, 1)
            for b in range(NB):
                dve.wait_ge(opened, b + 1)
                nc.vector.tensor_tensor(m.x[:, b, :], m.x[:, b, :], m.h[:, b, :], ALU.add).then_inc(added, 1)

        @block.scalar
        def _(act):
            for b in range(NB):
                act.wait_ge(biased, b + 1)
                nc.scalar.activation(m.h[:, b, :], m.h[:, b, :], ACT.Sigmoid).then_inc(opened, 1)


def gcn_nodes(nc, m, name):
    with stage_of(nc, name) as (st, block):
        step, root = st.sem("step"), st.sem("root")

        @block.scalar
        def _(act):
            act.wait_ge(step, 2)
            nc.scalar.activation(m.dinv[:, :], m.dinv[:, :], ACT.Sqrt).then_inc(root, 1)

        @block.vector
        def _(dve):
            nc.vector.tensor_scalar(m.dinv[:, :], m.deg[:, :], 1.0e-20, None, ALU.max).then_inc(step, 1)
            dve.wait_ge(step, 1)
            nc.vector.reciprocal(m.dinv[:, :], m.dinv[:, :]).then_inc(step, 1)
            dve.wait_ge(root, 1)
            for b in range(NB):
                nc.vector.tensor_scalar(m.h[:, b, :], m.h[:, b, :], m.dinv[:, b:b + 1], None, ALU.mult).then_inc(step, 1)


def gcn_out(nc, m, a, name, out):
    with stage_of(nc, name) as (st, block):
        arrived, summed, owned, ready = st.sems("arrived", R), st.sem("summed"), st.sem("owned"), st.sem("ready")
        loaded, taken, added, stored = st.sem("loaded"), st.sem("taken"), st.sem("added"), st.sem("stored")
        turned, moved, product = st.sem("turned"), st.sem("moved"), st.sem("product")

        @block.sync
        def _(sp):
            sp.dma_start(m.w[:, :, 0:D], a["L3_gnn_WT"].rearrange("(c p) n -> p c n", p=P)).then_inc(loaded, 16)
            for b in range(NB):
                if b >= R:
                    sp.wait_ge(summed, b - R + 1)
                for j in range(T):
                    sp.dma_start(m.gath[b % R][:, j, 0:D], m.sum3[j][b * P:(b + 1) * P, :]).then_inc(arrived[b % R], 16)
            for b in range(NB):
                sp.wait_ge(added, b + 1)
                sp.dma_start(out[b * P:(b + 1) * P, :], m.x[:, b, :]).then_inc(stored, 16)
            sp.wait_ge(stored, 16 * NB)

        @block.tensor
        def _(pe):
            pe.wait_ge(ready, NB)
            product_by_blocks(nc, m, pe, D, loaded, 1, turned, moved, product, taken)

        @block.scalar
        def _(act):
            move_transposed(nc, m, act, turned, moved, product)

        @block.vector
        def _(dve):
            for b in range(NB):
                dve.wait_ge(arrived[b % R], 16 * T * (b // R + 1))
                if b >= 2:
                    dve.wait_ge(owned, b - 1)
                t = m.prob2[b % 2][:, 0:D]
                nc.vector.tensor_reduce(t, m.gath[b % R][:, :, 0:D].rearrange("p j c -> p c j"), AX.X,
                                        ALU.add).then_inc(summed, 1)
                dve.wait_ge(summed, b + 1)
                nc.vector.tensor_tensor(m.h[:, b, :], m.h[:, b, :], t, ALU.add).then_inc(owned, 1)
                dve.wait_ge(owned, b + 1)
                nc.vector.tensor_scalar(m.h[:, b, :], m.h[:, b, :], m.dinv[:, b:b + 1], None, ALU.mult).then_inc(ready, 1)
            for b in range(NB):
                dve.wait_ge(product, b + 1)
                t = m.prob2[b % 2][:, 0:D]
                if b >= 2:
                    dve.wait_ge(added, b - 1)
                nc.vector.tensor_tensor(t, m.ps[4 + b % 4][:, 0:D], m.bc["L3_gnn_b"][:, :], ALU.add).then_inc(taken, 1)
                dve.wait_ge(taken, b + 1)
                nc.vector.scalar_tensor_tensor(m.x[:, b, :], t, 0.0, m.x[:, b, :], ALU.max, ALU.add).then_inc(added, 1)


ROWS = ["L1_gnn_att1", "L1_gnn_b1", "L1_gnn_g1", "L1_gnn_beta1", "L1_gnn_a1", "L1_gnn_att2", "L1_gnn_b2",
        "L1_gnn_g2", "L1_gnn_beta2", "L1_gnn_a2", "L2_gnn_att_src", "L2_gnn_att_dst", "L2_gnn_bias", "L3_gnn_b"]


def build(nc, a, out):
    m = Memory()
    with ExitStack() as ctx:
        def sb(name, *shape, dt=F32):
            return ctx.enter_context(nc.sbuf_tensor(name, list(shape), dt))

        def ring(name, n, *shape, dt=F32):
            return [sb(f"{name}{r}", *shape, dt=dt) for r in range(n)]

        def dram(name, *shape, dt=F32):
            return nc.dram_tensor(name, shape, dt, kind="Internal").ap()

        m.x, m.h = sb("x", P, NB, D), sb("h", P, NB + 1, D)
        m.xr3, m.acc = sb("xr3", P, NB + 1, 3 * D, dt=BF16), sb("acc", P, NB + 1, TW)
        m.top, m.adst, m.attr = (sb(k, P, NB + 1, 4) for k in ("top", "adst", "attr"))
        m.adst3 = sb("adst3", P, NB + 1, 3 * HEADS, dt=BF16)
        m.deg, m.dinv, m.rstd, m.cnt, m.self_dot = (sb(k, P, NB) for k in ("deg", "dinv", "rstd", "cnt", "self_dot"))
        m.mv, m.st6, m.share = sb("mv", P, NB, 2), sb("st6", P, NB, 6), sb("share", P, NB, HEADS)
        m.ident, m.ident_bf, m.later = sb("ident", P, P), sb("ident_bf", P, P, dt=BF16), sb("later", P, P, dt=BF16)
        m.one_bf, m.minus_big = sb("one_bf", P, 1, dt=BF16), sb("minus_big", P, 1)
        m.icol, m.irow, m.dumprow, m.real = sb("icol", P, 1), sb("irow", P, P), sb("dumprow", P, 1), sb("real", P, 1)
        m.mean_w = sb("mean_w", P, 2, P)
        m.of_tile, m.of_edge = sb("of_tile", 3 * T, T), sb("of_edge", 3 * T * HEADS, T * HEADS)
        m.tilesel = sb("tilesel", 3 * T, T, P, dt=BF16)
        m.edgesel = sb("edgesel", 3 * T * HEADS, T * HEADS, P, dt=BF16)
        m.bc = {k: sb(f"{k}_rows", P, a[k].shape[0]) for k in ROWS}
        m.We12 = {c: sb(f"We12_{c}", KE, D, dt=BF16) for c in (1, 2)}
        m.ea_lin = {c: sb(f"ea_lin{c}", P, 2) for c in (1, 2)}
        m.We_bc = {f"L1_gnn_We{c}": sb(f"We{c}_rows", P, 2, D) for c in (1, 2)}
        m.mean, m.gain = sb("mean", P, D), sb("gain", P, D)
        m.att_relu, m.junk = m.mean, m.gain
        m.later32 = m.junk[:, 0:P]
        m.tab = sb("tab", 1, NG, dt=I32)
        m.src_col, m.to_row = ring("src_col", R, P, T, dt=I32), ring("to_row", R, P, T, dt=I32)
        m.loc, m.ew, m.inb = ring("loc", R, P, T), ring("ew", R, P, T), ring("inb", R, P, T, dt=BF16)
        m.ea, m.eaT = ring("ea", R, P, 2, T), ring("eaT", R, KE, WIN, dt=BF16)
        m.lin, m.away = ring("lin", R, P, T), ring("away", R, P, T)
        m.locrow, m.ohT, m.off = (ring(k, R, P, WIN, dt=BF16) for k in ("locrow", "ohT", "off"))
        m.gath, m.zs, m.prob = ring("gath", R, P, T, TW), ring("zs", 2, P, T, D), sb("prob", P, 2, WIN)
        m.expT, m.rows = m.prob[:, 1, :], sb("rows", 3 * T * HEADS, P, dt=BF16)
        m.parts, m.new3 = sb("parts", P, 3 * T * HEADS, dt=BF16), sb("new3", P, 3 * HEADS, dt=BF16)
        m.lgs, m.depth, m.ex = (ring(k, R, P, T * HEADS) for k in ("lgs", "depth", "ex"))
        m.lg, m.dots, m.e4, m.rest, m.here = (sb(k, P, n) for k, n in (
            ("lg", T), ("dots", T), ("e4", T * HEADS), ("rest", T * HEADS), ("here", T * HEADS)))
        m.less = ring("less", R, P, HEADS)
        m.seen, m.new, m.drop, m.new_rest = (sb(k, P, HEADS) for k in ("seen", "new", "drop", "new_rest"))
        m.attr_sum = sb("attr_sum", P, 3)
        m.w, m.hT = m.prob, [m.zs[1][:, q, :] for q in (0, 1)]
        m.prob2 = ring("sums", 2, P, TW)
        ls = m.zs[0][:, :, :].rearrange("p j c -> p (j c)")
        room = m.xr3[:, :, :].rearrange("p b c -> p (b c)").bitcast(F32)
        m.list = {"ends": sb("ends", WH, 4, dt=I32), "ends_f": sb("ends_f", WH, 4),
                  "spread": room[0:WH, 3 * WIN:4 * WIN].rearrange("p (q c) -> p q c", q=4),
                  "fl": ls[:, 0:2 * NW], "cnt": ls[:, 2 * NW:3 * NW], "off": ls[:, 3 * NW:4 * NW],
                  "one": ls[:, 4 * NW:5 * NW]}
        for k in ("gid", "w", "o", "b", "base"):
            m.list[k] = sb(f"list_{k}", P, 2)
        for k in ("w_int", "b_int"):
            m.list[k] = sb(f"list_{k}", P, 2, dt=I32)
        m.list["loc"] = room[:, 0:2 * WIN].rearrange("p (h n) -> p h n", h=2)
        m.list["locb"] = room[:, 2 * WIN:3 * WIN].bitcast(BF16).rearrange("p (h n) -> p h n", h=2)
        m.psum = ctx.enter_context(nc.psum_tensor("psum", [P, 8, WIN], F32))
        m.ps = [m.psum[:, q, :] for q in range(8)]
        m.g_src, m.g_loc, m.g_ew = dram("g_src", NG, WIN, dt=I32), dram("g_loc", NG, WIN), dram("g_ew", NG, WIN)
        m.g_locb, m.g_ea = dram("g_locb", NG, WIN, dt=BF16), [dram(f"g_ea{c}", NG, WIN) for c in (0, 1)]
        m.g_eaT, m.g_lin = dram("g_eaT", NG, KE, WIN, dt=BF16), {c: dram(f"g_lin{c}", NG, WIN) for c in (1, 2)}
        m.block_of = dram("block_of", 2 * P, dt=I32)
        tables = [dram(f"table{q}", NP, TW) for q in range(3)]
        m.sum0 = [dram(f"sum0_{j}", NP + P, D + 1) for j in range(T)]
        m.sum3 = [dram(f"sum3_{j}", NP + P, D) for j in range(T)]

        constants(nc, m, a)
        group_list(nc, m, a)
        layer_norm(nc, m, "ln0")
        scatter_loop(nc, m, "spmm", m.sum0, True)
        add_sums(nc, m, "spmm_out")
        layer_norm(nc, m, "ln1")
        for c in (1, 2):
            gatv2_nodes(nc, m, a, f"gatv2_{c}", c, tables[c - 1])
            gatv2_loop(nc, m, f"edges{c}", tables[c - 1], c)
            batch_norm(nc, m, f"bn{c}", c, residual=(c == 2))
        layer_norm(nc, m, "ln2")
        gat_nodes(nc, m, a, "gat", tables[2])
        gat_loop(nc, m, "gat_edges", tables[2])
        gat_out(nc, m, "gat_out")
        layer_norm(nc, m, "ln3")
        gcn_nodes(nc, m, "gcn")
        scatter_loop(nc, m, "gcn_edges", m.sum3, False)
        gcn_out(nc, m, a, "gcn_out", out)


def kernel(**inputs):
    import numpy as np
    import concourse.bacc as bacc
    from concourse.bass_utils import run_bass_kernel_spmd

    def padded(v, n, fill):
        v = np.asarray(v)
        return np.concatenate([v, np.full((n - v.shape[0],) + v.shape[1:], fill, v.dtype)])

    arrays = {k: np.asarray(v) for k, v in inputs.items()}
    arrays["x"] = padded(arrays["x"], NP, 0)
    for k in ("src", "dst"):
        arrays[k] = padded(arrays[k], EP, NP - 1)
    ea = arrays.pop("edge_attr_2")
    for c in (0, 1):
        arrays[f"ea{c}"] = padded(ea[:, c], EP, 0)
    arrays["edge_weight"] = padded(arrays["edge_weight"], EP, 0)
    arrays["L3_gnn_WT"] = arrays.pop("L3_gnn_W").T
    for k in ROWS:
        arrays[k] = arrays[k].reshape(-1)
    arrays = {f"in_{k}": np.ascontiguousarray(v) for k, v in arrays.items()}

    nc = bacc.Bacc("TRN2", target_bir_lowering=False, num_devices=1)
    a = {k[3:]: nc.dram_tensor(k, v.shape, mybir.dt.from_np(v.dtype), kind="ExternalInput").ap()
         for k, v in arrays.items()}
    out = nc.dram_tensor("out", (NP, D), F32, kind="ExternalOutput").ap()
    build(nc, a, out)
    r = run_bass_kernel_spmd(nc, [arrays], core_ids=[0])
    return r.results[0]["out"][0:N]
```

```python
import concourse.bass as bass
from concourse import mybir
from concourse.alu_op_type import AluOpType as ALU
from contextlib import ExitStack, contextmanager

F32 = mybir.dt.float32
BF16 = mybir.dt.bfloat16
I32 = mybir.dt.int32
ACT = mybir.ActivationFunctionType
AX = mybir.AxisListType

P = 128
N = 3125
NB = (N + P - 1) // P
NP = NB * P
D = 256
E = 100000
T = 4
WIN = T * P
NW = (E + WIN - 1) // WIN
EP = NW * WIN
NG = NW + NB - 1
U = 10
R = 5
TURNS = NG // U
TW = 264
HEADS = 4
DH = D // HEADS
DUMP = NP
BIG = 2.0 ** 100
SLOPE = 0.2
EPS = 1e-5
WE_PARTS = [(0, 6), (6, 10), (10, 12)]
KE = 12
CHUNKS = 5
WH = NW // 2
GH = [(0, P), (P, NG - P)]
assert NG % U == 0 and U % R == 0 and NW % 2 == 0


def flat(ap):
    return ap.rearrange("p a c -> p (a c)")


def blk(t, b, lo, hi):
    return flat(t[:, bass.ds(b, 1), lo:hi])


def mid(ap, n):
    return ap.unsqueeze(1).to_broadcast([ap.shape[0], n, ap.shape[1]])


def last(ap, n):
    return ap.unsqueeze(2).to_broadcast([ap.shape[0], ap.shape[1], n])


def drow(t, g):
    return t[bass.ds(g, 1), :].rearrange("a n -> (a n)")


def pipelined(eng, stages, blocks=None):
    deepest = max(lag for lag, _ in stages)
    load = blocks if blocks else lambda first, n: [None] * n
    of = load(0, U)
    for s in range(U):
        for lag, stage in stages:
            if s >= lag:
                stage(s - lag, s - lag, 0, of[s - lag])
    with eng.Fori(1, TURNS) as i:
        of = load(i * U - deepest, U + deepest)
        for s in range(U):
            for lag, stage in stages:
                u, turn = (s - lag, i) if s >= lag else (s - lag + U, i - 1)
                stage(turn * U + u, u, turn, of[s - lag + deepest])
    if deepest:
        of = load(NG - deepest, deepest)
    for s in range(deepest):
        for lag, stage in stages:
            if s < lag:
                stage(NG + s - lag, (s - lag) % U, TURNS - 1, of[s - lag + deepest])


def blocks_on(nc, m, engine):
    def load(first, n):
        _, values = nc.values_load_multi_w_load_instructions(
            m.tab[0:1, bass.ds(first, n)], engines=[engine], min_val=0, max_val=NB,
            skip_runtime_bounds_check_because="the list of groups has blocks 0 to NB only")
        return values
    return load


def after(eng, sem, t, back=0, each=1):
    if not isinstance(t, int) or t >= back:
        eng.wait_ge(sem, (t - back + 1) * each)


def nth(u, turn, ring):
    return turn * (U // ring) + (u // ring + 1)


class Semaphores:

    def __init__(self, nc, stage):
        self.nc, self.stage, self.used = nc, stage, []

    def sem(self, what):
        self.used.append(self.nc.alloc_semaphore(f"{self.stage}_{what}"))
        return self.used[-1]

    def sems(self, what, n):
        return [self.sem(f"{what}{i}") for i in range(n)]


@contextmanager
def stage_of(nc, name):
    st = Semaphores(nc, name)
    with nc.Block() as block:
        yield st, block
    nc.clear_and_free_semaphores(st.used)
    nc.all_engine_barrier()


class Memory:
    pass


def constants(nc, m, a):
    with stage_of(nc, "const") as (st, block):
        loaded, made, step = st.sem("loaded"), st.sem("made"), st.sem("step")
        replicated, split, stacked = st.sem("replicated"), st.sem("split"), st.sem("stacked")
        we_rep = {c: m.zs[0][0:KE, c - 1, :] for c in (1, 2)}
        we_rest = {c: m.zs[0][0:KE, c + 1, :] for c in (1, 2)}
        we_part = {c: [m.zs[1][0:KE, 2 * (c - 1) + s // 2, :].bitcast(BF16)[:, (s % 2) * D:(s % 2 + 1) * D]
                       for s in range(3)] for c in (1, 2)}

        @block.sync
        def _(sp):
            loads = [(m.x[:, :, :], a["x"].rearrange("(b p) c -> p b c", p=P))]
            loads += [(t[:, :], a[k].partition_broadcast(P)) for k, t in m.bc.items()]
            loads += [(t[:, r, :], a[k][r].partition_broadcast(P)) for k, t in m.We_bc.items() for r in (0, 1)]
            for c in (1, 2):
                for q in range(KE // 2):
                    sp.dma_start(we_rep[c][2 * q:2 * q + 2, :], a[f"L1_gnn_We{c}"]).then_inc(replicated, 16)
            for dst, src in loads:
                sp.dma_start(dst, src).then_inc(loaded, 16)
            sp.wait_ge(split, 8)
            for c in (1, 2):
                for s, (lo, hi) in enumerate(WE_PARTS):
                    sp.dma_start(m.We12[c][lo:hi, :], we_part[c][s][lo:hi, :]).then_inc(stacked, 16)
            sp.wait_ge(loaded, 16 * len(loads))
            sp.wait_ge(stacked, 16 * 2 * len(WE_PARTS))

        @block.gpsimd
        def _(pool):
            nc.gpsimd.memset(m.zero[:, :], 0.0).then_inc(made, 1)
            nc.gpsimd.memset(m.ident[:, :], 0.0).then_inc(made, 1)
            nc.gpsimd.memset(m.later32[:, :], 0.0).then_inc(made, 1)
            nc.gpsimd.iota(m.icol[:, :], [[0, 1]], base=0, channel_multiplier=1,
                           allow_small_or_imprecise_dtypes=True).then_inc(made, 1)
            nc.gpsimd.iota(m.irow[:, :], [[1, P]], base=0, channel_multiplier=0,
                           allow_small_or_imprecise_dtypes=True).then_inc(made, 1)
            pool.wait_ge(made, 3)
            nc.gpsimd.affine_select(out=m.ident[:, :], in_=m.ident[:, :], compare_op=ALU.not_equal, fill=1.0,
                                    base=0, pattern=[[-1, P]], channel_multiplier=1).then_inc(made, 1)
            nc.gpsimd.affine_select(out=m.later32[:, :], in_=m.later32[:, :], compare_op=ALU.is_ge, fill=1.0,
                                    base=0, pattern=[[-1, P]], channel_multiplier=1).then_inc(made, 1)

        @block.vector
        def _(dve):
            dve.wait_ge(made, 7)
            count = 0
            for ins in (
                    nc.vector.tensor_copy(m.ident_bf[:, :], m.ident[:, :]),
                    nc.vector.tensor_copy(m.later[:, :], m.later32[:, :]),
                    nc.vector.tensor_scalar(m.real[:, :], m.icol[:, :], float(N - (NB - 1) * P), 1.0 / N,
                                            ALU.is_lt, ALU.mult),
                    nc.vector.memset(m.mean_w[:, 0, :], 1.0 / N),
                    nc.vector.tensor_scalar(m.dumprow[:, :], m.icol[:, :], float(DUMP), None, ALU.add),
                    nc.vector.memset(m.one_bf[:, :], 1.0),
                    nc.vector.memset(m.minus_big[:, :], -BIG),
                    nc.vector.memset(m.one[:, :], 1.0),
                    nc.vector.tensor_scalar(m.minus_icol[:, :], m.icol[:, :], -1.0, None, ALU.mult),
                    nc.vector.memset(m.attr[:, :, :], 0.0),
                    nc.vector.memset(m.top[:, :, :], 0.0),
                    nc.vector.memset(m.adst3[:, :, :], 0.0),
                    nc.vector.memset(m.h[:, NB, :], 0.0)):
                ins.then_inc(step, 1)
                count += 1
            for C, of in ((T, m.of_tile), (T * HEADS, m.of_edge)):
                nc.vector.tensor_reduce(of[:, :], m.ident[0:3 * C, 0:3 * C].rearrange("k (c s) -> k c s", s=3), AX.X,
                                        ALU.add).then_inc(step, 1)
                count += 1
            dve.wait_ge(step, count)
            nc.vector.tensor_copy(m.mean_w[:, 1, :], m.real[:, 0:1].to_broadcast([P, P])).then_inc(step, 1)
            nc.vector.tensor_copy(m.tilesel[:, :, :], last(m.of_tile[:, :], P)).then_inc(step, 1)
            nc.vector.tensor_copy(m.edgesel[:, :, :], last(m.of_edge[:, :], P)).then_inc(step, 1)
            dve.wait_ge(replicated, 16 * KE)
            count = 0
            for c in (1, 2):
                hi, md, lo = we_part[c]
                for op in (lambda: nc.vector.tensor_copy(hi, we_rep[c]),
                           lambda: nc.vector.tensor_tensor(we_rest[c], we_rep[c], hi, ALU.subtract),
                           lambda: nc.vector.tensor_copy(md, we_rest[c]),
                           lambda: nc.vector.tensor_tensor(lo, we_rest[c], md, ALU.subtract)):
                    op().then_inc(split, 1)
                    count += 1
                    dve.wait_ge(split, count)


def zero_sums(eng, m, sums, zeroed):
    for j in range(T):
        rows = sums[j].rearrange("(b p) c -> p b c", p=P)
        eng.dma_start(rows, mid(m.zero[:, 0:rows.shape[2]], rows.shape[1])).then_inc(zeroed, 16)
    return 16 * T


def group_list(nc, m, a):
    with stage_of(nc, "list") as (st, block):
        loaded, step, spread = st.sem("loaded"), st.sem("step"), st.sem("spread")
        picked, windows, laid, done = st.sem("picked"), st.sem("windows"), st.sem("laid"), st.sem("done")
        local, linear, split, zeroed = st.sem("local"), st.sem("linear"), st.sem("split"), st.sem("zeroed")
        stage = m.h[:, 0:NB, :].rearrange("p b c -> p (b c)")
        part = [[stage[:, (5 * hh + q) * WIN:(5 * hh + q + 1) * WIN] for q in range(5)] for hh in (0, 1)]
        room = m.acc[:, :, :].rearrange("p b c -> p (b c)")
        lin = {c: [room[:, (2 * (c - 1) + hh) * WIN:(2 * (c - 1) + hh + 1) * WIN] for hh in (0, 1)] for c in (1, 2)}
        rest = [[m.gath[hh][:, 2 * r:2 * r + 2, :].rearrange("p j c -> p (j c)")[:, 0:WIN] for r in (0, 1)] for hh in (0, 1)]
        eab = [room[:, (6 + 3 * hh) * WIN:(9 + 3 * hh) * WIN].bitcast(BF16).rearrange("p (k n) -> p k n", k=6)
               for hh in (0, 1)]
        pairs = [(hh, r) for hh in (0, 1) for r in (0, 1)]
        casts, rests = st.sem("casts"), st.sem("rests")

        def by_tile(ap, hh):
            return ap[0:GH[hh][1], :].rearrange("p (e j) -> p j e", j=T)

        def part_of(s, hh, r):
            return eab[hh][0:GH[hh][1], 2 * s + r, :].rearrange("p (j e) -> p j e", j=T)

        sb = m.list
        ps = m.ps[0]

        @block.sync
        def _(sp):
            ends_of = a["dst"].rearrange("(h p n) -> p h n", p=WH, n=WIN)
            with nc.allow_non_contiguous_dma(reason="the two ends of each window"):
                sp.dma_start(sb["ends"][:, 0:2], ends_of[:, :, 0]).then_inc(loaded, 16)
                sp.dma_start(sb["ends"][:, 2:4], ends_of[:, :, WIN - 1]).then_inc(loaded, 16)
            sp.wait_ge(picked, 1)
            for hh, (g0, k) in enumerate(GH):
                sp.dma_start(m.block_of[g0:g0 + k].rearrange("(k a) -> k a", a=1),
                             sb["b_int"][0:k, hh:hh + 1]).then_inc(laid, 16)
            sp.wait_ge(windows, 16 * 10)
            sp.wait_ge(local, 2)
            for hh, (g0, k) in enumerate(GH):
                for q, t in enumerate((m.g_src, None, m.g_ea[0], m.g_ea[1], m.g_ew)):
                    if t is not None:
                        src = part[hh][q][0:k, :]
                        sp.dma_start(t[g0:g0 + k, :], src.bitcast(I32) if q == 0 else src).then_inc(laid, 16)
                sp.dma_start(m.g_loc[g0:g0 + k, :], sb["loc"][0:k, hh, :]).then_inc(laid, 16)
                sp.dma_start(m.g_locb[g0:g0 + k, :], sb["locb"][0:k, hh, :]).then_inc(laid, 16)
            sp.wait_ge(linear, 4)
            sp.wait_ge(split, 4)
            for hh, (g0, k) in enumerate(GH):
                for c in (1, 2):
                    sp.dma_start(m.g_lin[c][g0:g0 + k, :], lin[c][hh][0:k, :]).then_inc(laid, 16)
                for lo, hi in WE_PARTS:
                    sp.dma_start(m.g_eaT[g0:g0 + k, lo:hi, :], eab[hh][0:k, 0:hi - lo, :]).then_inc(laid, 16)
            sp.wait_ge(laid, 16 * 24)
            sp.dma_start(m.tab[0:1, 0:NG], m.block_of[0:NG].rearrange("(a g) -> a g", a=1)).then_inc(done, 16)
            sp.wait_ge(done, 16)

        @block.scalar
        def _(act):
            zeros = zero_sums(act, m, m.sum0, zeroed)
            act.wait_ge(windows, 16 * 10)
            for s in (0, 1):
                for hh, r in pairs:
                    if s == 1:
                        act.wait_ge(rests, 2 * hh + r + 1)
                    nc.scalar.copy(part_of(s, hh, r), by_tile(rest[hh][r] if s else part[hh][2 + r], hh)).then_inc(casts, 1)
            act.wait_ge(zeroed, zeros)

        @block.tensor
        def _(pe):
            pe.wait_ge(step, 3)
            for q in range(4):
                mm = nc.tensor.matmul(ps[:, q * WH:(q + 1) * WH], sb["spread"][:, q, :], m.ident[0:WH, 0:WH],
                                      start=True, stop=True)
            mm.then_inc(spread, 1)

        @block.vector
        def _(dve):
            count = [0]

            def link(ins):
                count[0] += 1
                ins.then_inc(step, 1)
                dve.wait_ge(step, count[0])

            dve.wait_ge(loaded, 32)
            link(nc.vector.tensor_scalar(sb["ends"][:, :], sb["ends"][:, :], 7, None, ALU.logical_shift_right))
            link(nc.vector.tensor_copy(sb["ends_f"][:, :], sb["ends"][:, :]))
            link(nc.vector.tensor_copy(sb["spread"][:, :, :], last(sb["ends_f"][:, :], P)))
            dve.wait_ge(spread, 1)
            link(nc.vector.tensor_copy(sb["fl"][:, :], ps[:, 0:2 * NW]))
            first, final = sb["fl"][:, 0:NW], sb["fl"][:, NW:2 * NW]
            link(nc.vector.tensor_tensor(sb["cnt"][:, :], final, first, ALU.subtract))
            link(nc.vector.tensor_scalar(sb["cnt"][:, :], sb["cnt"][:, :], 1.0, None, ALU.add))
            link(nc.vector.memset(sb["one"][:, :], 1.0))
            link(nc.vector.tensor_tensor_scan(sb["off"][:, :], sb["one"][:, :], sb["cnt"][:, :], 0.0,
                                              ALU.mult, ALU.add))
            link(nc.vector.tensor_tensor(sb["off"][:, :], sb["off"][:, :], sb["cnt"][:, :], ALU.subtract))
            for hh in (0, 1):
                gid, w, o, b = (sb[k][:, hh:hh + 1] for k in ("gid", "w", "o", "b"))
                link(nc.vector.tensor_scalar(gid, m.icol[:, :], float(P * hh), None, ALU.add))
                link(nc.vector.tensor_scalar(sb["one"][:, :], sb["off"][:, :], gid, None, ALU.is_le))
                link(nc.vector.tensor_reduce(w, sb["one"][:, :], AX.X, ALU.add))
                link(nc.vector.tensor_scalar(w, w, 1.0, None, ALU.subtract))
                link(nc.vector.tensor_tensor(sb["cnt"][:, :], sb["one"][:, :], sb["off"][:, :], ALU.mult))
                link(nc.vector.tensor_reduce(o, sb["cnt"][:, :], AX.X, ALU.max))
                link(nc.vector.tensor_tensor(sb["cnt"][:, :], sb["one"][:, :], first, ALU.mult))
                link(nc.vector.tensor_reduce(b, sb["cnt"][:, :], AX.X, ALU.max))
                link(nc.vector.tensor_tensor(b, b, gid, ALU.add))
                link(nc.vector.tensor_tensor(b, b, o, ALU.subtract))
                link(nc.vector.tensor_scalar(b, b, float(NB), None, ALU.min))
            link(nc.vector.tensor_copy(sb["w_int"][:, :], sb["w"][:, :]))
            link(nc.vector.tensor_scalar(sb["base"][:, :], sb["b"][:, :], float(P), None, ALU.mult))
            nc.vector.tensor_copy(sb["b_int"][:, :], sb["b"][:, :]).then_inc(picked, 1)
            dve.wait_ge(windows, 16 * 10)
            for hh, (g0, k) in enumerate(GH):
                loc = sb["loc"][0:k, hh, :]
                link(nc.vector.tensor_scalar(loc, part[hh][1][0:k, :].bitcast(I32), sb["base"][0:k, hh:hh + 1], -1.0,
                                             ALU.subtract, ALU.max))
                link(nc.vector.tensor_scalar(loc, loc, float(P), None, ALU.min))
                nc.vector.tensor_copy(sb["locb"][0:k, hh, :].rearrange("p (j e) -> p j e", j=T),
                                      loc.rearrange("p (e j) -> p j e", j=T)).then_inc(local, 1)
            for c in (1, 2):
                for r in (0, 1):
                    link(nc.vector.scalar_tensor_tensor(m.junk[:, :], m.We_bc[f"L1_gnn_We{c}"][:, r, :], SLOPE,
                                                        m.bc[f"L1_gnn_att{c}"][:, :], ALU.mult, ALU.mult,
                                                        accum_out=m.ea_lin[c][:, r:r + 1]))
            for hh, (g0, k) in enumerate(GH):
                ea = [part[hh][2 + r][0:k, :] for r in (0, 1)]
                for c in (1, 2):
                    out = lin[c][hh][0:k, :]
                    link(nc.vector.tensor_scalar(out, ea[0], m.ea_lin[c][0:k, 0:1], None, ALU.mult))
                    nc.vector.scalar_tensor_tensor(out, ea[1], m.ea_lin[c][0:k, 1:2], out, ALU.mult,
                                                   ALU.add).then_inc(linear, 1)
            for n, (hh, r) in enumerate(pairs):
                dve.wait_ge(casts, n + 1)
                nc.vector.tensor_tensor(by_tile(rest[hh][r], hh), by_tile(part[hh][2 + r], hh), part_of(0, hh, r),
                                        ALU.subtract).then_inc(rests, 1)
            for n, (hh, r) in enumerate(pairs):
                dve.wait_ge(casts, 4 + n + 1)
                nc.vector.tensor_tensor(part_of(2, hh, r), by_tile(rest[hh][r], hh), part_of(1, hh, r),
                                        ALU.subtract).then_inc(split, 1)

        @block.gpsimd
        def _(pool):
            pool.wait_ge(picked, 1)
            for hh, (g0, k) in enumerate(GH):
                for q, name in enumerate(("src", "dst", "ea0", "ea1", "edge_weight")):
                    out = part[hh][q][0:k, :]
                    pool.indirect_dma_start(out.bitcast(I32) if q < 2 else out, None,
                                            a[name].rearrange("(w n) -> w n", n=WIN),
                                            bass.IndirectOffsetOnAxis(sb["w_int"][0:k, hh:hh + 1], 0)
                                            ).then_inc(windows, 16)


def layer_norm(nc, m, name, scale=None):
    with stage_of(nc, name) as (st, block):
        stats, step, root, normed = st.sem("stats"), st.sem("step"), st.sem("root"), st.sem("normed")
        halves = [(0, NB // 2 + 2), (NB // 2 + 2, NB)]
        n_steps = 6 if scale else 4

        @block.scalar
        def _(act):
            for q, (lo, hi) in enumerate(halves):
                act.wait_ge(step, n_steps * q + 1)
                nc.scalar.activation(m.rstd[:, lo:hi], m.mv[:, lo:hi, 1], ACT.Sqrt).then_inc(root, 1)
                act.wait_ge(step, n_steps * (q + 1))
                for b in range(lo, hi):
                    nc.scalar.activation(m.h[:, b, :], m.x[:, b, :], ACT.Relu, scale=m.rstd[:, b:b + 1],
                                         bias=m.shift[:, b:b + 1]).then_inc(normed, 1)

        @block.vector
        def _(dve):
            for q, (lo, hi) in enumerate(halves):
                n = n_steps * q
                for b in range(lo, hi):
                    nc.vector.bn_stats(m.st6[:, b, :], m.x[:, b, :]).then_inc(stats, 1)
                for b in range(lo, hi):
                    dve.wait_ge(stats, lo + b + 1)
                    nc.vector.bn_aggr(m.mv[:, b, :], m.st6[:, b, :]).then_inc(stats, 1)
                dve.wait_ge(stats, 2 * hi)
                mean, rstd, shift = m.mv[:, lo:hi, 0], m.rstd[:, lo:hi], m.shift[:, lo:hi]
                nc.vector.tensor_scalar(m.mv[:, lo:hi, 1], m.mv[:, lo:hi, 1], EPS, None, ALU.add).then_inc(step, 1)
                dve.wait_ge(root, q + 1)
                nc.vector.reciprocal(rstd, rstd).then_inc(step, 1)
                dve.wait_ge(step, n + 2)
                nc.vector.tensor_tensor(shift, mean, rstd, ALU.mult).then_inc(step, 1)
                dve.wait_ge(step, n + 3)
                nc.vector.tensor_scalar(shift, shift, -1.0, None, ALU.mult).then_inc(step, 1)
                if scale:
                    dve.wait_ge(step, n + 4)
                    for t in (rstd, shift):
                        nc.vector.tensor_tensor(t, t, scale[:, lo:hi], ALU.mult).then_inc(step, 1)


def scatter_loop(nc, m, name, sums, weighted):
    W = D + 1 if weighted else D
    PW = P + 3 if weighted else P
    spare = m.xr3[:, :, :].rearrange("p b c -> p (b c)").bitcast(F32)
    spare2 = m.acc[:, :, :].rearrange("p b c -> p (b c)")

    def ring_in(space, start, n, width, dt=F32):
        words = T * width * (2 if dt == BF16 else 4) // 4
        bufs = [space[:, start + r * words:start + (r + 1) * words] for r in range(n)]
        return [(t if dt == F32 else t.bitcast(dt)).rearrange("p (j e) -> p j e", j=T) for t in bufs]

    pick, eqw = ring_in(spare, 0, R, P), ring_in(spare, R * WIN, R, P + 3)
    oh = ring_in(spare, R * T * (2 * P + 3), R, P, F32 if weighted else BF16)
    srow = [spare2[:, r * WIN:(r + 1) * WIN].bitcast(I32) for r in range(R)]
    eq, eqb = ring_in(spare2, R * WIN, R, P, BF16), ring_in(spare2, 2 * R * WIN, 2, P, BF16)
    rhs = eqw if weighted else eq
    y = m.gath
    banks = [m.psum[:, 2 * q:2 * q + 2, :] for q in range(4)]
    pick_ps = [banks[q][:, :, 0:2 * PW].rearrange("p a (i c) -> p a i c", i=2) for q in (0, 1)]
    dup_ps, cnt_ps = ([banks[q][:, a, 2 * PW:2 * PW + T] for q in (0, 1)] for a in (0, 1))
    rows_ps = [banks[2 + q].rearrange("p a (i c) -> p (a i) c", i=2) for q in (0, 1)]
    with stage_of(nc, name) as (st, block):
        arrived = st.sems("arrived", R)
        eq_made, inb_made, matrices = st.sem("eq_made"), st.sem("inb_made"), st.sem("matrices")
        ones, eqb_made, away_made, moved = st.sem("ones"), st.sem("eqb_made"), st.sem("away_made"), st.sem("moved")
        targets, attr_summed, attr_added = st.sem("targets"), st.sem("attr_summed"), st.sem("attr_added")
        multiplied, pick_ready, rows_made, copied = (st.sem(k) for k in ("multiplied", "pick_ready", "rows_made", "copied"))
        added, begun = st.sems("added", T), st.sem("begun")
        n_loads = 6 if weighted else 3

        @block.sync
        def _(sp):
            def load(t, u, turn, b):
                r = u % R
                after(sp, targets, t, R)

                def col(dst, src):
                    sp.dma_start(dst, drow(src, t).rearrange("(p j) -> p j", j=T)).then_inc(arrived[r], 16)

                col(m.src_col[r][:, :], m.g_src)
                col(m.loc[r][:, :], m.g_loc)
                sp.dma_start(srow[r], drow(m.g_src, t).partition_broadcast(P)).then_inc(arrived[r], 16)
                if weighted:
                    col(m.ew[r][:, :], m.g_ew)
                    col(m.ea[r][:, 0, :], m.g_ea[0])
                    col(m.ea[r][:, 1, :], m.g_ea[1])

            pipelined(sp, [(0, load)])
            for j in range(T):
                sp.wait_ge(added[j], 16 * NG)

        @block.vector
        def _(dve):
            if weighted:
                for r in range(R):
                    nc.vector.memset(eqw[r][:, :, P + 2], 1.0).then_inc(ones, 1)
                dve.wait_ge(ones, R)

            def make_matrices(t, u, turn, b):
                r = u % R
                dve.wait_ge(arrived[r], 16 * n_loads * nth(u, turn, R))
                nc.vector.tensor_tensor(eq[r], srow[r].rearrange("p (e j) -> p j e", j=T),
                                        last(m.src_col[r][:, :], P), ALU.is_equal).then_inc(eq_made, 1)
                nc.vector.tensor_tensor(m.away[r][:, :], m.dumprow[:, 0:1].to_broadcast([P, T]), m.src_col[r][:, :],
                                        ALU.subtract).then_inc(away_made, 1)
                if weighted:
                    nc.vector.tensor_scalar(m.inb[r][:, :], m.loc[r][:, :], 0.0, None, ALU.is_ge).then_inc(inb_made, 1)
                    nc.vector.tensor_copy(eqw[r][:, :, P:P + 2], m.ea[r][:, :, :].rearrange("p c j -> p j c"))
                nc.vector.tensor_tensor(oh[r], mid(m.irow[:, :], T), last(m.loc[r][:, :], P),
                                        ALU.is_equal).then_inc(matrices, 1)
                if weighted:
                    dve.wait_ge(inb_made, t + 1)
                    nc.vector.scalar_tensor_tensor(m.inb[r][:, :], m.loc[r][:, :], float(P), m.inb[r][:, :],
                                                   ALU.is_lt, ALU.mult).then_inc(matrices, 1)
                    dve.wait_ge(eq_made, t + 1)
                    nc.vector.tensor_tensor(eqw[r][:, :, 0:P], eq[r], last(m.ew[r][:, :], P),
                                            ALU.mult).then_inc(matrices, 1)
                dve.wait_ge(eq_made, t + 1)
                after(dve, multiplied, t, 2)
                nc.vector.tensor_tensor(eqb[u % 2], eq[r], mid(m.later[:, :], T), ALU.mult).then_inc(eqb_made, 1)

            def finish(t, u, turn, b):
                r = u % R
                dve.wait_ge(pick_ready, t + 1)
                dve.wait_ge(away_made, t + 1)
                for j in range(T):
                    after(dve, added[j], t, R, 16)
                nc.vector.scalar_tensor_tensor(m.away[r][:, :], dup_ps[u % 2], 0.5, m.away[r][:, :], ALU.is_gt,
                                               ALU.mult).then_inc(moved, 1)
                if weighted:
                    nc.vector.tensor_copy(y[r][:, :, D], cnt_ps[u % 2])
                    after(dve, attr_added, t, 1)
                    nc.vector.tensor_reduce(m.attr_sum[:, :], pick_ps[u % 2][:, :, :, P:P + 3].rearrange("p a i c -> p c a i"),
                                            AX.XY, ALU.add).then_inc(attr_summed, 1)
                dve.wait_ge(moved, t + 1)
                nc.vector.tensor_tensor(m.to_row[r][:, :], m.away[r][:, :], m.src_col[r][:, :],
                                        ALU.add).then_inc(targets, 1)
                if weighted:
                    dve.wait_ge(attr_summed, t + 1)
                    nc.vector.tensor_tensor(blk(m.attr, b, 0, 3), blk(m.attr, b, 0, 3), m.attr_sum[:, :],
                                            ALU.add).then_inc(attr_added, 1)

            pipelined(dve, [(0, make_matrices), (1, finish)], blocks_on(nc, m, mybir.EngineType.DVE) if weighted else None)

        @block.tensor
        def _(pe):
            n_mat = 3 if weighted else 1

            def pick_rows(t, u, turn, b):
                r, q = u % R, u % 2
                pe.wait_ge(matrices, n_mat * (t + 1))
                pe.wait_ge(eqb_made, t + 1)
                after(pe, pick_ready, t, 2)
                after(pe, targets, t, 2)
                for j in range(T):
                    nc.tensor.matmul(pick_ps[q][:, j // 2, j % 2, :], oh[r][:, j, :], rhs[r][:, j, 0:PW],
                                     start=True, stop=True)
                for j in range(T):
                    mm = nc.tensor.matmul(dup_ps[q][:, j:j + 1], eqb[q][:, j, :], m.one_bf[:, :],
                                          start=True, stop=True)
                if weighted:
                    for j in range(T):
                        mm = nc.tensor.matmul(cnt_ps[q][:, j:j + 1], eq[r][:, j, :], m.inb[r][:, j:j + 1],
                                              start=True, stop=True)
                mm.then_inc(multiplied, 1)

            def make_rows(t, u, turn, b):
                r, q = u % R, u % 2
                pe.wait_ge(pick_ready, t + 1)
                after(pe, copied, t, 2)
                for j in range(T):
                    mm = nc.tensor.matmul(rows_ps[q][:, j, :], pick[r][:, j, :], blk(m.h, b, 0, D),
                                          start=True, stop=True)
                mm.then_inc(rows_made, 1)

            pipelined(pe, [(0, pick_rows), (1, make_rows)], blocks_on(nc, m, mybir.EngineType.PE))

        @block.scalar
        def _(act):
            def copy_pick(t, u, turn, b):
                r = u % R
                act.wait_ge(multiplied, t + 1)
                nc.scalar.copy(pick[r].rearrange("p (a i) e -> p a i e", i=2),
                               pick_ps[u % 2][:, :, :, 0:P]).then_inc(pick_ready, 1)

            def copy_rows(t, u, turn, b):
                r = u % R
                act.wait_ge(rows_made, t + 1)
                for j in range(T):
                    after(act, added[j], t, R, 16)
                nc.scalar.copy(y[r][:, :, 0:D], rows_ps[u % 2]).then_inc(copied, 1)

            pipelined(act, [(0, copy_pick), (1, copy_rows)])

        @block.gpsimd
        def _(pool):
            def add_rows(t, u, turn, b):
                r = u % R
                for sem in (copied, targets):
                    pool.wait_ge(sem, t + 1)
                for j in range(T):
                    after(pool, added[j], t, 1, 16)
                    pool.sem_inc(begun, 1)
                    pool.indirect_dma_start(sums[j], bass.IndirectOffsetOnAxis(m.to_row[r][:, j:j + 1], 0),
                                            y[r][:, j, 0:W], None, compute_op=ALU.add).then_inc(added[j], 16)

            pipelined(pool, [(0, add_rows)])


def gatv2_loop(nc, m, name, table, c):
    WA = D + 1
    K = 3 * T
    with stage_of(nc, name) as (st, block):
        arrived, gathered, begun = st.sems("arrived", R), st.sems("gathered", R), st.sem("begun")
        distance = st.sem("distance")
        placed, masked, mixed, summed = (st.sem(k) for k in ("placed", "masked", "mixed", "summed"))
        dotted, logits, hi_made, rest_made = (st.sem(k) for k in ("dotted", "logits", "hi_made", "rest_made"))
        mid_made, parts, turned, copied = (st.sem(k) for k in ("mid_made", "parts", "turned", "copied"))
        shown, seen, raised, dropped = (st.sem(k) for k in ("shown", "seen", "raised", "dropped"))
        top_set, shrink, exps, flipped = (st.sem(k) for k in ("top_set", "shrink", "exps", "flipped"))
        weights, group_sum, done = (st.sem(k) for k in ("weights", "group_sum", "done"))
        n_loads = 4
        zb = [m.psum[:, 2 * q:2 * q + 2, :].rearrange("p a (c f) -> p (a c) f", f=D) for q in (0, 1)]
        shown_ps, flip_ps, sum_ps, turn_ps = m.ps[4], m.ps[5], m.ps[6], m.ps[7]
        rows = m.rows[0:K, :]

        @block.sync
        def _(sp):
            def load(t, u, turn, b):
                r = u % R
                after(sp, logits, t, R)

                def col(dst, src):
                    sp.dma_start(dst, drow(src, t).rearrange("(p j) -> p j", j=T)).then_inc(arrived[r], 16)

                col(m.src_col[r][:, :], m.g_src)
                col(m.lin[r][:, :], m.g_lin[c])
                sp.dma_start(m.locrow[r][:, :], drow(m.g_locb, t).partition_broadcast(P)).then_inc(arrived[r], 16)
                sp.dma_start(m.eaT[r][:, :], m.g_eaT[bass.ds(t, 1), :, :].rearrange("a k n -> (a k) n")
                             ).then_inc(arrived[r], 16)

            pipelined(sp, [(0, load)])

        @block.gpsimd
        def _(pool):
            def gather(t, u, turn, b):
                r = u % R
                pool.wait_ge(arrived[r], 16 * n_loads * nth(u, turn, R))
                after(pool, group_sum, t, R)
                pool.sem_inc(begun, 1)
                for j in range(T):
                    pool.indirect_dma_start(m.gath[r][:, j, :], None, table,
                                            bass.IndirectOffsetOnAxis(m.src_col[r][:, j:j + 1], 0)
                                            ).then_inc(gathered[r], 16)

            pipelined(pool, [(0, gather)])

        @block.vector
        def _(dve):
            def sum_inputs(t, u, turn, b):
                r, q = u % R, u % 2
                dve.wait_ge(mixed, t + 1)
                dve.wait_ge(gathered[r], 16 * T * nth(u, turn, R))
                nc.vector.tensor_tensor(m.zs[q][:, :, :], zb[q], m.gath[r][:, :, 0:D], ALU.add).then_inc(summed, 1)
                nc.vector.tensor_tensor(m.lin[r][:, :], m.gath[r][:, :, WA], m.lin[r][:, :], ALU.add)

            def dot(t, u, turn, b):
                q = u % 2
                dve.wait_ge(summed, t + 1)
                for j in range(T):
                    ins = nc.vector.scalar_tensor_tensor(m.zs[q][:, j, :], m.zs[q][:, j, :], 0.0, m.att_relu[:, :],
                                                         ALU.max, ALU.mult, accum_out=m.dots[:, j:j + 1])
                ins.then_inc(dotted, 1)

            def see(t, u, turn, b):
                dve.wait_ge(shown, t + 1)
                nc.vector.tensor_reduce(m.seen[:, 0:1], shown_ps[:, :], AX.X, ALU.max).then_inc(seen, 1)

            def add_linear(t, u, turn, b):
                r = u % R
                dve.wait_ge(dotted, t + 1)
                nc.vector.tensor_tensor(m.lg[:, 0:T], m.dots[:, :], m.lin[r][:, :], ALU.add).then_inc(logits, 1)

            hi, md, lo = (m.parts[:, 0:K].rearrange("p (c s) -> p c s", s=3)[:, :, s] for s in range(3))

            def raise_top(t, u, turn, b):
                dve.wait_ge(seen, t + 1)
                after(dve, top_set, t, 1)
                nc.vector.scalar_tensor_tensor(m.new[:, 0:1], m.seen[:, 0:1], -1.0, blk(m.top, b, 0, 1), ALU.mult,
                                               ALU.min).then_inc(raised, 1)

            def high_part(t, u, turn, b):
                dve.wait_ge(logits, t + 1)
                after(dve, turned, t, 1)
                nc.vector.tensor_copy(hi, m.lg[:, 0:T]).then_inc(hi_made, 1)

            def drop(t, u, turn, b):
                dve.wait_ge(raised, t + 1)
                after(dve, shrink, t, 1)
                nc.vector.tensor_tensor(m.drop[:, 0:1], m.new[:, 0:1], blk(m.top, b, 0, 1),
                                        ALU.subtract).then_inc(dropped, 1)

            def without_high(t, u, turn, b):
                dve.wait_ge(hi_made, t + 1)
                nc.vector.tensor_tensor(m.rest[:, 0:T], m.lg[:, 0:T], hi, ALU.subtract).then_inc(rest_made, 1)

            def set_top(t, u, turn, b):
                dve.wait_ge(dropped, t + 1)
                nc.vector.tensor_tensor(blk(m.top, b, 0, 1), blk(m.top, b, 0, 1), m.new[:, 0:1],
                                        ALU.min).then_inc(top_set, 1)

            def middle_part(t, u, turn, b):
                dve.wait_ge(rest_made, t + 1)
                nc.vector.tensor_copy(md, m.rest[:, 0:T]).then_inc(mid_made, 1)

            def add_group(t, u, turn, b):
                r = u % R
                dve.wait_ge(group_sum, t + 1)
                dve.wait_ge(shrink, t + 1)
                after(dve, done, t, 1)
                acc = blk(m.acc, b, 0, WA)
                nc.vector.scalar_tensor_tensor(acc, acc, m.less[r][:, 0:1], sum_ps[:, 0:WA], ALU.mult,
                                               ALU.add).then_inc(done, 1)

            def low_part(t, u, turn, b):
                dve.wait_ge(mid_made, t + 1)
                nc.vector.tensor_tensor(lo, m.rest[:, 0:T], md, ALU.subtract).then_inc(parts, 1)

            pipelined(dve, [(2, sum_inputs), (2, dot), (3, see), (2, add_linear), (5, add_group), (3, raise_top),
                            (2, high_part), (3, drop), (2, without_high), (3, set_top), (2, middle_part),
                            (2, low_part)], blocks_on(nc, m, mybir.EngineType.DVE))
            dve.wait_ge(done, NG)

        @block.scalar
        def _(act):
            def copy_turned(t, u, turn, b):
                act.wait_ge(turned, t + 1)
                nc.scalar.copy(rows, turn_ps[0:K, 0:P]).then_inc(copied, 1)

            def copy_weights(t, u, turn, b):
                act.wait_ge(flipped, t + 1)
                nc.scalar.copy(m.prob[:, 0, :], flip_ps[:, :]).then_inc(weights, 1)

            def place(t, u, turn, b):
                r = u % R
                act.wait_ge(arrived[r], 16 * n_loads * nth(u, turn, R))
                nc.scalar.activation(m.locrow[r][:, :], m.locrow[r][:, :], ACT.Abs,
                                     bias=m.minus_icol[:, 0:1]).then_inc(distance, 1)
                act.wait_ge(distance, t + 1)
                nc.scalar.activation(m.ohT[r][:, :], m.locrow[r][:, :], ACT.Relu, scale=-1.0,
                                     bias=m.one[:, 0:1]).then_inc(placed, 1)

            def mask(t, u, turn, b):
                r = u % R
                act.wait_ge(placed, t + 1)
                nc.scalar.activation(m.off[r][:, :], m.ohT[r][:, :], ACT.Identity, scale=BIG,
                                     bias=m.minus_big[:, 0:1]).then_inc(masked, 1)

            def exponentials(t, u, turn, b):
                r = u % R
                act.wait_ge(raised, t + 1)
                nc.scalar.activation(m.expT[:, :], shown_ps[:, :], ACT.Exp, bias=m.new[:, 0:1]).then_inc(exps, 1)
                act.wait_ge(dropped, t + 1)
                nc.scalar.activation(m.less[r][:, 0:1], m.drop[:, 0:1], ACT.Exp).then_inc(shrink, 1)

            pipelined(act, [(3, copy_turned), (4, copy_weights), (0, place), (1, mask), (3, exponentials)])

        @block.tensor
        def _(pe):
            def turn_parts(t, u, turn, b):
                pe.wait_ge(parts, t + 1)
                nc.tensor.matmul(turn_ps[0:K, 0:P], m.parts[:, 0:K], m.ident_bf[:, :], start=True,
                                 stop=True).then_inc(turned, 1)

            def flip(t, u, turn, b):
                pe.wait_ge(exps, t + 1)
                for j in range(T):
                    mm = nc.tensor.transpose(flip_ps[:, j * P:(j + 1) * P], m.expT[:, j * P:(j + 1) * P], m.ident[:, :])
                mm.then_inc(flipped, 1)

            def mix(t, u, turn, b):
                r, q = u % R, u % 2
                pe.wait_ge(placed, t + 1)
                after(pe, summed, t, 2)
                for j in range(T):
                    e = slice(j * P, (j + 1) * P)
                    for s in range(3):
                        nc.tensor.matmul(zb[q][:, j, :], m.ohT[r][:, e], blk(m.xr3, b, s * D, (s + 1) * D),
                                         start=(s == 0), stop=False)
                    mm = nc.tensor.matmul(zb[q][:, j, :], m.eaT[r][:, e], m.We12[c][:, :], start=False, stop=True)
                mm.then_inc(mixed, 1)

            def show_logits(t, u, turn, b):
                r = u % R
                pe.wait_ge(copied, t + 1)
                pe.wait_ge(masked, t + 1)
                nc.tensor.matmul(shown_ps[:, :], m.ident_bf[:, :], m.off[r][:, :], start=True, stop=False)
                for j in range(T):
                    mm = nc.tensor.matmul(shown_ps[:, j * P:(j + 1) * P], m.tilesel[:, j, :], rows,
                                          start=False, stop=(j == T - 1))
                mm.then_inc(shown, 1)

            def sum_group(t, u, turn, b):
                r = u % R
                pe.wait_ge(weights, t + 1)
                after(pe, done, t, 1)
                for j in range(T):
                    mm = nc.tensor.matmul(sum_ps[:, 0:WA], m.prob[:, 0, j * P:(j + 1) * P], m.gath[r][:, j, 0:WA],
                                          start=(j == 0), stop=(j == T - 1))
                mm.then_inc(group_sum, 1)

            pipelined(pe, [(3, turn_parts), (4, flip), (3, show_logits), (1, mix), (4, sum_group)],
                      blocks_on(nc, m, mybir.EngineType.PE))


def gat_loop(nc, m, name, table):
    H = HEADS
    C = T * H
    K = 3 * C
    DVE_TILES = 2
    WA = H * (DH + 1)
    with stage_of(nc, name) as (st, block):
        arrived, gathered, begun = st.sems("arrived", R), st.sems("gathered", R), st.sem("begun")
        placed, masked, mixed, summed = (st.sem(k) for k in ("placed", "masked", "mixed", "summed"))
        pairs, logits, hi_made, rest_made = (st.sem(k) for k in ("pairs", "logits", "hi_made", "rest_made"))
        mid_made, parts, turned, copied = (st.sem(k) for k in ("mid_made", "parts", "turned", "copied"))
        shown, seen, raised, dropped = (st.sem(k) for k in ("shown", "seen", "raised", "dropped"))
        top_set, shrink, exps, top_here = (st.sem(k) for k in ("top_set", "shrink", "exps", "top_here"))
        top_hi, top_rest, top_mid, top_parts = (st.sem(k) for k in ("top_hi", "top_rest", "top_mid", "top_parts"))
        here, below, depth, flipped, chosen = (st.sem(k) for k in ("here", "below", "depth", "flipped", "chosen"))
        dve_weighed, act_weighed = st.sem("dve_weighed"), st.sem("act_weighed")
        group_sum, rescaled, done = (st.sem(k) for k in ("group_sum", "rescaled", "done"))
        n_loads = 2
        sum_ps, turn_ps, flip_ps = m.ps[5], m.ps[6], m.ps[7]
        adst_ps, here_ps = m.ps[4][:, 0:K], m.ps[4][:, K:2 * K]
        rows = m.rows[0:K, :]

        def heads(ap):
            return ap.rearrange("p j (h c) -> p j h c", h=H)

        @block.sync
        def _(sp):
            def load(t, u, turn, b):
                r = u % R
                after(sp, logits, t, R)

                sp.dma_start(m.src_col[r][:, :], drow(m.g_src, t).rearrange("(p j) -> p j", j=T)).then_inc(arrived[r], 16)
                sp.dma_start(m.locrow[r][:, :], drow(m.g_locb, t).partition_broadcast(P)).then_inc(arrived[r], 16)

            pipelined(sp, [(0, load)])

        @block.gpsimd
        def _(pool):
            def gather(t, u, turn, b):
                r = u % R
                pool.wait_ge(arrived[r], 16 * n_loads * nth(u, turn, R))
                after(pool, group_sum, t, R)
                pool.sem_inc(begun, 1)
                for j in range(T):
                    pool.indirect_dma_start(m.gath[r][:, j, :], None, table,
                                            bass.IndirectOffsetOnAxis(m.src_col[r][:, j:j + 1], 0)
                                            ).then_inc(gathered[r], 16)

            pipelined(pool, [(0, gather)])

        @block.vector
        def _(dve):
            def three(ap):
                return [ap.rearrange("p (c s) -> p c s", s=3)[:, :, s] for s in range(3)]

            def place(t, u, turn, b):
                r = u % R
                dve.wait_ge(arrived[r], 16 * n_loads * nth(u, turn, R))
                nc.vector.tensor_scalar(m.ohT[r][:, :], m.locrow[r][:, :], m.icol[:, 0:1], None,
                                        ALU.is_equal).then_inc(placed, 1)

            def sum_parts(t, u, turn, b):
                dve.wait_ge(mixed, t + 1)
                nc.vector.tensor_reduce(m.e4[:, :], adst_ps.rearrange("p (c s) -> p c s", s=3), AX.X,
                                        ALU.add).then_inc(summed, 1)

            def add_src(t, u, turn, b):
                r = u % R
                dve.wait_ge(summed, t + 1)
                dve.wait_ge(gathered[r], 16 * T * nth(u, turn, R))
                e4 = m.e4[:, :].rearrange("p (j h) -> p j h", h=H)
                nc.vector.tensor_tensor(e4, e4, m.gath[r][:, :, WA:WA + H], ALU.add).then_inc(pairs, 1)

            def leak(t, u, turn, b):
                dve.wait_ge(pairs, t + 1)
                nc.vector.scalar_tensor_tensor(m.lgs[u % R][:, :], m.e4[:, :], SLOPE, m.e4[:, :], ALU.mult,
                                               ALU.max).then_inc(logits, 1)

            hi, md, lo = three(m.parts[:, 0:K])

            def high_part(t, u, turn, b):
                dve.wait_ge(logits, t + 1)
                after(dve, turned, t, 1)
                nc.vector.tensor_copy(hi, m.lgs[u % R][:, :]).then_inc(hi_made, 1)

            def without_high(t, u, turn, b):
                dve.wait_ge(hi_made, t + 1)
                nc.vector.tensor_tensor(m.rest[:, 0:C], m.lgs[u % R][:, :], hi, ALU.subtract).then_inc(rest_made, 1)

            def middle_part(t, u, turn, b):
                dve.wait_ge(rest_made, t + 1)
                nc.vector.tensor_copy(md, m.rest[:, 0:C]).then_inc(mid_made, 1)

            def low_part(t, u, turn, b):
                dve.wait_ge(mid_made, t + 1)
                nc.vector.tensor_tensor(lo, m.rest[:, 0:C], md, ALU.subtract).then_inc(parts, 1)

            def take_top(t, u, turn, b):
                dve.wait_ge(top_here, t + 1)
                nc.vector.tensor_reduce(m.here[:, :], here_ps.rearrange("p (c s) -> p c s", s=3), AX.X,
                                        ALU.add).then_inc(here, 1)

            def sink(t, u, turn, b):
                dve.wait_ge(here, t + 1)
                nc.vector.tensor_tensor(m.here[:, :], m.here[:, :], m.lgs[u % R][:, :], ALU.add).then_inc(below, 1)

            def bound(t, u, turn, b):
                dve.wait_ge(below, t + 1)
                nc.vector.tensor_scalar(m.depth[u % R][:, :], m.here[:, :], 0.0, None, ALU.min).then_inc(depth, 1)

            def weigh(t, u, turn, b):
                r = u % R
                dve.wait_ge(exps, t + 1)
                own = heads(m.gath[r][:, 0:DVE_TILES, 0:WA])
                by = m.ex[r][:, 0:DVE_TILES * H].rearrange("p (j h) -> p j h", h=H)
                nc.vector.tensor_tensor(own, own, by.unsqueeze(3).to_broadcast([P, DVE_TILES, H, DH + 1]),
                                        ALU.mult).then_inc(dve_weighed, 1)

            def see(t, u, turn, b):
                for q in (0, 1):
                    dve.wait_ge(shown, 2 * t + q + 1)
                    ins = nc.vector.tensor_reduce(m.seen[:, 2 * q:2 * q + 2], m.psum[:, 2 * q:2 * q + 2, :], AX.X, ALU.max)
                ins.then_inc(seen, 1)

            def raise_top(t, u, turn, b):
                after(dve, top_set, t, 1)
                dve.wait_ge(seen, t + 1)
                nc.vector.scalar_tensor_tensor(new, m.seen[:, 0:H], -1.0, blk(m.top, b, 0, H), ALU.mult,
                                               ALU.min).then_inc(raised, 1)

            new = m.new[:, 0:H]
            new_hi, new_md, new_lo = three(m.new3[:, 0:3 * H])

            def top_high_part(t, u, turn, b):
                dve.wait_ge(raised, t + 1)
                after(dve, top_here, t, 1)
                nc.vector.tensor_copy(new_hi, new).then_inc(top_hi, 1)

            def drop(t, u, turn, b):
                after(dve, shrink, t, 1)
                nc.vector.tensor_tensor(m.drop[:, 0:H], new, blk(m.top, b, 0, H), ALU.subtract).then_inc(dropped, 1)

            def top_without_high(t, u, turn, b):
                dve.wait_ge(top_hi, t + 1)
                nc.vector.tensor_tensor(m.new_rest[:, 0:H], new, new_hi, ALU.subtract).then_inc(top_rest, 1)

            def set_top(t, u, turn, b):
                dve.wait_ge(dropped, t + 1)
                nc.vector.tensor_tensor(blk(m.top, b, 0, H), blk(m.top, b, 0, H), new, ALU.min).then_inc(top_set, 1)

            def top_middle_part(t, u, turn, b):
                dve.wait_ge(top_rest, t + 1)
                nc.vector.tensor_copy(new_md, m.new_rest[:, 0:H]).then_inc(top_mid, 1)

            def top_low_part(t, u, turn, b):
                dve.wait_ge(top_mid, t + 1)
                nc.vector.tensor_tensor(new_lo, m.new_rest[:, 0:H], new_md, ALU.subtract).then_inc(top_parts, 1)

            def rescale(t, u, turn, b):
                acc = blk(m.acc, b, 0, WA).rearrange("p (h c) -> p h c", h=H)
                dve.wait_ge(shrink, t + 1)
                after(dve, done, t, 1)
                nc.vector.tensor_tensor(acc, acc, last(m.less[u % R][:, 0:H], DH + 1), ALU.mult).then_inc(rescaled, 1)

            def add_group(t, u, turn, b):
                acc = blk(m.acc, b, 0, WA)
                dve.wait_ge(group_sum, t + 1)
                dve.wait_ge(rescaled, t + 1)
                nc.vector.tensor_tensor(acc, acc, sum_ps[:, 0:WA], ALU.add).then_inc(done, 1)

            pipelined(dve, [(2, see), (4, rescale), (1, sum_parts), (2, raise_top), (3, take_top), (1, add_src), (2, top_high_part),
                            (3, sink), (1, leak), (2, drop), (3, bound), (1, high_part), (2, top_without_high),
                            (2, set_top), (1, without_high), (2, top_middle_part), (1, middle_part),
                            (2, top_low_part), (1, low_part), (0, place), (3, weigh), (4, add_group)],
                      blocks_on(nc, m, mybir.EngineType.DVE))
            dve.wait_ge(done, NG)

        @block.scalar
        def _(act):
            def copy_turned(t, u, turn, b):
                act.wait_ge(turned, t + 1)
                nc.scalar.copy(rows, turn_ps[0:K, 0:P]).then_inc(copied, 1)

            def exponentials(t, u, turn, b):
                r = u % R
                act.wait_ge(depth, t + 1)
                nc.scalar.activation(m.ex[r][:, :], m.depth[r][:, :], ACT.Exp).then_inc(exps, 1)

            pairs_of = [(j, h) for j in range(DVE_TILES, T) for h in range(H)]
            early = 3

            def weigh(r, some):
                for j, h in some:
                    part = m.gath[r][:, j, h * (DH + 1):(h + 1) * (DH + 1)]
                    ins = nc.scalar.mul(part, part, m.ex[r][:, j * H + h:j * H + h + 1])
                return ins

            def weigh_early(t, u, turn, b):
                act.wait_ge(exps, t + 1)
                weigh(u % R, pairs_of[:early])

            def weigh_late(t, u, turn, b):
                weigh(u % R, pairs_of[early:]).then_inc(act_weighed, 1)

            def mask(t, u, turn, b):
                r = u % R
                act.wait_ge(placed, t + 1)
                nc.scalar.activation(m.off[r][:, :], m.ohT[r][:, :], ACT.Identity, scale=BIG,
                                     bias=m.minus_big[:, 0:1]).then_inc(masked, 1)

            def choose(t, u, turn, b):
                act.wait_ge(flipped, t + 1)
                after(act, group_sum, t, 2)
                nc.scalar.copy(m.prob[:, u % 2, :], flip_ps[:, :]).then_inc(chosen, 1)

            def shrinkage(t, u, turn, b):
                r = u % R
                act.wait_ge(dropped, t + 1)
                nc.scalar.activation(m.less[r][:, 0:H], m.drop[:, 0:H], ACT.Exp).then_inc(shrink, 1)

            pipelined(act, [(2, copy_turned), (3, shrinkage), (4, weigh_late), (1, mask), (3, choose), (3, exponentials),
                            (3, weigh_early)])

        @block.tensor
        def _(pe):
            def bring_top(t, u, turn, b):
                r = u % R
                pe.wait_ge(top_parts, t + 1)
                after(pe, here, t, 1)
                for j in range(T):
                    mm = nc.tensor.matmul(here_ps[:, j * 3 * H:(j + 1) * 3 * H], m.ohT[r][:, j * P:(j + 1) * P],
                                          m.new3[:, 0:3 * H], start=True, stop=True)
                mm.then_inc(top_here, 1)

            def turn_parts(t, u, turn, b):
                pe.wait_ge(parts, t + 1)
                nc.tensor.matmul(turn_ps[0:K, 0:P], m.parts[:, 0:K], m.ident_bf[:, :], start=True,
                                 stop=True).then_inc(turned, 1)

            def mask_heads(u, heads_of):
                for h in heads_of:
                    nc.tensor.matmul(m.ps[h][:, :], m.ident_bf[:, :], m.off[u % R][:, :], start=True, stop=False)

            def mask_first_heads(t, u, turn, b):
                pe.wait_ge(masked, t + 1)
                after(pe, seen, t, 1)
                mask_heads(u, (0, 1))

            def mask_last_heads(t, u, turn, b):
                mask_heads(u, (2, 3))

            def show_logits(t, u, turn, b):
                pe.wait_ge(copied, t + 1)
                for h in range(H):
                    for j in range(T):
                        mm = nc.tensor.matmul(m.ps[h][:, j * P:(j + 1) * P], m.edgesel[:, j * H + h, :], rows,
                                              start=False, stop=(j == T - 1))
                    if h % 2 == 1:
                        mm.then_inc(shown, 1)

            def flip(t, u, turn, b):
                r = u % R
                after(pe, chosen, t, 1)
                for j in range(T):
                    mm = nc.tensor.matmul(flip_ps[:, j * P:(j + 1) * P], m.ohT[r][:, j * P:(j + 1) * P],
                                          m.ident_bf[:, :], start=True, stop=True)
                mm.then_inc(flipped, 1)

            def sum_group(t, u, turn, b):
                r = u % R
                pe.wait_ge(dve_weighed, t + 1)
                pe.wait_ge(act_weighed, t + 1)
                after(pe, done, t, 1)
                for j in range(T):
                    mm = nc.tensor.matmul(sum_ps[:, 0:WA], m.prob[:, u % 2, j * P:(j + 1) * P], m.gath[r][:, j, 0:WA],
                                          start=(j == 0), stop=(j == T - 1))
                mm.then_inc(group_sum, 1)

            def mix(t, u, turn, b):
                r = u % R
                pe.wait_ge(placed, t + 1)
                after(pe, summed, t, 1)
                for j in range(T):
                    mm = nc.tensor.matmul(adst_ps[:, j * 3 * H:(j + 1) * 3 * H], m.ohT[r][:, j * P:(j + 1) * P],
                                          blk(m.adst3, b, 0, 3 * H), start=True, stop=True)
                mm.then_inc(mixed, 1)

            pipelined(pe, [(2, mask_first_heads), (2, turn_parts), (2, mask_last_heads), (2, show_logits), (3, bring_top),
                           (1, mix), (3, flip), (4, sum_group)],
                      blocks_on(nc, m, mybir.EngineType.PE))


def add_sums(nc, m, name):
    with stage_of(nc, name) as (st, block):
        root, inverse = st.sem("root"), st.sem("inverse")

        @block.scalar
        def _(act):
            act.wait_ge(inverse, 2)
            nc.scalar.activation(m.dinv[:, :], m.dinv[:, :], ACT.Sqrt).then_inc(root, 1)

        arrived, summed, used, step = st.sems("arrived", R), st.sem("summed"), st.sem("used"), st.sem("step")

        @block.sync
        def _(sp):
            for b in range(NB):
                if b >= R:
                    sp.wait_ge(summed, b - R + 1)
                for j in range(T):
                    sp.dma_start(m.gath[b % R][:, j, 0:D + 1], m.sum0[j][b * P:(b + 1) * P, :]).then_inc(arrived[b % R], 16)

        @block.gpsimd
        def _(pool):
            for b in range(NB):
                pool.wait_ge(summed, b + 1)
                nc.gpsimd.tensor_tensor(m.x[:, b, :], m.x[:, b, :], m.prob2[b % 2][:, 0:D], ALU.add).then_inc(used, 1)
                nc.gpsimd.tensor_copy(m.deg[:, b:b + 1], m.prob2[b % 2][:, D:D + 1]).then_inc(used, 1)

        @block.vector
        def _(dve):
            for b in range(NB):
                dve.wait_ge(arrived[b % R], 16 * T * (b // R + 1))
                if b >= 2:
                    dve.wait_ge(used, 2 * (b - 1))
                nc.vector.tensor_reduce(m.prob2[b % 2][:, 0:D + 1],
                                        m.gath[b % R][:, :, 0:D + 1].rearrange("p j c -> p c j"), AX.X,
                                        ALU.add).then_inc(summed, 1)
            dve.wait_ge(used, 2 * NB)
            nc.vector.tensor_scalar(m.dinv[:, :], m.deg[:, :], 1.0e-20, None, ALU.max).then_inc(inverse, 1)
            dve.wait_ge(inverse, 1)
            nc.vector.reciprocal(m.dinv[:, :], m.dinv[:, :]).then_inc(inverse, 1)
            nc.vector.tensor_scalar(m.cnt[:, :], m.attr[:, 0:NB, 2], 1.0, None, ALU.max).then_inc(step, 1)
            dve.wait_ge(step, 1)
            nc.vector.reciprocal(m.cnt[:, :], m.cnt[:, :]).then_inc(step, 1)
            dve.wait_ge(step, 2)
            nc.vector.tensor_tensor(m.attr[:, 0:NB, 0:2], m.attr[:, 0:NB, 0:2], last(m.cnt[:, :], 2),
                                    ALU.mult).then_inc(step, 1)


def store_table(m, sp, table, rows_done, each, written):
    rows = table.rearrange("(b p) c -> p b c", p=P)
    n = NB // CHUNKS
    for b in range(0, NB, n):
        sp.wait_ge(rows_done, each * (b + n))
        sp.dma_start(rows[:, b:b + n, :], m.acc[:, b:b + n, :]).then_inc(written, 16)


def gatv2_nodes(nc, m, a, name, c, table):
    att = m.bc[f"L1_gnn_att{c}"]
    with stage_of(nc, name) as (st, block):
        loaded, taken, filled, written = st.sem("loaded"), st.sem("taken"), st.sem("filled"), st.sem("written")
        turned, moved, product = st.sem("turned"), st.sem("moved"), st.sem("product")
        mixed, rest_made, mid_made, parts, rows_done = (
            st.sem(k) for k in ("mixed", "rest_made", "mid_made", "parts", "rows_done"))
        step, zeroed = st.sem("step"), st.sem("zeroed")

        @block.sync
        def _(sp):
            for q, k in enumerate((f"L1_gnn_Wl{c}", f"L1_gnn_Wr{c}")):
                sp.dma_start(m.w[:, :, q * D:(q + 1) * D], a[k].rearrange("(c p) n -> p c n", p=P)).then_inc(loaded, 16)
            if c == 1:
                sp.wait_ge(zeroed, zero_sums(sp, m, m.sum3, zeroed))
            sp.wait_ge(filled, 4)
            store_table(m, sp, table, rows_done, 1, written)
            sp.wait_ge(written, 16 * CHUNKS)

        @block.tensor
        def _(pe):
            product_by_blocks(nc, m, pe, 2 * D, loaded, 2, turned, moved, product, taken)

        @block.scalar
        def _(act):
            def move(b):
                act.wait_ge(turned, b + 1)
                if b >= 2:
                    act.wait_ge(product, b - 1)
                nc.scalar.copy(m.hT[b % 2][:, :], m.ps[b % 2][:, 0:D]).then_inc(moved, 1)

            def middle(b):
                act.wait_ge(rest_made, b + 1)
                nc.scalar.copy(m.xr3[:, b, D:2 * D], m.h[:, b, :]).then_inc(mid_made, 1)

            move(0)
            act.wait_ge(filled, 4)
            for b in range(NB):
                if b + 1 < NB:
                    move(b + 1)
                act.wait_ge(product, b + 1)
                out = m.ps[4 + b % 4]
                nc.scalar.copy(m.acc[:, b, 0:D], out[:, 0:D])
                nc.scalar.copy(m.h[:, b, :], out[:, D:2 * D])
                nc.scalar.copy(m.xr3[:, b, 0:D], out[:, D:2 * D]).then_inc(taken, 1)
                if b >= 1:
                    middle(b - 1)
            middle(NB - 1)

        @block.gpsimd
        def _(pool):
            def rest(b):
                pool.wait_ge(mixed, 4 * b + 1)
                nc.gpsimd.tensor_tensor(m.h[:, b, :], m.h[:, b, :], m.xr3[:, b, 0:D], ALU.subtract).then_inc(rest_made, 1)

            rest(0)
            for b in range(NB):
                if b + 1 < NB:
                    rest(b + 1)
                pool.wait_ge(mid_made, b + 1)
                nc.gpsimd.tensor_tensor(m.xr3[:, b, 2 * D:3 * D], m.h[:, b, :], m.xr3[:, b, D:2 * D],
                                        ALU.subtract).then_inc(parts, 1)

        @block.vector
        def _(dve):
            nc.vector.memset(m.acc[:, 0:NB, D:TW], 1.0).then_inc(filled, 1)
            nc.vector.memset(m.acc[:, NB, :], 0.0).then_inc(filled, 1)
            nc.vector.memset(m.xr3[:, NB, :], 0.0).then_inc(filled, 1)
            nc.vector.tensor_scalar(m.att_relu[:, :], att[:, :], 1.0 - SLOPE, None, ALU.mult).then_inc(filled, 1)
            dve.wait_ge(filled, 4)
            for b in range(NB):
                dve.wait_ge(taken, b + 1)
                z = m.prob2[b % 2][:, 0:D]
                if b >= 2:
                    dve.wait_ge(mixed, 4 * (b - 1))
                nc.vector.tensor_tensor(z, m.acc[:, b, 0:D], m.h[:, b, :], ALU.add).then_inc(mixed, 1)
                nc.vector.scalar_tensor_tensor(m.junk[:, :], m.acc[:, b, 0:D], SLOPE, att[:, :], ALU.mult, ALU.mult,
                                               accum_out=m.acc[:, b, D + 1:D + 2]).then_inc(rows_done, 1)
                for r in (0, 1):
                    dve.wait_ge(mixed, 4 * b + 1 + r)
                    nc.vector.scalar_tensor_tensor(z, m.We_bc[f"L1_gnn_We{c}"][:, r, :], m.attr[:, b, r:r + 1], z,
                                                   ALU.mult, ALU.add).then_inc(mixed, 1)
                dve.wait_ge(mixed, 4 * b + 3)
                nc.vector.scalar_tensor_tensor(z, z, 0.0, m.att_relu[:, :], ALU.max, ALU.mult,
                                               accum_out=m.self_dot[:, b:b + 1]).then_inc(mixed, 1)
                dve.wait_ge(rows_done, b + 1)
            lg = m.self_dot[:, :]
            dve.wait_ge(mixed, 4 * NB)
            nc.vector.tensor_tensor(lg, lg, m.acc[:, 0:NB, D + 1], ALU.add).then_inc(step, 1)
            for r in (0, 1):
                dve.wait_ge(step, r + 1)
                nc.vector.scalar_tensor_tensor(lg, m.attr[:, 0:NB, r], m.ea_lin[c][:, r:r + 1], lg, ALU.mult,
                                               ALU.add).then_inc(step, 1)
            dve.wait_ge(step, 3)
            nc.vector.tensor_scalar(m.top[:, 0:NB, 0], lg, -1.0, None, ALU.mult).then_inc(step, 1)


def product_by_blocks(nc, m, pe, n_out, loaded, n_loads, turned, moved, product, taken, ready=None):
    def turn(b):
        if b >= 2:
            pe.wait_ge(moved, b - 1)
        if ready:
            pe.wait_ge(ready, b + 1)
        for c in (0, 1):
            mm = nc.tensor.transpose(m.ps[b % 2][:, c * P:(c + 1) * P], m.h[:, b, c * P:(c + 1) * P], m.ident[:, :])
        mm.then_inc(turned, 1)

    pe.wait_ge(loaded, 16 * n_loads)
    turn(0)
    for b in range(NB):
        if b + 1 < NB:
            turn(b + 1)
        pe.wait_ge(moved, b + 1)
        if b >= 4:
            pe.wait_ge(taken, b - 3)
        for c in (0, 1):
            mm = nc.tensor.matmul(m.ps[4 + b % 4][:, 0:n_out], m.hT[b % 2][:, c * P:(c + 1) * P],
                                  m.w[:, c, 0:n_out], start=(c == 0), stop=(c == 1))
        mm.then_inc(product, 1)


def move_transposed(nc, m, act, turned, moved, product):
    for b in range(NB):
        act.wait_ge(turned, b + 1)
        if b >= 2:
            act.wait_ge(product, b - 1)
        nc.scalar.copy(m.hT[b % 2][:, :], m.ps[b % 2][:, 0:D]).then_inc(moved, 1)


def batch_norm(nc, m, name, c, residual):
    with stage_of(nc, name) as (st, block):
        step, means, centred, squared, variances, root, scaled = (
            st.sem(k) for k in ("step", "means", "centred", "squared", "variances", "root", "scaled"))
        biased, shifted, folded, lifted, normed, negated = (
            st.sem(k) for k in ("biased", "shifted", "folded", "lifted", "normed", "negated"))
        sq = [m.prob2[q][:, 0:D] for q in (0, 1)]
        mean_ps, var_ps = m.ps[0], m.ps[1]
        beta, slope = m.bc[f"L1_gnn_beta{c}"][:, :], m.bc[f"L1_gnn_a{c}"][:, 0:1]

        @block.tensor
        def _(pe):
            for b in range(NB):
                pe.wait_ge(biased, b + 1)
                mm = nc.tensor.matmul(mean_ps[:, 0:D], m.mean_w[:, b // (NB - 1), :], m.h[:, b, :],
                                      start=(b == 0), stop=(b == NB - 1))
            mm.then_inc(means, 1)
            for b in range(NB):
                pe.wait_ge(squared, b + 1)
                mm = nc.tensor.matmul(var_ps[:, 0:D], m.mean_w[:, b // (NB - 1), :], sq[b % 2],
                                      start=(b == 0), stop=(b == NB - 1))
                if b < NB - 1:
                    mm.then_inc(variances, 1)
            mm.then_inc(variances, 1)

        @block.scalar
        def _(act):
            if residual:
                for b in range(NB):
                    act.wait_ge(biased, b + 1)
                    nc.scalar.activation(m.acc[:, b, 0:D], m.x[:, b, :], ACT.Relu, scale=m.rstd[:, b:b + 1],
                                         bias=m.shift[:, b:b + 1]).then_inc(normed, 1)
            for b in range(NB):
                act.wait_ge(centred, b + 1)
                if b >= 2:
                    act.wait_ge(variances, b - 1)
                nc.scalar.activation(sq[b % 2], m.h[:, b, :], ACT.Square).then_inc(squared, 1)
            act.wait_ge(step, 3)
            nc.scalar.activation(m.gain[:, :], m.gain[:, :], ACT.Sqrt).then_inc(root, 1)
            for b in range(NB):
                act.wait_ge(lifted if residual else shifted, b + 1)
                nc.scalar.activation(m.acc[:, b, 0:D], m.h[:, b, :], ACT.Relu, scale=-1.0).then_inc(negated, 1)

        @block.gpsimd
        def _(pool):
            for b in range(NB):
                t = m.acc[:, b, 0:D] if residual else m.h[:, b, :]
                pool.wait_ge(normed if residual else scaled, b + 1)
                nc.gpsimd.tensor_tensor(t, t, beta, ALU.add).then_inc(shifted, 1)

        @block.vector
        def _(dve):
            nc.vector.reciprocal(m.cnt[:, :], m.acc[:, 0:NB, D]).then_inc(step, 1)
            nc.vector.tensor_scalar(m.fold[:, :], slope, -1.0, 1.0, ALU.mult, ALU.add).then_inc(step, 1)
            dve.wait_ge(step, 2)
            for b in range(NB):
                nc.vector.scalar_tensor_tensor(m.h[:, b, :], m.acc[:, b, 0:D], m.cnt[:, b:b + 1],
                                               m.bc[f"L1_gnn_b{c}"][:, :], ALU.mult, ALU.add).then_inc(biased, 1)
            dve.wait_ge(means, 1)
            dve.wait_ge(biased, NB)
            for b in range(NB):
                nc.vector.tensor_tensor(m.h[:, b, :], m.h[:, b, :], mean_ps[:, 0:D], ALU.subtract).then_inc(centred, 1)
            dve.wait_ge(variances, NB)
            nc.vector.tensor_scalar(m.gain[:, :], var_ps[:, 0:D], EPS, None, ALU.add).then_inc(step, 1)
            dve.wait_ge(root, 1)
            nc.vector.reciprocal(m.gain[:, :], m.gain[:, :]).then_inc(step, 1)
            dve.wait_ge(step, 4)
            nc.vector.tensor_tensor(m.gain[:, :], m.gain[:, :], m.bc[f"L1_gnn_g{c}"][:, :], ALU.mult).then_inc(step, 1)
            dve.wait_ge(step, 5)
            dve.wait_ge(squared, NB)

            def scale(b):
                nc.vector.tensor_tensor(m.h[:, b, :], m.h[:, b, :], m.gain[:, :], ALU.mult).then_inc(scaled, 1)

            def lift(b):
                dve.wait_ge(scaled, b + 1)
                dve.wait_ge(shifted, b + 1)
                nc.vector.tensor_tensor(m.h[:, b, :], m.h[:, b, :], m.acc[:, b, 0:D], ALU.add).then_inc(lifted, 1)

            def fold(b):
                dve.wait_ge(negated, b + 1)
                nc.vector.scalar_tensor_tensor(m.h[:, b, :], m.acc[:, b, 0:D], m.fold[:, 0:1], m.h[:, b, :], ALU.mult,
                                               ALU.add).then_inc(folded, 1)

            def add(b):
                dve.wait_ge(folded, b + 1)
                nc.vector.tensor_tensor(m.x[:, b, :], m.x[:, b, :], m.h[:, b, :], ALU.add).then_inc(step, 1)

            stages = [(0, scale), (1, lift), (4, fold), (5, add)] if residual else [(0, scale), (5, fold)]
            for s in range(NB + stages[-1][0]):
                for lag, run in stages:
                    if 0 <= s - lag < NB:
                        run(s - lag)


def gat_nodes(nc, m, a, name, table):
    WA = HEADS * (DH + 1)
    with stage_of(nc, name) as (st, block):
        loaded, taken, filled, written = st.sem("loaded"), st.sem("taken"), st.sem("filled"), st.sem("written")
        turned, moved, product = st.sem("turned"), st.sem("moved"), st.sem("product")
        heads = m.acc[:, 0:NB, 0:WA].rearrange("p b (h c) -> p b h c", h=HEADS)
        by_src, by_dst, cleared, parts = st.sem("by_src"), st.sem("by_dst"), st.sem("cleared"), st.sem("parts")

        @block.sync
        def _(sp):
            sp.dma_start(m.w[:, :, 0:D], a["L2_gnn_W"].rearrange("(c p) n -> p c n", p=P)).then_inc(loaded, 16)
            sp.wait_ge(filled, 2)
            store_table(m, sp, table, by_src, 2, written)
            sp.wait_ge(written, 16 * CHUNKS)

        @block.tensor
        def _(pe):
            product_by_blocks(nc, m, pe, D, loaded, 1, turned, moved, product, taken)

        @block.scalar
        def _(act):
            def move(b):
                act.wait_ge(turned, b + 1)
                if b >= 2:
                    act.wait_ge(product, b - 1)
                nc.scalar.copy(m.hT[b % 2][:, :], m.ps[b % 2][:, 0:D]).then_inc(moved, 1)

            move(0)
            for b in range(NB):
                if b + 1 < NB:
                    move(b + 1)
                act.wait_ge(product, b + 1)
                nc.scalar.copy(heads[:, b, :, 0:DH], m.ps[4 + b % 4][:, 0:D].rearrange("p (h c) -> p h c", h=HEADS)
                               ).then_inc(taken, 1)

        @block.vector
        def _(dve):
            nc.vector.memset(heads[:, :, :, DH], 1.0).then_inc(filled, 1)
            nc.vector.memset(m.top[:, :, :], BIG).then_inc(filled, 1)
            for b in range(NB):
                dve.wait_ge(taken, b + 1)
                numbers = (("src", m.acc[:, b, WA:WA + HEADS], by_src), ("dst", m.adst[:, b, :], by_dst))
                by_att = [m.prob2[q][:, 0:D].rearrange("p (h c) -> p h c", h=HEADS) for q in (0, 1)]
                for q, (k, out, sem) in enumerate(numbers):
                    if b:
                        dve.wait_ge(sem, 2 * b)
                    nc.vector.tensor_tensor(by_att[q], heads[:, b, :, 0:DH],
                                            m.bc[f"L2_gnn_att_{k}"][:, :].rearrange("p (h c) -> p h c", h=HEADS),
                                            ALU.mult).then_inc(sem, 1)
                for q, (k, out, sem) in enumerate(numbers):
                    dve.wait_ge(sem, 2 * b + 1)
                    nc.vector.tensor_reduce(out, by_att[q], AX.X, ALU.add).then_inc(sem, 1)
            dve.wait_ge(by_dst, 2 * NB)
            hi, md, lo = (m.adst3[:, 0:NB, :].rearrange("p b (h s) -> p b h s", s=3)[:, :, :, s] for s in range(3))
            nums = m.adst[:, 0:NB, :]
            nc.vector.tensor_copy(hi, nums).then_inc(parts, 1)
            dve.wait_ge(parts, 1)
            nc.vector.tensor_tensor(nums, nums, hi, ALU.subtract).then_inc(parts, 1)
            dve.wait_ge(parts, 2)
            nc.vector.tensor_copy(md, nums).then_inc(parts, 1)
            dve.wait_ge(parts, 3)
            nc.vector.tensor_tensor(lo, nums, md, ALU.subtract).then_inc(parts, 1)
            dve.wait_ge(written, 16 * CHUNKS)
            nc.vector.memset(m.acc[:, :, :], 0.0).then_inc(cleared, 1)


def gat_out(nc, m, name):
    WA = HEADS * (DH + 1)
    with stage_of(nc, name) as (st, block):
        step, biased, divided, opened, added = (st.sem(k) for k in ("step", "biased", "divided", "opened", "added"))
        heads = m.acc[:, 0:NB, 0:WA].rearrange("p b (h c) -> p b h c", h=HEADS)

        @block.vector
        def _(dve):
            s = m.share[:, :, :]
            nc.vector.tensor_scalar(s, heads[:, :, :, DH], 0.0, None, ALU.is_equal).then_inc(step, 1)
            dve.wait_ge(step, 1)
            nc.vector.tensor_tensor(s, s, heads[:, :, :, DH], ALU.add).then_inc(step, 1)
            dve.wait_ge(step, 2)
            nc.vector.reciprocal(s, s).then_inc(step, 1)
            dve.wait_ge(step, 3)
            for b in range(NB):
                nc.vector.tensor_tensor(m.h[:, b, :].rearrange("p (h c) -> p h c", h=HEADS), heads[:, b, :, 0:DH],
                                        last(m.share[:, b, :], DH), ALU.mult).then_inc(divided, 1)
            for b in range(NB):
                dve.wait_ge(divided, b + 1)
                nc.vector.tensor_tensor(m.h[:, b, :], m.h[:, b, :], m.bc["L2_gnn_bias"][:, :], ALU.add).then_inc(biased, 1)
            for b in range(NB):
                dve.wait_ge(opened, b + 1)
                nc.vector.tensor_tensor(m.x[:, b, :], m.x[:, b, :], m.h[:, b, :], ALU.add).then_inc(added, 1)

        @block.scalar
        def _(act):
            for b in range(NB):
                act.wait_ge(biased, b + 1)
                nc.scalar.activation(m.h[:, b, :], m.h[:, b, :], ACT.Sigmoid).then_inc(opened, 1)


def gcn_out(nc, m, a, name, out):
    with stage_of(nc, name) as (st, block):
        arrived, summed, scaled, ready = st.sems("arrived", R), st.sem("summed"), st.sem("scaled"), st.sem("ready")
        loaded, taken, added, stored = st.sem("loaded"), st.sem("taken"), st.sem("added"), st.sem("stored")
        turned, moved, product, paired = (st.sem(k) for k in ("turned", "moved", "product", "paired"))

        @block.sync
        def _(sp):
            sp.dma_start(m.w[:, :, 0:D], a["L3_gnn_WT"].rearrange("(c p) n -> p c n", p=P)).then_inc(loaded, 16)
            n = NB // CHUNKS
            rows = out.rearrange("(b p) c -> p b c", p=P)
            for b in range(NB):
                if b >= R:
                    sp.wait_ge(summed, b - R + 1)
                for j in range(T):
                    sp.dma_start(m.gath[b % R][:, j, 0:D], m.sum3[j][b * P:(b + 1) * P, :]).then_inc(arrived[b % R], 16)
                if b % n == n - 1 and b >= 2 * n:
                    sp.wait_ge(added, b + 1 - 2 * n)
                    sp.dma_start(rows[:, b + 1 - 3 * n:b + 1 - 2 * n, :], m.x[:, b + 1 - 3 * n:b + 1 - 2 * n, :]
                                 ).then_inc(stored, 16)
            for b in (NB - 2 * n, NB - n):
                sp.wait_ge(added, b + n)
                sp.dma_start(rows[:, b:b + n, :], m.x[:, b:b + n, :]).then_inc(stored, 16)
            sp.wait_ge(stored, 16 * CHUNKS)

        @block.gpsimd
        def _(pool):
            for b in range(NB):
                copies = m.gath[b % R][:, :, 0:D].rearrange("p (i q) c -> p i q c", i=2)
                pool.wait_ge(arrived[b % R], 16 * T * (b // R + 1))
                nc.gpsimd.tensor_tensor(copies[:, :, 0, :], copies[:, :, 0, :], copies[:, :, 1, :],
                                        ALU.add).then_inc(paired, 1)

        @block.tensor
        def _(pe):
            product_by_blocks(nc, m, pe, D, loaded, 1, turned, moved, product, taken, ready)

        @block.scalar
        def _(act):
            for b in range(NB):
                nc.scalar.mul(m.h[:, b, :], m.h[:, b, :], m.dinv[:, b:b + 1]).then_inc(scaled, 1)
            move_transposed(nc, m, act, turned, moved, product)

        @block.vector
        def _(dve):
            def sum_copies(b):
                dve.wait_ge(paired, b + 1)
                if b >= 2:
                    dve.wait_ge(ready, b - 1)
                t = m.prob2[b % 2][:, 0:D]
                nc.vector.tensor_tensor(t, m.gath[b % R][:, 0, 0:D], m.gath[b % R][:, 2, 0:D], ALU.add).then_inc(summed, 1)
                dve.wait_ge(summed, b + 1)
                dve.wait_ge(scaled, b + 1)
                nc.vector.scalar_tensor_tensor(m.h[:, b, :], t, m.dinv[:, b:b + 1], m.h[:, b, :], ALU.mult,
                                               ALU.add).then_inc(ready, 1)

            def finish(b):
                dve.wait_ge(product, b + 1)
                t = (m.mean, m.gain)[b % 2][:, :]
                if b >= 2:
                    dve.wait_ge(added, b - 1)
                nc.vector.tensor_tensor(t, m.ps[4 + b % 4][:, 0:D], m.bc["L3_gnn_b"][:, :], ALU.add).then_inc(taken, 1)
                dve.wait_ge(taken, b + 1)
                nc.vector.scalar_tensor_tensor(m.x[:, b, :], t, 0.0, m.x[:, b, :], ALU.max, ALU.add).then_inc(added, 1)

            behind = 3
            for b in range(NB + behind):
                if b < NB:
                    sum_copies(b)
                if b >= behind:
                    finish(b - behind)


ROWS = ["L1_gnn_att1", "L1_gnn_b1", "L1_gnn_g1", "L1_gnn_beta1", "L1_gnn_a1", "L1_gnn_att2", "L1_gnn_b2",
        "L1_gnn_g2", "L1_gnn_beta2", "L1_gnn_a2", "L2_gnn_att_src", "L2_gnn_att_dst", "L2_gnn_bias", "L3_gnn_b"]


def build(nc, a, out):
    m = Memory()
    with ExitStack() as ctx:
        def sb(name, *shape, dt=F32):
            return ctx.enter_context(nc.sbuf_tensor(name, list(shape), dt))

        def ring(name, n, *shape, dt=F32):
            return [sb(f"{name}{r}", *shape, dt=dt) for r in range(n)]

        def dram(name, *shape, dt=F32):
            return nc.dram_tensor(name, shape, dt, kind="Internal").ap()

        m.x, m.h = sb("x", P, NB, D), sb("h", P, NB + 1, D)
        m.xr3, m.acc = sb("xr3", P, NB + 1, 3 * D, dt=BF16), sb("acc", P, NB + 1, TW)
        m.top, m.adst, m.attr = (sb(k, P, NB + 1, 4) for k in ("top", "adst", "attr"))
        m.adst3 = sb("adst3", P, NB + 1, 3 * HEADS, dt=BF16)
        m.deg, m.dinv, m.rstd, m.shift, m.cnt, m.self_dot = (
            sb(k, P, NB) for k in ("deg", "dinv", "rstd", "shift", "cnt", "self_dot"))
        m.mv, m.st6, m.share = sb("mv", P, NB, 2), sb("st6", P, NB, 6), sb("share", P, NB, HEADS)
        m.ident, m.ident_bf, m.later = sb("ident", P, P), sb("ident_bf", P, P, dt=BF16), sb("later", P, P, dt=BF16)
        m.one_bf, m.minus_big = sb("one_bf", P, 1, dt=BF16), sb("minus_big", P, 1)
        m.one, m.minus_icol = sb("one", P, 1), sb("minus_icol", P, 1)
        m.icol, m.irow, m.dumprow, m.real = sb("icol", P, 1), sb("irow", P, P), sb("dumprow", P, 1), sb("real", P, 1)
        m.mean_w, m.fold = sb("mean_w", P, 2, P), sb("fold", P, 1)
        m.of_tile, m.of_edge = sb("of_tile", 3 * T, T), sb("of_edge", 3 * T * HEADS, T * HEADS)
        m.tilesel = sb("tilesel", 3 * T, T, P, dt=BF16)
        m.edgesel = sb("edgesel", 3 * T * HEADS, T * HEADS, P, dt=BF16)
        m.bc = {k: sb(f"{k}_rows", P, a[k].shape[0]) for k in ROWS}
        m.We12 = {c: sb(f"We12_{c}", KE, D, dt=BF16) for c in (1, 2)}
        m.ea_lin = {c: sb(f"ea_lin{c}", P, 2) for c in (1, 2)}
        m.We_bc = {f"L1_gnn_We{c}": sb(f"We{c}_rows", P, 2, D) for c in (1, 2)}
        m.mean, m.gain = sb("mean", P, D), sb("gain", P, D)
        m.att_relu, m.junk = m.mean, m.gain
        m.later32 = m.junk[:, 0:P]
        m.tab = sb("tab", 1, NG, dt=I32)
        m.src_col, m.to_row = ring("src_col", R, P, T, dt=I32), ring("to_row", R, P, T, dt=I32)
        m.loc, m.ew, m.inb = ring("loc", R, P, T), ring("ew", R, P, T), ring("inb", R, P, T, dt=BF16)
        m.ea, m.eaT = ring("ea", R, P, 2, T), ring("eaT", R, KE, WIN, dt=BF16)
        m.lin, m.away = ring("lin", R, P, T), ring("away", R, P, T)
        m.locrow, m.ohT, m.off = (ring(k, R, P, WIN, dt=BF16) for k in ("locrow", "ohT", "off"))
        m.gath, m.zs, m.prob = ring("gath", R, P, T, TW), ring("zs", 2, P, T, D), sb("prob", P, 2, WIN)
        m.expT, m.rows = m.prob[:, 1, :], sb("rows", 3 * T * HEADS, P, dt=BF16)
        m.parts, m.new3 = sb("parts", P, 3 * T * HEADS, dt=BF16), sb("new3", P, 3 * HEADS, dt=BF16)
        m.lgs, m.depth, m.ex = (ring(k, R, P, T * HEADS) for k in ("lgs", "depth", "ex"))
        m.lg, m.dots, m.e4, m.rest, m.here = (sb(k, P, n) for k, n in (
            ("lg", T), ("dots", T), ("e4", T * HEADS), ("rest", T * HEADS), ("here", T * HEADS)))
        m.less = ring("less", R, P, HEADS)
        m.zero = sb("zero", P, D + 1)
        m.seen, m.new, m.drop, m.new_rest = (sb(k, P, HEADS) for k in ("seen", "new", "drop", "new_rest"))
        m.attr_sum = sb("attr_sum", P, 3)
        m.w, m.hT = m.prob, [m.zs[1][:, q, :] for q in (0, 1)]
        m.prob2 = ring("sums", 2, P, TW)
        ls = m.zs[0][:, :, :].rearrange("p j c -> p (j c)")
        room = m.xr3[:, :, :].rearrange("p b c -> p (b c)").bitcast(F32)
        m.list = {"ends": sb("ends", WH, 4, dt=I32), "ends_f": sb("ends_f", WH, 4),
                  "spread": room[0:WH, 3 * WIN:4 * WIN].rearrange("p (q c) -> p q c", q=4),
                  "fl": ls[:, 0:2 * NW], "cnt": ls[:, 2 * NW:3 * NW], "off": ls[:, 3 * NW:4 * NW],
                  "one": ls[:, 4 * NW:5 * NW]}
        for k in ("gid", "w", "o", "b", "base"):
            m.list[k] = sb(f"list_{k}", P, 2)
        for k in ("w_int", "b_int"):
            m.list[k] = sb(f"list_{k}", P, 2, dt=I32)
        m.list["loc"] = room[:, 0:2 * WIN].rearrange("p (h n) -> p h n", h=2)
        m.list["locb"] = room[:, 2 * WIN:3 * WIN].bitcast(BF16).rearrange("p (h n) -> p h n", h=2)
        m.psum = ctx.enter_context(nc.psum_tensor("psum", [P, 8, WIN], F32))
        m.ps = [m.psum[:, q, :] for q in range(8)]
        m.g_src, m.g_loc, m.g_ew = dram("g_src", NG, WIN, dt=I32), dram("g_loc", NG, WIN), dram("g_ew", NG, WIN)
        m.g_locb, m.g_ea = dram("g_locb", NG, WIN, dt=BF16), [dram(f"g_ea{c}", NG, WIN) for c in (0, 1)]
        m.g_eaT, m.g_lin = dram("g_eaT", NG, KE, WIN, dt=BF16), {c: dram(f"g_lin{c}", NG, WIN) for c in (1, 2)}
        m.block_of = dram("block_of", 2 * P, dt=I32)
        tables = [dram(f"table{q}", NP, TW) for q in range(3)]
        m.sum0 = [dram(f"sum0_{j}", NP + P, D + 1) for j in range(T)]
        m.sum3 = [dram(f"sum3_{j}", NP + P, D) for j in range(T)]

        constants(nc, m, a)
        group_list(nc, m, a)
        layer_norm(nc, m, "ln0")
        scatter_loop(nc, m, "spmm", m.sum0, True)
        add_sums(nc, m, "spmm_out")
        layer_norm(nc, m, "ln1")
        for c in (1, 2):
            gatv2_nodes(nc, m, a, f"gatv2_{c}", c, tables[c - 1])
            gatv2_loop(nc, m, f"edges{c}", tables[c - 1], c)
            batch_norm(nc, m, f"bn{c}", c, residual=(c == 2))
        layer_norm(nc, m, "ln2")
        gat_nodes(nc, m, a, "gat", tables[2])
        gat_loop(nc, m, "gat_edges", tables[2])
        gat_out(nc, m, "gat_out")
        layer_norm(nc, m, "ln3", scale=m.dinv)
        scatter_loop(nc, m, "gcn_edges", m.sum3, False)
        gcn_out(nc, m, a, "gcn_out", out)


def kernel(**inputs):
    import numpy as np
    import concourse.bacc as bacc
    from concourse.bass_utils import run_bass_kernel_spmd

    def padded(v, n, fill):
        v = np.asarray(v)
        return np.concatenate([v, np.full((n - v.shape[0],) + v.shape[1:], fill, v.dtype)])

    arrays = {k: np.asarray(v) for k, v in inputs.items()}
    arrays["x"] = padded(arrays["x"], NP, 0)
    for k in ("src", "dst"):
        arrays[k] = padded(arrays[k], EP, NP - 1)
    ea = arrays.pop("edge_attr_2")
    for c in (0, 1):
        arrays[f"ea{c}"] = padded(ea[:, c], EP, 0)
    arrays["edge_weight"] = padded(arrays["edge_weight"], EP, 0)
    arrays["L3_gnn_WT"] = arrays.pop("L3_gnn_W").T
    for k in ROWS:
        arrays[k] = arrays[k].reshape(-1)
    arrays = {f"in_{k}": np.ascontiguousarray(v) for k, v in arrays.items()}

    nc = bacc.Bacc("TRN2", target_bir_lowering=False, num_devices=1)
    a = {k[3:]: nc.dram_tensor(k, v.shape, mybir.dt.from_np(v.dtype), kind="ExternalInput").ap()
         for k, v in arrays.items()}
    out = nc.dram_tensor("out", (NP, D), F32, kind="ExternalOutput").ap()
    build(nc, a, out)
    r = run_bass_kernel_spmd(nc, [arrays], core_ids=[0])
    return r.results[0]["out"][0:N]
```
